# Optimizing a Trainium2 kernel written in Bass

```python
import numpy as np
import jax
import jax.numpy as jnp

def _softmax(x, axis=-1):
    return jax.nn.softmax(x, axis=axis)

def _gelu(x):
    return jax.nn.gelu(x, approximate=True)

def _silu(x):
    return jax.nn.silu(x)

def _sigmoid(x):
    return jax.nn.sigmoid(x)

def _layernorm(x, axis=-1, eps=1e-05):
    m = jnp.mean(x, axis=axis, keepdims=True)
    v = jnp.var(x, axis=axis, keepdims=True)
    return (x - m) / jnp.sqrt(v + eps)

def _scatter_add(tgt, idx, src, axis=0):
    return tgt.at[idx].add(src)

def _segment_sum(src, seg, n):
    return jax.ops.segment_sum(src, seg, n)
kernel_name = 'mk_rec_standalone_d1_rec_r8_6f8892'

def setup_inputs(seed: int=0):
    np.random.seed(seed)
    _w = jnp.asarray

    def _rec_inputs():
        import jax
        import jax.numpy as jnp
        _rk = jax.random.key(seed)
        r_num_feat1 = -0.0580273 + 0.99462 * jax.random.normal(jax.random.fold_in(_rk, 1), (2048,), jnp.float32)
        r_num_feat2 = -0.0209273 + 1.04763 * jax.random.normal(jax.random.fold_in(_rk, 2), (2048,), jnp.float32)
        r_score = jax.random.uniform(jax.random.fold_in(_rk, 3), (2048,), jnp.float32, 0.0, 0.949735)
        r_user_id = jax.random.randint(jax.random.fold_in(_rk, 4), (2048,), 52, 99938, jnp.int32)
        r_cand_item_id = jax.random.randint(jax.random.fold_in(_rk, 5), (2048,), 110, 99915, jnp.int32)
        r_cand_item_cat = jax.random.randint(jax.random.fold_in(_rk, 6), (2048,), 1, 1000, jnp.int32)
        r_exp_item_id = jnp.stack([jax.random.randint(jax.random.fold_in(jax.random.fold_in(_rk, 7), 0), (2048,), 124, 12498, jnp.int32), jax.random.randint(jax.random.fold_in(jax.random.fold_in(_rk, 7), 1), (2048,), 82, 99347, jnp.int32), jax.random.randint(jax.random.fold_in(jax.random.fold_in(_rk, 7), 2), (2048,), 7, 99989, jnp.int32), jax.random.randint(jax.random.fold_in(jax.random.fold_in(_rk, 7), 3), (2048,), 167, 99978, jnp.int32), jax.random.randint(jax.random.fold_in(jax.random.fold_in(_rk, 7), 4), (2048,), 25, 99999, jnp.int32), jax.random.randint(jax.random.fold_in(jax.random.fold_in(_rk, 7), 5), (2048,), 117, 99739, jnp.int32), jax.random.randint(jax.random.fold_in(jax.random.fold_in(_rk, 7), 6), (2048,), 151, 99855, jnp.int32), jax.random.randint(jax.random.fold_in(jax.random.fold_in(_rk, 7), 7), (2048,), 26, 12500, jnp.int32), jax.random.randint(jax.random.fold_in(jax.random.fold_in(_rk, 7), 8), (2048,), 36, 99751, jnp.int32), jax.random.randint(jax.random.fold_in(jax.random.fold_in(_rk, 7), 9), (2048,), 40, 99999, jnp.int32), jax.random.randint(jax.random.fold_in(jax.random.fold_in(_rk, 7), 10), (2048,), 148, 99826, jnp.int32), jax.random.randint(jax.random.fold_in(jax.random.fold_in(_rk, 7), 11), (2048,), 43, 99793, jnp.int32), jax.random.randint(jax.random.fold_in(jax.random.fold_in(_rk, 7), 12), (2048,), 53, 99961, jnp.int32), jax.random.randint(jax.random.fold_in(jax.random.fold_in(_rk, 7), 13), (2048,), 52, 99973, jnp.int32), jax.random.randint(jax.random.fold_in(jax.random.fold_in(_rk, 7), 14), (2048,), 25, 99956, jnp.int32), jax.random.randint(jax.random.fold_in(jax.random.fold_in(_rk, 7), 15), (2048,), 72, 99996, jnp.int32), jax.random.randint(jax.random.fold_in(jax.random.fold_in(_rk, 7), 16), (2048,), 2, 12485, jnp.int32), jax.random.randint(jax.random.fold_in(jax.random.fold_in(_rk, 7), 17), (2048,), 30, 99987, jnp.int32), jax.random.randint(jax.random.fold_in(jax.random.fold_in(_rk, 7), 18), (2048,), 174, 12498, jnp.int32), jax.random.randint(jax.random.fold_in(jax.random.fold_in(_rk, 7), 19), (2048,), 108, 99957, jnp.int32), jax.random.randint(jax.random.fold_in(jax.random.fold_in(_rk, 7), 20), (2048,), 69, 99934, jnp.int32), jax.random.randint(jax.random.fold_in(jax.random.fold_in(_rk, 7), 21), (2048,), 76, 99844, jnp.int32), jax.random.randint(jax.random.fold_in(jax.random.fold_in(_rk, 7), 22), (2048,), 12, 99862, jnp.int32), jax.random.randint(jax.random.fold_in(jax.random.fold_in(_rk, 7), 23), (2048,), 203, 99607, jnp.int32), jax.random.randint(jax.random.fold_in(jax.random.fold_in(_rk, 7), 24), (2048,), 52, 12493, jnp.int32), jax.random.randint(jax.random.fold_in(jax.random.fold_in(_rk, 7), 25), (2048,), 31, 99841, jnp.int32), jax.random.randint(jax.random.fold_in(jax.random.fold_in(_rk, 7), 26), (2048,), 71, 99987, jnp.int32), jax.random.randint(jax.random.fold_in(jax.random.fold_in(_rk, 7), 27), (2048,), 63, 99881, jnp.int32), jax.random.randint(jax.random.fold_in(jax.random.fold_in(_rk, 7), 28), (2048,), 62, 99903, jnp.int32), jax.random.randint(jax.random.fold_in(jax.random.fold_in(_rk, 7), 29), (2048,), 137, 99759, jnp.int32), jax.random.randint(jax.random.fold_in(jax.random.fold_in(_rk, 7), 30), (2048,), 60, 99820, jnp.int32), jax.random.randint(jax.random.fold_in(jax.random.fold_in(_rk, 7), 31), (2048,), 85, 99675, jnp.int32), jax.random.randint(jax.random.fold_in(jax.random.fold_in(_rk, 7), 32), (2048,), 95, 99958, jnp.int32), jax.random.randint(jax.random.fold_in(jax.random.fold_in(_rk, 7), 33), (2048,), 222, 99898, jnp.int32), jax.random.randint(jax.random.fold_in(jax.random.fold_in(_rk, 7), 34), (2048,), 53, 12468, jnp.int32), jax.random.randint(jax.random.fold_in(jax.random.fold_in(_rk, 7), 35), (2048,), 44, 99945, jnp.int32), jax.random.randint(jax.random.fold_in(jax.random.fold_in(_rk, 7), 36), (2048,), 82, 99940, jnp.int32), jax.random.randint(jax.random.fold_in(jax.random.fold_in(_rk, 7), 37), (2048,), 268, 12500, jnp.int32), jax.random.randint(jax.random.fold_in(jax.random.fold_in(_rk, 7), 38), (2048,), 68, 12498, jnp.int32), jax.random.randint(jax.random.fold_in(jax.random.fold_in(_rk, 7), 39), (2048,), 16, 99972, jnp.int32), jax.random.randint(jax.random.fold_in(jax.random.fold_in(_rk, 7), 40), (2048,), 154, 12494, jnp.int32), jax.random.randint(jax.random.fold_in(jax.random.fold_in(_rk, 7), 41), (2048,), 122, 99967, jnp.int32), jax.random.randint(jax.random.fold_in(jax.random.fold_in(_rk, 7), 42), (2048,), 241, 99895, jnp.int32), jax.random.randint(jax.random.fold_in(jax.random.fold_in(_rk, 7), 43), (2048,), 120, 99755, jnp.int32), jax.random.randint(jax.random.fold_in(jax.random.fold_in(_rk, 7), 44), (2048,), 99, 99951, jnp.int32), jax.random.randint(jax.random.fold_in(jax.random.fold_in(_rk, 7), 45), (2048,), 103, 99923, jnp.int32), jax.random.randint(jax.random.fold_in(jax.random.fold_in(_rk, 7), 46), (2048,), 308, 12493, jnp.int32), jax.random.randint(jax.random.fold_in(jax.random.fold_in(_rk, 7), 47), (2048,), 135, 99778, jnp.int32), jax.random.randint(jax.random.fold_in(jax.random.fold_in(_rk, 7), 48), (2048,), 15, 12477, jnp.int32), jax.random.randint(jax.random.fold_in(jax.random.fold_in(_rk, 7), 49), (2048,), 73, 12500, jnp.int32), jax.random.randint(jax.random.fold_in(jax.random.fold_in(_rk, 7), 50), (2048,), 108, 99698, jnp.int32), jax.random.randint(jax.random.fold_in(jax.random.fold_in(_rk, 7), 51), (2048,), 125, 99682, jnp.int32), jax.random.randint(jax.random.fold_in(jax.random.fold_in(_rk, 7), 52), (2048,), 204, 99980, jnp.int32), jax.random.randint(jax.random.fold_in(jax.random.fold_in(_rk, 7), 53), (2048,), 26, 99965, jnp.int32), jax.random.randint(jax.random.fold_in(jax.random.fold_in(_rk, 7), 54), (2048,), 20, 99771, jnp.int32), jax.random.randint(jax.random.fold_in(jax.random.fold_in(_rk, 7), 55), (2048,), 58, 99676, jnp.int32), jax.random.randint(jax.random.fold_in(jax.random.fold_in(_rk, 7), 56), (2048,), 13, 99970, jnp.int32), jax.random.randint(jax.random.fold_in(jax.random.fold_in(_rk, 7), 57), (2048,), 12, 99765, jnp.int32), jax.random.randint(jax.random.fold_in(jax.random.fold_in(_rk, 7), 58), (2048,), 16, 99949, jnp.int32), jax.random.randint(jax.random.fold_in(jax.random.fold_in(_rk, 7), 59), (2048,), 230, 99811, jnp.int32), jax.random.randint(jax.random.fold_in(jax.random.fold_in(_rk, 7), 60), (2048,), 82, 99666, jnp.int32), jax.random.randint(jax.random.fold_in(jax.random.fold_in(_rk, 7), 61), (2048,), 124, 99877, jnp.int32), jax.random.randint(jax.random.fold_in(jax.random.fold_in(_rk, 7), 62), (2048,), 57, 99995, jnp.int32), jax.random.randint(jax.random.fold_in(jax.random.fold_in(_rk, 7), 63), (2048,), 164, 99966, jnp.int32), jax.random.randint(jax.random.fold_in(jax.random.fold_in(_rk, 7), 64), (2048,), 65, 99955, jnp.int32), jax.random.randint(jax.random.fold_in(jax.random.fold_in(_rk, 7), 65), (2048,), 1, 99958, jnp.int32), jax.random.randint(jax.random.fold_in(jax.random.fold_in(_rk, 7), 66), (2048,), 69, 99902, jnp.int32), jax.random.randint(jax.random.fold_in(jax.random.fold_in(_rk, 7), 67), (2048,), 146, 99685, jnp.int32), jax.random.randint(jax.random.fold_in(jax.random.fold_in(_rk, 7), 68), (2048,), 59, 99956, jnp.int32), jax.random.randint(jax.random.fold_in(jax.random.fold_in(_rk, 7), 69), (2048,), 72, 99945, jnp.int32), jax.random.randint(jax.random.fold_in(jax.random.fold_in(_rk, 7), 70), (2048,), 58, 99870, jnp.int32), jax.random.randint(jax.random.fold_in(jax.random.fold_in(_rk, 7), 71), (2048,), 8, 99948, jnp.int32), jax.random.randint(jax.random.fold_in(jax.random.fold_in(_rk, 7), 72), (2048,), 53, 99841, jnp.int32), jax.random.randint(jax.random.fold_in(jax.random.fold_in(_rk, 7), 73), (2048,), 243, 99998, jnp.int32), jax.random.randint(jax.random.fold_in(jax.random.fold_in(_rk, 7), 74), (2048,), 45, 99993, jnp.int32), jax.random.randint(jax.random.fold_in(jax.random.fold_in(_rk, 7), 75), (2048,), 71, 99873, jnp.int32), jax.random.randint(jax.random.fold_in(jax.random.fold_in(_rk, 7), 76), (2048,), 8, 99717, jnp.int32), jax.random.randint(jax.random.fold_in(jax.random.fold_in(_rk, 7), 77), (2048,), 54, 99908, jnp.int32), jax.random.randint(jax.random.fold_in(jax.random.fold_in(_rk, 7), 78), (2048,), 66, 99934, jnp.int32), jax.random.randint(jax.random.fold_in(jax.random.fold_in(_rk, 7), 79), (2048,), 48, 99956, jnp.int32), jax.random.randint(jax.random.fold_in(jax.random.fold_in(_rk, 7), 80), (2048,), 99, 99915, jnp.int32), jax.random.randint(jax.random.fold_in(jax.random.fold_in(_rk, 7), 81), (2048,), 108, 99917, jnp.int32), jax.random.randint(jax.random.fold_in(jax.random.fold_in(_rk, 7), 82), (2048,), 49, 99639, jnp.int32), jax.random.randint(jax.random.fold_in(jax.random.fold_in(_rk, 7), 83), (2048,), 189, 99887, jnp.int32), jax.random.randint(jax.random.fold_in(jax.random.fold_in(_rk, 7), 84), (2048,), 160, 99972, jnp.int32), jax.random.randint(jax.random.fold_in(jax.random.fold_in(_rk, 7), 85), (2048,), 93, 99974, jnp.int32), jax.random.randint(jax.random.fold_in(jax.random.fold_in(_rk, 7), 86), (2048,), 45, 99975, jnp.int32), jax.random.randint(jax.random.fold_in(jax.random.fold_in(_rk, 7), 87), (2048,), 16, 99908, jnp.int32), jax.random.randint(jax.random.fold_in(jax.random.fold_in(_rk, 7), 88), (2048,), 101, 99892, jnp.int32), jax.random.randint(jax.random.fold_in(jax.random.fold_in(_rk, 7), 89), (2048,), 33, 12496, jnp.int32), jax.random.randint(jax.random.fold_in(jax.random.fold_in(_rk, 7), 90), (2048,), 11, 99899, jnp.int32), jax.random.randint(jax.random.fold_in(jax.random.fold_in(_rk, 7), 91), (2048,), 96, 99924, jnp.int32), jax.random.randint(jax.random.fold_in(jax.random.fold_in(_rk, 7), 92), (2048,), 77, 99666, jnp.int32), jax.random.randint(jax.random.fold_in(jax.random.fold_in(_rk, 7), 93), (2048,), 30, 99901, jnp.int32), jax.random.randint(jax.random.fold_in(jax.random.fold_in(_rk, 7), 94), (2048,), 242, 99991, jnp.int32), jax.random.randint(jax.random.fold_in(jax.random.fold_in(_rk, 7), 95), (2048,), 155, 99661, jnp.int32), jax.random.randint(jax.random.fold_in(jax.random.fold_in(_rk, 7), 96), (2048,), 17, 99970, jnp.int32), jax.random.randint(jax.random.fold_in(jax.random.fold_in(_rk, 7), 97), (2048,), 71, 99882, jnp.int32), jax.random.randint(jax.random.fold_in(jax.random.fold_in(_rk, 7), 98), (2048,), 294, 12500, jnp.int32), jax.random.randint(jax.random.fold_in(jax.random.fold_in(_rk, 7), 99), (2048,), 19, 99845, jnp.int32), jax.random.randint(jax.random.fold_in(jax.random.fold_in(_rk, 7), 100), (2048,), 48, 99918, jnp.int32), jax.random.randint(jax.random.fold_in(jax.random.fold_in(_rk, 7), 101), (2048,), 39, 99989, jnp.int32), jax.random.randint(jax.random.fold_in(jax.random.fold_in(_rk, 7), 102), (2048,), 44, 99997, jnp.int32), jax.random.randint(jax.random.fold_in(jax.random.fold_in(_rk, 7), 103), (2048,), 201, 12488, jnp.int32), jax.random.randint(jax.random.fold_in(jax.random.fold_in(_rk, 7), 104), (2048,), 22, 99962, jnp.int32), jax.random.randint(jax.random.fold_in(jax.random.fold_in(_rk, 7), 105), (2048,), 195, 99898, jnp.int32), jax.random.randint(jax.random.fold_in(jax.random.fold_in(_rk, 7), 106), (2048,), 10, 12499, jnp.int32), jax.random.randint(jax.random.fold_in(jax.random.fold_in(_rk, 7), 107), (2048,), 53, 99869, jnp.int32), jax.random.randint(jax.random.fold_in(jax.random.fold_in(_rk, 7), 108), (2048,), 124, 99997, jnp.int32), jax.random.randint(jax.random.fold_in(jax.random.fold_in(_rk, 7), 109), (2048,), 84, 99955, jnp.int32), jax.random.randint(jax.random.fold_in(jax.random.fold_in(_rk, 7), 110), (2048,), 82, 99939, jnp.int32), jax.random.randint(jax.random.fold_in(jax.random.fold_in(_rk, 7), 111), (2048,), 125, 99985, jnp.int32), jax.random.randint(jax.random.fold_in(jax.random.fold_in(_rk, 7), 112), (2048,), 6, 99997, jnp.int32), jax.random.randint(jax.random.fold_in(jax.random.fold_in(_rk, 7), 113), (2048,), 58, 99833, jnp.int32), jax.random.randint(jax.random.fold_in(jax.random.fold_in(_rk, 7), 114), (2048,), 70, 99945, jnp.int32), jax.random.randint(jax.random.fold_in(jax.random.fold_in(_rk, 7), 115), (2048,), 9, 99763, jnp.int32), jax.random.randint(jax.random.fold_in(jax.random.fold_in(_rk, 7), 116), (2048,), 20, 99963, jnp.int32), jax.random.randint(jax.random.fold_in(jax.random.fold_in(_rk, 7), 117), (2048,), 173, 99986, jnp.int32), jax.random.randint(jax.random.fold_in(jax.random.fold_in(_rk, 7), 118), (2048,), 24, 99938, jnp.int32), jax.random.randint(jax.random.fold_in(jax.random.fold_in(_rk, 7), 119), (2048,), 139, 99409, jnp.int32), jax.random.randint(jax.random.fold_in(jax.random.fold_in(_rk, 7), 120), (2048,), 7, 99962, jnp.int32), jax.random.randint(jax.random.fold_in(jax.random.fold_in(_rk, 7), 121), (2048,), 93, 99973, jnp.int32), jax.random.randint(jax.random.fold_in(jax.random.fold_in(_rk, 7), 122), (2048,), 138, 99987, jnp.int32), jax.random.randint(jax.random.fold_in(jax.random.fold_in(_rk, 7), 123), (2048,), 121, 99874, jnp.int32), jax.random.randint(jax.random.fold_in(jax.random.fold_in(_rk, 7), 124), (2048,), 1, 99945, jnp.int32), jax.random.randint(jax.random.fold_in(jax.random.fold_in(_rk, 7), 125), (2048,), 49, 99910, jnp.int32), jax.random.randint(jax.random.fold_in(jax.random.fold_in(_rk, 7), 126), (2048,), 373, 99796, jnp.int32), jax.random.randint(jax.random.fold_in(jax.random.fold_in(_rk, 7), 127), (2048,), 175, 99915, jnp.int32), jax.random.randint(jax.random.fold_in(jax.random.fold_in(_rk, 7), 128), (2048,), 42, 99969, jnp.int32), jax.random.randint(jax.random.fold_in(jax.random.fold_in(_rk, 7), 129), (2048,), 91, 12494, jnp.int32), jax.random.randint(jax.random.fold_in(jax.random.fold_in(_rk, 7), 130), (2048,), 164, 99963, jnp.int32), jax.random.randint(jax.random.fold_in(jax.random.fold_in(_rk, 7), 131), (2048,), 76, 99498, jnp.int32), jax.random.randint(jax.random.fold_in(jax.random.fold_in(_rk, 7), 132), (2048,), 7, 99839, jnp.int32), jax.random.randint(jax.random.fold_in(jax.random.fold_in(_rk, 7), 133), (2048,), 145, 99851, jnp.int32), jax.random.randint(jax.random.fold_in(jax.random.fold_in(_rk, 7), 134), (2048,), 14, 99892, jnp.int32), jax.random.randint(jax.random.fold_in(jax.random.fold_in(_rk, 7), 135), (2048,), 10, 99961, jnp.int32), jax.random.randint(jax.random.fold_in(jax.random.fold_in(_rk, 7), 136), (2048,), 235, 12486, jnp.int32), jax.random.randint(jax.random.fold_in(jax.random.fold_in(_rk, 7), 137), (2048,), 222, 99973, jnp.int32), jax.random.randint(jax.random.fold_in(jax.random.fold_in(_rk, 7), 138), (2048,), 96, 99983, jnp.int32), jax.random.randint(jax.random.fold_in(jax.random.fold_in(_rk, 7), 139), (2048,), 59, 12490, jnp.int32), jax.random.randint(jax.random.fold_in(jax.random.fold_in(_rk, 7), 140), (2048,), 88, 12473, jnp.int32), jax.random.randint(jax.random.fold_in(jax.random.fold_in(_rk, 7), 141), (2048,), 15, 99887, jnp.int32), jax.random.randint(jax.random.fold_in(jax.random.fold_in(_rk, 7), 142), (2048,), 128, 99798, jnp.int32), jax.random.randint(jax.random.fold_in(jax.random.fold_in(_rk, 7), 143), (2048,), 51, 99914, jnp.int32), jax.random.randint(jax.random.fold_in(jax.random.fold_in(_rk, 7), 144), (2048,), 24, 12455, jnp.int32), jax.random.randint(jax.random.fold_in(jax.random.fold_in(_rk, 7), 145), (2048,), 23, 99961, jnp.int32), jax.random.randint(jax.random.fold_in(jax.random.fold_in(_rk, 7), 146), (2048,), 59, 12499, jnp.int32), jax.random.randint(jax.random.fold_in(jax.random.fold_in(_rk, 7), 147), (2048,), 208, 99935, jnp.int32), jax.random.randint(jax.random.fold_in(jax.random.fold_in(_rk, 7), 148), (2048,), 152, 99740, jnp.int32), jax.random.randint(jax.random.fold_in(jax.random.fold_in(_rk, 7), 149), (2048,), 264, 99955, jnp.int32), jax.random.randint(jax.random.fold_in(jax.random.fold_in(_rk, 7), 150), (2048,), 33, 99777, jnp.int32), jax.random.randint(jax.random.fold_in(jax.random.fold_in(_rk, 7), 151), (2048,), 54, 99871, jnp.int32), jax.random.randint(jax.random.fold_in(jax.random.fold_in(_rk, 7), 152), (2048,), 238, 99493, jnp.int32), jax.random.randint(jax.random.fold_in(jax.random.fold_in(_rk, 7), 153), (2048,), 69, 99778, jnp.int32), jax.random.randint(jax.random.fold_in(jax.random.fold_in(_rk, 7), 154), (2048,), 130, 99654, jnp.int32), jax.random.randint(jax.random.fold_in(jax.random.fold_in(_rk, 7), 155), (2048,), 120, 99827, jnp.int32), jax.random.randint(jax.random.fold_in(jax.random.fold_in(_rk, 7), 156), (2048,), 120, 12495, jnp.int32), jax.random.randint(jax.random.fold_in(jax.random.fold_in(_rk, 7), 157), (2048,), 24, 99994, jnp.int32), jax.random.randint(jax.random.fold_in(jax.random.fold_in(_rk, 7), 158), (2048,), 23, 99870, jnp.int32), jax.random.randint(jax.random.fold_in(jax.random.fold_in(_rk, 7), 159), (2048,), 10, 99929, jnp.int32), jax.random.randint(jax.random.fold_in(jax.random.fold_in(_rk, 7), 160), (2048,), 87, 99838, jnp.int32), jax.random.randint(jax.random.fold_in(jax.random.fold_in(_rk, 7), 161), (2048,), 9, 99969, jnp.int32), jax.random.randint(jax.random.fold_in(jax.random.fold_in(_rk, 7), 162), (2048,), 83, 99849, jnp.int32), jax.random.randint(jax.random.fold_in(jax.random.fold_in(_rk, 7), 163), (2048,), 41, 99926, jnp.int32), jax.random.randint(jax.random.fold_in(jax.random.fold_in(_rk, 7), 164), (2048,), 24, 99995, jnp.int32), jax.random.randint(jax.random.fold_in(jax.random.fold_in(_rk, 7), 165), (2048,), 124, 99933, jnp.int32), jax.random.randint(jax.random.fold_in(jax.random.fold_in(_rk, 7), 166), (2048,), 149, 99789, jnp.int32), jax.random.randint(jax.random.fold_in(jax.random.fold_in(_rk, 7), 167), (2048,), 86, 99820, jnp.int32), jax.random.randint(jax.random.fold_in(jax.random.fold_in(_rk, 7), 168), (2048,), 6, 99977, jnp.int32), jax.random.randint(jax.random.fold_in(jax.random.fold_in(_rk, 7), 169), (2048,), 104, 12496, jnp.int32), jax.random.randint(jax.random.fold_in(jax.random.fold_in(_rk, 7), 170), (2048,), 34, 99955, jnp.int32), jax.random.randint(jax.random.fold_in(jax.random.fold_in(_rk, 7), 171), (2048,), 22, 99990, jnp.int32), jax.random.randint(jax.random.fold_in(jax.random.fold_in(_rk, 7), 172), (2048,), 78, 99495, jnp.int32), jax.random.randint(jax.random.fold_in(jax.random.fold_in(_rk, 7), 173), (2048,), 64, 12498, jnp.int32), jax.random.randint(jax.random.fold_in(jax.random.fold_in(_rk, 7), 174), (2048,), 123, 99951, jnp.int32), jax.random.randint(jax.random.fold_in(jax.random.fold_in(_rk, 7), 175), (2048,), 17, 99932, jnp.int32), jax.random.randint(jax.random.fold_in(jax.random.fold_in(_rk, 7), 176), (2048,), 162, 99950, jnp.int32), jax.random.randint(jax.random.fold_in(jax.random.fold_in(_rk, 7), 177), (2048,), 48, 12460, jnp.int32), jax.random.randint(jax.random.fold_in(jax.random.fold_in(_rk, 7), 178), (2048,), 175, 99364, jnp.int32), jax.random.randint(jax.random.fold_in(jax.random.fold_in(_rk, 7), 179), (2048,), 83, 99815, jnp.int32), jax.random.randint(jax.random.fold_in(jax.random.fold_in(_rk, 7), 180), (2048,), 51, 99958, jnp.int32), jax.random.randint(jax.random.fold_in(jax.random.fold_in(_rk, 7), 181), (2048,), 56, 99575, jnp.int32), jax.random.randint(jax.random.fold_in(jax.random.fold_in(_rk, 7), 182), (2048,), 62, 99943, jnp.int32), jax.random.randint(jax.random.fold_in(jax.random.fold_in(_rk, 7), 183), (2048,), 170, 99915, jnp.int32), jax.random.randint(jax.random.fold_in(jax.random.fold_in(_rk, 7), 184), (2048,), 139, 99946, jnp.int32), jax.random.randint(jax.random.fold_in(jax.random.fold_in(_rk, 7), 185), (2048,), 55, 99697, jnp.int32), jax.random.randint(jax.random.fold_in(jax.random.fold_in(_rk, 7), 186), (2048,), 378, 99758, jnp.int32), jax.random.randint(jax.random.fold_in(jax.random.fold_in(_rk, 7), 187), (2048,), 22, 99954, jnp.int32), jax.random.randint(jax.random.fold_in(jax.random.fold_in(_rk, 7), 188), (2048,), 40, 99818, jnp.int32), jax.random.randint(jax.random.fold_in(jax.random.fold_in(_rk, 7), 189), (2048,), 25, 99889, jnp.int32), jax.random.randint(jax.random.fold_in(jax.random.fold_in(_rk, 7), 190), (2048,), 87, 99855, jnp.int32), jax.random.randint(jax.random.fold_in(jax.random.fold_in(_rk, 7), 191), (2048,), 80, 99820, jnp.int32), jax.random.randint(jax.random.fold_in(jax.random.fold_in(_rk, 7), 192), (2048,), 33, 99996, jnp.int32), jax.random.randint(jax.random.fold_in(jax.random.fold_in(_rk, 7), 193), (2048,), 60, 99956, jnp.int32), jax.random.randint(jax.random.fold_in(jax.random.fold_in(_rk, 7), 194), (2048,), 272, 99943, jnp.int32), jax.random.randint(jax.random.fold_in(jax.random.fold_in(_rk, 7), 195), (2048,), 72, 99722, jnp.int32), jax.random.randint(jax.random.fold_in(jax.random.fold_in(_rk, 7), 196), (2048,), 124, 99981, jnp.int32), jax.random.randint(jax.random.fold_in(jax.random.fold_in(_rk, 7), 197), (2048,), 55, 99910, jnp.int32), jax.random.randint(jax.random.fold_in(jax.random.fold_in(_rk, 7), 198), (2048,), 136, 99890, jnp.int32), jax.random.randint(jax.random.fold_in(jax.random.fold_in(_rk, 7), 199), (2048,), 23, 99955, jnp.int32)], axis=1)
        r_exp_item_cat = jnp.stack([jax.random.randint(jax.random.fold_in(jax.random.fold_in(_rk, 8), 0), (2048,), 2, 1000, jnp.int32), jax.random.randint(jax.random.fold_in(jax.random.fold_in(_rk, 8), 1), (2048,), 2, 1000, jnp.int32), jax.random.randint(jax.random.fold_in(jax.random.fold_in(_rk, 8), 2), (2048,), 0, 999, jnp.int32), jax.random.randint(jax.random.fold_in(jax.random.fold_in(_rk, 8), 3), (2048,), 3, 1000, jnp.int32), jax.random.randint(jax.random.fold_in(jax.random.fold_in(_rk, 8), 4), (2048,), 3, 1000, jnp.int32), jax.random.randint(jax.random.fold_in(jax.random.fold_in(_rk, 8), 5), (2048,), 0, 1000, jnp.int32), jax.random.randint(jax.random.fold_in(jax.random.fold_in(_rk, 8), 6), (2048,), 0, 1000, jnp.int32), jax.random.randint(jax.random.fold_in(jax.random.fold_in(_rk, 8), 7), (2048,), 0, 1000, jnp.int32), jax.random.randint(jax.random.fold_in(jax.random.fold_in(_rk, 8), 8), (2048,), 0, 1000, jnp.int32), jax.random.randint(jax.random.fold_in(jax.random.fold_in(_rk, 8), 9), (2048,), 1, 1000, jnp.int32), jax.random.randint(jax.random.fold_in(jax.random.fold_in(_rk, 8), 10), (2048,), 0, 1000, jnp.int32), jax.random.randint(jax.random.fold_in(jax.random.fold_in(_rk, 8), 11), (2048,), 0, 998, jnp.int32), jax.random.randint(jax.random.fold_in(jax.random.fold_in(_rk, 8), 12), (2048,), 1, 1000, jnp.int32), jax.random.randint(jax.random.fold_in(jax.random.fold_in(_rk, 8), 13), (2048,), 0, 999, jnp.int32), jax.random.randint(jax.random.fold_in(jax.random.fold_in(_rk, 8), 14), (2048,), 0, 1000, jnp.int32), jax.random.randint(jax.random.fold_in(jax.random.fold_in(_rk, 8), 15), (2048,), 0, 1000, jnp.int32), jax.random.randint(jax.random.fold_in(jax.random.fold_in(_rk, 8), 16), (2048,), 0, 1000, jnp.int32), jax.random.randint(jax.random.fold_in(jax.random.fold_in(_rk, 8), 17), (2048,), 0, 1000, jnp.int32), jax.random.randint(jax.random.fold_in(jax.random.fold_in(_rk, 8), 18), (2048,), 0, 999, jnp.int32), jax.random.randint(jax.random.fold_in(jax.random.fold_in(_rk, 8), 19), (2048,), 0, 1000, jnp.int32), jax.random.randint(jax.random.fold_in(jax.random.fold_in(_rk, 8), 20), (2048,), 1, 999, jnp.int32), jax.random.randint(jax.random.fold_in(jax.random.fold_in(_rk, 8), 21), (2048,), 0, 999, jnp.int32), jax.random.randint(jax.random.fold_in(jax.random.fold_in(_rk, 8), 22), (2048,), 0, 1000, jnp.int32), jax.random.randint(jax.random.fold_in(jax.random.fold_in(_rk, 8), 23), (2048,), 1, 1000, jnp.int32), jax.random.randint(jax.random.fold_in(jax.random.fold_in(_rk, 8), 24), (2048,), 1, 1000, jnp.int32), jax.random.randint(jax.random.fold_in(jax.random.fold_in(_rk, 8), 25), (2048,), 0, 1000, jnp.int32), jax.random.randint(jax.random.fold_in(jax.random.fold_in(_rk, 8), 26), (2048,), 2, 999, jnp.int32), jax.random.randint(jax.random.fold_in(jax.random.fold_in(_rk, 8), 27), (2048,), 0, 1000, jnp.int32), jax.random.randint(jax.random.fold_in(jax.random.fold_in(_rk, 8), 28), (2048,), 0, 1000, jnp.int32), jax.random.randint(jax.random.fold_in(jax.random.fold_in(_rk, 8), 29), (2048,), 0, 999, jnp.int32), jax.random.randint(jax.random.fold_in(jax.random.fold_in(_rk, 8), 30), (2048,), 0, 999, jnp.int32), jax.random.randint(jax.random.fold_in(jax.random.fold_in(_rk, 8), 31), (2048,), 1, 1000, jnp.int32), jax.random.randint(jax.random.fold_in(jax.random.fold_in(_rk, 8), 32), (2048,), 0, 1000, jnp.int32), jax.random.randint(jax.random.fold_in(jax.random.fold_in(_rk, 8), 33), (2048,), 4, 1000, jnp.int32), jax.random.randint(jax.random.fold_in(jax.random.fold_in(_rk, 8), 34), (2048,), 0, 1000, jnp.int32), jax.random.randint(jax.random.fold_in(jax.random.fold_in(_rk, 8), 35), (2048,), 0, 1000, jnp.int32), jax.random.randint(jax.random.fold_in(jax.random.fold_in(_rk, 8), 36), (2048,), 1, 999, jnp.int32), jax.random.randint(jax.random.fold_in(jax.random.fold_in(_rk, 8), 37), (2048,), 0, 999, jnp.int32), jax.random.randint(jax.random.fold_in(jax.random.fold_in(_rk, 8), 38), (2048,), 0, 1000, jnp.int32), jax.random.randint(jax.random.fold_in(jax.random.fold_in(_rk, 8), 39), (2048,), 2, 1000, jnp.int32), jax.random.randint(jax.random.fold_in(jax.random.fold_in(_rk, 8), 40), (2048,), 0, 999, jnp.int32), jax.random.randint(jax.random.fold_in(jax.random.fold_in(_rk, 8), 41), (2048,), 0, 1000, jnp.int32), jax.random.randint(jax.random.fold_in(jax.random.fold_in(_rk, 8), 42), (2048,), 0, 1000, jnp.int32), jax.random.randint(jax.random.fold_in(jax.random.fold_in(_rk, 8), 43), (2048,), 0, 1000, jnp.int32), jax.random.randint(jax.random.fold_in(jax.random.fold_in(_rk, 8), 44), (2048,), 0, 1000, jnp.int32), jax.random.randint(jax.random.fold_in(jax.random.fold_in(_rk, 8), 45), (2048,), 0, 999, jnp.int32), jax.random.randint(jax.random.fold_in(jax.random.fold_in(_rk, 8), 46), (2048,), 3, 998, jnp.int32), jax.random.randint(jax.random.fold_in(jax.random.fold_in(_rk, 8), 47), (2048,), 1, 1000, jnp.int32), jax.random.randint(jax.random.fold_in(jax.random.fold_in(_rk, 8), 48), (2048,), 0, 1000, jnp.int32), jax.random.randint(jax.random.fold_in(jax.random.fold_in(_rk, 8), 49), (2048,), 0, 999, jnp.int32), jax.random.randint(jax.random.fold_in(jax.random.fold_in(_rk, 8), 50), (2048,), 0, 1000, jnp.int32), jax.random.randint(jax.random.fold_in(jax.random.fold_in(_rk, 8), 51), (2048,), 0, 1000, jnp.int32), jax.random.randint(jax.random.fold_in(jax.random.fold_in(_rk, 8), 52), (2048,), 1, 999, jnp.int32), jax.random.randint(jax.random.fold_in(jax.random.fold_in(_rk, 8), 53), (2048,), 0, 995, jnp.int32), jax.random.randint(jax.random.fold_in(jax.random.fold_in(_rk, 8), 54), (2048,), 0, 998, jnp.int32), jax.random.randint(jax.random.fold_in(jax.random.fold_in(_rk, 8), 55), (2048,), 1, 999, jnp.int32), jax.random.randint(jax.random.fold_in(jax.random.fold_in(_rk, 8), 56), (2048,), 0, 1000, jnp.int32), jax.random.randint(jax.random.fold_in(jax.random.fold_in(_rk, 8), 57), (2048,), 0, 1000, jnp.int32), jax.random.randint(jax.random.fold_in(jax.random.fold_in(_rk, 8), 58), (2048,), 2, 1000, jnp.int32), jax.random.randint(jax.random.fold_in(jax.random.fold_in(_rk, 8), 59), (2048,), 0, 998, jnp.int32), jax.random.randint(jax.random.fold_in(jax.random.fold_in(_rk, 8), 60), (2048,), 1, 999, jnp.int32), jax.random.randint(jax.random.fold_in(jax.random.fold_in(_rk, 8), 61), (2048,), 0, 999, jnp.int32), jax.random.randint(jax.random.fold_in(jax.random.fold_in(_rk, 8), 62), (2048,), 1, 1000, jnp.int32), jax.random.randint(jax.random.fold_in(jax.random.fold_in(_rk, 8), 63), (2048,), 0, 1000, jnp.int32), jax.random.randint(jax.random.fold_in(jax.random.fold_in(_rk, 8), 64), (2048,), 2, 1000, jnp.int32), jax.random.randint(jax.random.fold_in(jax.random.fold_in(_rk, 8), 65), (2048,), 1, 1000, jnp.int32), jax.random.randint(jax.random.fold_in(jax.random.fold_in(_rk, 8), 66), (2048,), 0, 1000, jnp.int32), jax.random.randint(jax.random.fold_in(jax.random.fold_in(_rk, 8), 67), (2048,), 0, 1000, jnp.int32), jax.random.randint(jax.random.fold_in(jax.random.fold_in(_rk, 8), 68), (2048,), 0, 996, jnp.int32), jax.random.randint(jax.random.fold_in(jax.random.fold_in(_rk, 8), 69), (2048,), 0, 1000, jnp.int32), jax.random.randint(jax.random.fold_in(jax.random.fold_in(_rk, 8), 70), (2048,), 1, 1000, jnp.int32), jax.random.randint(jax.random.fold_in(jax.random.fold_in(_rk, 8), 71), (2048,), 0, 999, jnp.int32), jax.random.randint(jax.random.fold_in(jax.random.fold_in(_rk, 8), 72), (2048,), 2, 1000, jnp.int32), jax.random.randint(jax.random.fold_in(jax.random.fold_in(_rk, 8), 73), (2048,), 2, 1000, jnp.int32), jax.random.randint(jax.random.fold_in(jax.random.fold_in(_rk, 8), 74), (2048,), 3, 999, jnp.int32), jax.random.randint(jax.random.fold_in(jax.random.fold_in(_rk, 8), 75), (2048,), 0, 1000, jnp.int32), jax.random.randint(jax.random.fold_in(jax.random.fold_in(_rk, 8), 76), (2048,), 4, 999, jnp.int32), jax.random.randint(jax.random.fold_in(jax.random.fold_in(_rk, 8), 77), (2048,), 1, 999, jnp.int32), jax.random.randint(jax.random.fold_in(jax.random.fold_in(_rk, 8), 78), (2048,), 0, 1000, jnp.int32), jax.random.randint(jax.random.fold_in(jax.random.fold_in(_rk, 8), 79), (2048,), 1, 1000, jnp.int32), jax.random.randint(jax.random.fold_in(jax.random.fold_in(_rk, 8), 80), (2048,), 0, 1000, jnp.int32), jax.random.randint(jax.random.fold_in(jax.random.fold_in(_rk, 8), 81), (2048,), 1, 1000, jnp.int32), jax.random.randint(jax.random.fold_in(jax.random.fold_in(_rk, 8), 82), (2048,), 0, 1000, jnp.int32), jax.random.randint(jax.random.fold_in(jax.random.fold_in(_rk, 8), 83), (2048,), 0, 1000, jnp.int32), jax.random.randint(jax.random.fold_in(jax.random.fold_in(_rk, 8), 84), (2048,), 1, 1000, jnp.int32), jax.random.randint(jax.random.fold_in(jax.random.fold_in(_rk, 8), 85), (2048,), 0, 1000, jnp.int32), jax.random.randint(jax.random.fold_in(jax.random.fold_in(_rk, 8), 86), (2048,), 0, 1000, jnp.int32), jax.random.randint(jax.random.fold_in(jax.random.fold_in(_rk, 8), 87), (2048,), 0, 994, jnp.int32), jax.random.randint(jax.random.fold_in(jax.random.fold_in(_rk, 8), 88), (2048,), 0, 1000, jnp.int32), jax.random.randint(jax.random.fold_in(jax.random.fold_in(_rk, 8), 89), (2048,), 0, 1000, jnp.int32), jax.random.randint(jax.random.fold_in(jax.random.fold_in(_rk, 8), 90), (2048,), 0, 1000, jnp.int32), jax.random.randint(jax.random.fold_in(jax.random.fold_in(_rk, 8), 91), (2048,), 0, 999, jnp.int32), jax.random.randint(jax.random.fold_in(jax.random.fold_in(_rk, 8), 92), (2048,), 1, 1000, jnp.int32), jax.random.randint(jax.random.fold_in(jax.random.fold_in(_rk, 8), 93), (2048,), 0, 1000, jnp.int32), jax.random.randint(jax.random.fold_in(jax.random.fold_in(_rk, 8), 94), (2048,), 0, 1000, jnp.int32), jax.random.randint(jax.random.fold_in(jax.random.fold_in(_rk, 8), 95), (2048,), 1, 1000, jnp.int32), jax.random.randint(jax.random.fold_in(jax.random.fold_in(_rk, 8), 96), (2048,), 0, 1000, jnp.int32), jax.random.randint(jax.random.fold_in(jax.random.fold_in(_rk, 8), 97), (2048,), 0, 998, jnp.int32), jax.random.randint(jax.random.fold_in(jax.random.fold_in(_rk, 8), 98), (2048,), 0, 1000, jnp.int32), jax.random.randint(jax.random.fold_in(jax.random.fold_in(_rk, 8), 99), (2048,), 2, 1000, jnp.int32), jax.random.randint(jax.random.fold_in(jax.random.fold_in(_rk, 8), 100), (2048,), 0, 998, jnp.int32), jax.random.randint(jax.random.fold_in(jax.random.fold_in(_rk, 8), 101), (2048,), 1, 999, jnp.int32), jax.random.randint(jax.random.fold_in(jax.random.fold_in(_rk, 8), 102), (2048,), 0, 1000, jnp.int32), jax.random.randint(jax.random.fold_in(jax.random.fold_in(_rk, 8), 103), (2048,), 0, 1000, jnp.int32), jax.random.randint(jax.random.fold_in(jax.random.fold_in(_rk, 8), 104), (2048,), 0, 1000, jnp.int32), jax.random.randint(jax.random.fold_in(jax.random.fold_in(_rk, 8), 105), (2048,), 0, 1000, jnp.int32), jax.random.randint(jax.random.fold_in(jax.random.fold_in(_rk, 8), 106), (2048,), 1, 1000, jnp.int32), jax.random.randint(jax.random.fold_in(jax.random.fold_in(_rk, 8), 107), (2048,), 1, 1000, jnp.int32), jax.random.randint(jax.random.fold_in(jax.random.fold_in(_rk, 8), 108), (2048,), 0, 996, jnp.int32), jax.random.randint(jax.random.fold_in(jax.random.fold_in(_rk, 8), 109), (2048,), 0, 1000, jnp.int32), jax.random.randint(jax.random.fold_in(jax.random.fold_in(_rk, 8), 110), (2048,), 0, 1000, jnp.int32), jax.random.randint(jax.random.fold_in(jax.random.fold_in(_rk, 8), 111), (2048,), 0, 1000, jnp.int32), jax.random.randint(jax.random.fold_in(jax.random.fold_in(_rk, 8), 112), (2048,), 0, 996, jnp.int32), jax.random.randint(jax.random.fold_in(jax.random.fold_in(_rk, 8), 113), (2048,), 0, 997, jnp.int32), jax.random.randint(jax.random.fold_in(jax.random.fold_in(_rk, 8), 114), (2048,), 0, 999, jnp.int32), jax.random.randint(jax.random.fold_in(jax.random.fold_in(_rk, 8), 115), (2048,), 1, 999, jnp.int32), jax.random.randint(jax.random.fold_in(jax.random.fold_in(_rk, 8), 116), (2048,), 0, 1000, jnp.int32), jax.random.randint(jax.random.fold_in(jax.random.fold_in(_rk, 8), 117), (2048,), 0, 997, jnp.int32), jax.random.randint(jax.random.fold_in(jax.random.fold_in(_rk, 8), 118), (2048,), 0, 1000, jnp.int32), jax.random.randint(jax.random.fold_in(jax.random.fold_in(_rk, 8), 119), (2048,), 1, 1000, jnp.int32), jax.random.randint(jax.random.fold_in(jax.random.fold_in(_rk, 8), 120), (2048,), 1, 1000, jnp.int32), jax.random.randint(jax.random.fold_in(jax.random.fold_in(_rk, 8), 121), (2048,), 0, 1000, jnp.int32), jax.random.randint(jax.random.fold_in(jax.random.fold_in(_rk, 8), 122), (2048,), 0, 999, jnp.int32), jax.random.randint(jax.random.fold_in(jax.random.fold_in(_rk, 8), 123), (2048,), 0, 1000, jnp.int32), jax.random.randint(jax.random.fold_in(jax.random.fold_in(_rk, 8), 124), (2048,), 0, 1000, jnp.int32), jax.random.randint(jax.random.fold_in(jax.random.fold_in(_rk, 8), 125), (2048,), 1, 999, jnp.int32), jax.random.randint(jax.random.fold_in(jax.random.fold_in(_rk, 8), 126), (2048,), 0, 1000, jnp.int32), jax.random.randint(jax.random.fold_in(jax.random.fold_in(_rk, 8), 127), (2048,), 0, 1000, jnp.int32), jax.random.randint(jax.random.fold_in(jax.random.fold_in(_rk, 8), 128), (2048,), 0, 1000, jnp.int32), jax.random.randint(jax.random.fold_in(jax.random.fold_in(_rk, 8), 129), (2048,), 5, 1000, jnp.int32), jax.random.randint(jax.random.fold_in(jax.random.fold_in(_rk, 8), 130), (2048,), 1, 1000, jnp.int32), jax.random.randint(jax.random.fold_in(jax.random.fold_in(_rk, 8), 131), (2048,), 1, 998, jnp.int32), jax.random.randint(jax.random.fold_in(jax.random.fold_in(_rk, 8), 132), (2048,), 0, 1000, jnp.int32), jax.random.randint(jax.random.fold_in(jax.random.fold_in(_rk, 8), 133), (2048,), 2, 1000, jnp.int32), jax.random.randint(jax.random.fold_in(jax.random.fold_in(_rk, 8), 134), (2048,), 1, 1000, jnp.int32), jax.random.randint(jax.random.fold_in(jax.random.fold_in(_rk, 8), 135), (2048,), 0, 1000, jnp.int32), jax.random.randint(jax.random.fold_in(jax.random.fold_in(_rk, 8), 136), (2048,), 0, 1000, jnp.int32), jax.random.randint(jax.random.fold_in(jax.random.fold_in(_rk, 8), 137), (2048,), 1, 997, jnp.int32), jax.random.randint(jax.random.fold_in(jax.random.fold_in(_rk, 8), 138), (2048,), 0, 1000, jnp.int32), jax.random.randint(jax.random.fold_in(jax.random.fold_in(_rk, 8), 139), (2048,), 0, 1000, jnp.int32), jax.random.randint(jax.random.fold_in(jax.random.fold_in(_rk, 8), 140), (2048,), 0, 1000, jnp.int32), jax.random.randint(jax.random.fold_in(jax.random.fold_in(_rk, 8), 141), (2048,), 0, 1000, jnp.int32), jax.random.randint(jax.random.fold_in(jax.random.fold_in(_rk, 8), 142), (2048,), 0, 1000, jnp.int32), jax.random.randint(jax.random.fold_in(jax.random.fold_in(_rk, 8), 143), (2048,), 0, 999, jnp.int32), jax.random.randint(jax.random.fold_in(jax.random.fold_in(_rk, 8), 144), (2048,), 1, 999, jnp.int32), jax.random.randint(jax.random.fold_in(jax.random.fold_in(_rk, 8), 145), (2048,), 0, 1000, jnp.int32), jax.random.randint(jax.random.fold_in(jax.random.fold_in(_rk, 8), 146), (2048,), 0, 1000, jnp.int32), jax.random.randint(jax.random.fold_in(jax.random.fold_in(_rk, 8), 147), (2048,), 0, 1000, jnp.int32), jax.random.randint(jax.random.fold_in(jax.random.fold_in(_rk, 8), 148), (2048,), 1, 1000, jnp.int32), jax.random.randint(jax.random.fold_in(jax.random.fold_in(_rk, 8), 149), (2048,), 0, 1000, jnp.int32), jax.random.randint(jax.random.fold_in(jax.random.fold_in(_rk, 8), 150), (2048,), 1, 1000, jnp.int32), jax.random.randint(jax.random.fold_in(jax.random.fold_in(_rk, 8), 151), (2048,), 1, 1000, jnp.int32), jax.random.randint(jax.random.fold_in(jax.random.fold_in(_rk, 8), 152), (2048,), 0, 1000, jnp.int32), jax.random.randint(jax.random.fold_in(jax.random.fold_in(_rk, 8), 153), (2048,), 3, 1000, jnp.int32), jax.random.randint(jax.random.fold_in(jax.random.fold_in(_rk, 8), 154), (2048,), 2, 998, jnp.int32), jax.random.randint(jax.random.fold_in(jax.random.fold_in(_rk, 8), 155), (2048,), 0, 1000, jnp.int32), jax.random.randint(jax.random.fold_in(jax.random.fold_in(_rk, 8), 156), (2048,), 0, 1000, jnp.int32), jax.random.randint(jax.random.fold_in(jax.random.fold_in(_rk, 8), 157), (2048,), 0, 1000, jnp.int32), jax.random.randint(jax.random.fold_in(jax.random.fold_in(_rk, 8), 158), (2048,), 0, 999, jnp.int32), jax.random.randint(jax.random.fold_in(jax.random.fold_in(_rk, 8), 159), (2048,), 0, 997, jnp.int32), jax.random.randint(jax.random.fold_in(jax.random.fold_in(_rk, 8), 160), (2048,), 1, 999, jnp.int32), jax.random.randint(jax.random.fold_in(jax.random.fold_in(_rk, 8), 161), (2048,), 0, 1000, jnp.int32), jax.random.randint(jax.random.fold_in(jax.random.fold_in(_rk, 8), 162), (2048,), 2, 999, jnp.int32), jax.random.randint(jax.random.fold_in(jax.random.fold_in(_rk, 8), 163), (2048,), 1, 1000, jnp.int32), jax.random.randint(jax.random.fold_in(jax.random.fold_in(_rk, 8), 164), (2048,), 0, 1000, jnp.int32), jax.random.randint(jax.random.fold_in(jax.random.fold_in(_rk, 8), 165), (2048,), 0, 997, jnp.int32), jax.random.randint(jax.random.fold_in(jax.random.fold_in(_rk, 8), 166), (2048,), 0, 1000, jnp.int32), jax.random.randint(jax.random.fold_in(jax.random.fold_in(_rk, 8), 167), (2048,), 1, 1000, jnp.int32), jax.random.randint(jax.random.fold_in(jax.random.fold_in(_rk, 8), 168), (2048,), 0, 1000, jnp.int32), jax.random.randint(jax.random.fold_in(jax.random.fold_in(_rk, 8), 169), (2048,), 1, 1000, jnp.int32), jax.random.randint(jax.random.fold_in(jax.random.fold_in(_rk, 8), 170), (2048,), 0, 999, jnp.int32), jax.random.randint(jax.random.fold_in(jax.random.fold_in(_rk, 8), 171), (2048,), 0, 1000, jnp.int32), jax.random.randint(jax.random.fold_in(jax.random.fold_in(_rk, 8), 172), (2048,), 0, 1000, jnp.int32), jax.random.randint(jax.random.fold_in(jax.random.fold_in(_rk, 8), 173), (2048,), 1, 1000, jnp.int32), jax.random.randint(jax.random.fold_in(jax.random.fold_in(_rk, 8), 174), (2048,), 0, 999, jnp.int32), jax.random.randint(jax.random.fold_in(jax.random.fold_in(_rk, 8), 175), (2048,), 2, 1000, jnp.int32), jax.random.randint(jax.random.fold_in(jax.random.fold_in(_rk, 8), 176), (2048,), 0, 998, jnp.int32), jax.random.randint(jax.random.fold_in(jax.random.fold_in(_rk, 8), 177), (2048,), 0, 1000, jnp.int32), jax.random.randint(jax.random.fold_in(jax.random.fold_in(_rk, 8), 178), (2048,), 1, 1000, jnp.int32), jax.random.randint(jax.random.fold_in(jax.random.fold_in(_rk, 8), 179), (2048,), 0, 999, jnp.int32), jax.random.randint(jax.random.fold_in(jax.random.fold_in(_rk, 8), 180), (2048,), 0, 1000, jnp.int32), jax.random.randint(jax.random.fold_in(jax.random.fold_in(_rk, 8), 181), (2048,), 0, 1000, jnp.int32), jax.random.randint(jax.random.fold_in(jax.random.fold_in(_rk, 8), 182), (2048,), 0, 998, jnp.int32), jax.random.randint(jax.random.fold_in(jax.random.fold_in(_rk, 8), 183), (2048,), 1, 1000, jnp.int32), jax.random.randint(jax.random.fold_in(jax.random.fold_in(_rk, 8), 184), (2048,), 0, 1000, jnp.int32), jax.random.randint(jax.random.fold_in(jax.random.fold_in(_rk, 8), 185), (2048,), 0, 999, jnp.int32), jax.random.randint(jax.random.fold_in(jax.random.fold_in(_rk, 8), 186), (2048,), 0, 999, jnp.int32), jax.random.randint(jax.random.fold_in(jax.random.fold_in(_rk, 8), 187), (2048,), 1, 999, jnp.int32), jax.random.randint(jax.random.fold_in(jax.random.fold_in(_rk, 8), 188), (2048,), 0, 999, jnp.int32), jax.random.randint(jax.random.fold_in(jax.random.fold_in(_rk, 8), 189), (2048,), 0, 1000, jnp.int32), jax.random.randint(jax.random.fold_in(jax.random.fold_in(_rk, 8), 190), (2048,), 0, 1000, jnp.int32), jax.random.randint(jax.random.fold_in(jax.random.fold_in(_rk, 8), 191), (2048,), 2, 999, jnp.int32), jax.random.randint(jax.random.fold_in(jax.random.fold_in(_rk, 8), 192), (2048,), 0, 1000, jnp.int32), jax.random.randint(jax.random.fold_in(jax.random.fold_in(_rk, 8), 193), (2048,), 0, 1000, jnp.int32), jax.random.randint(jax.random.fold_in(jax.random.fold_in(_rk, 8), 194), (2048,), 1, 1000, jnp.int32), jax.random.randint(jax.random.fold_in(jax.random.fold_in(_rk, 8), 195), (2048,), 2, 1000, jnp.int32), jax.random.randint(jax.random.fold_in(jax.random.fold_in(_rk, 8), 196), (2048,), 0, 998, jnp.int32), jax.random.randint(jax.random.fold_in(jax.random.fold_in(_rk, 8), 197), (2048,), 0, 1000, jnp.int32), jax.random.randint(jax.random.fold_in(jax.random.fold_in(_rk, 8), 198), (2048,), 0, 1000, jnp.int32), jax.random.randint(jax.random.fold_in(jax.random.fold_in(_rk, 8), 199), (2048,), 1, 998, jnp.int32)], axis=1)
        r_ipv_item_id = jnp.stack([jax.random.randint(jax.random.fold_in(jax.random.fold_in(_rk, 9), 0), (2048,), 64, 99938, jnp.int32), jax.random.randint(jax.random.fold_in(jax.random.fold_in(_rk, 9), 1), (2048,), 3, 99950, jnp.int32), jax.random.randint(jax.random.fold_in(jax.random.fold_in(_rk, 9), 2), (2048,), 18, 99921, jnp.int32), jax.random.randint(jax.random.fold_in(jax.random.fold_in(_rk, 9), 3), (2048,), 13, 99873, jnp.int32), jax.random.randint(jax.random.fold_in(jax.random.fold_in(_rk, 9), 4), (2048,), 31, 12495, jnp.int32), jax.random.randint(jax.random.fold_in(jax.random.fold_in(_rk, 9), 5), (2048,), 10, 99884, jnp.int32), jax.random.randint(jax.random.fold_in(jax.random.fold_in(_rk, 9), 6), (2048,), 92, 99990, jnp.int32), jax.random.randint(jax.random.fold_in(jax.random.fold_in(_rk, 9), 7), (2048,), 7, 12499, jnp.int32), jax.random.randint(jax.random.fold_in(jax.random.fold_in(_rk, 9), 8), (2048,), 44, 12491, jnp.int32), jax.random.randint(jax.random.fold_in(jax.random.fold_in(_rk, 9), 9), (2048,), 65, 99923, jnp.int32), jax.random.randint(jax.random.fold_in(jax.random.fold_in(_rk, 9), 10), (2048,), 31, 99909, jnp.int32), jax.random.randint(jax.random.fold_in(jax.random.fold_in(_rk, 9), 11), (2048,), 331, 99993, jnp.int32), jax.random.randint(jax.random.fold_in(jax.random.fold_in(_rk, 9), 12), (2048,), 171, 99975, jnp.int32), jax.random.randint(jax.random.fold_in(jax.random.fold_in(_rk, 9), 13), (2048,), 84, 99933, jnp.int32), jax.random.randint(jax.random.fold_in(jax.random.fold_in(_rk, 9), 14), (2048,), 5, 99894, jnp.int32), jax.random.randint(jax.random.fold_in(jax.random.fold_in(_rk, 9), 15), (2048,), 12, 99821, jnp.int32), jax.random.randint(jax.random.fold_in(jax.random.fold_in(_rk, 9), 16), (2048,), 5, 99997, jnp.int32), jax.random.randint(jax.random.fold_in(jax.random.fold_in(_rk, 9), 17), (2048,), 162, 12495, jnp.int32), jax.random.randint(jax.random.fold_in(jax.random.fold_in(_rk, 9), 18), (2048,), 51, 99900, jnp.int32), jax.random.randint(jax.random.fold_in(jax.random.fold_in(_rk, 9), 19), (2048,), 101, 99979, jnp.int32), jax.random.randint(jax.random.fold_in(jax.random.fold_in(_rk, 9), 20), (2048,), 381, 99787, jnp.int32), jax.random.randint(jax.random.fold_in(jax.random.fold_in(_rk, 9), 21), (2048,), 57, 12478, jnp.int32), jax.random.randint(jax.random.fold_in(jax.random.fold_in(_rk, 9), 22), (2048,), 139, 99948, jnp.int32), jax.random.randint(jax.random.fold_in(jax.random.fold_in(_rk, 9), 23), (2048,), 47, 99695, jnp.int32), jax.random.randint(jax.random.fold_in(jax.random.fold_in(_rk, 9), 24), (2048,), 193, 12495, jnp.int32), jax.random.randint(jax.random.fold_in(jax.random.fold_in(_rk, 9), 25), (2048,), 64, 99878, jnp.int32), jax.random.randint(jax.random.fold_in(jax.random.fold_in(_rk, 9), 26), (2048,), 5, 99972, jnp.int32), jax.random.randint(jax.random.fold_in(jax.random.fold_in(_rk, 9), 27), (2048,), 68, 99965, jnp.int32), jax.random.randint(jax.random.fold_in(jax.random.fold_in(_rk, 9), 28), (2048,), 9, 99820, jnp.int32), jax.random.randint(jax.random.fold_in(jax.random.fold_in(_rk, 9), 29), (2048,), 30, 99991, jnp.int32), jax.random.randint(jax.random.fold_in(jax.random.fold_in(_rk, 9), 30), (2048,), 121, 99843, jnp.int32), jax.random.randint(jax.random.fold_in(jax.random.fold_in(_rk, 9), 31), (2048,), 94, 99911, jnp.int32), jax.random.randint(jax.random.fold_in(jax.random.fold_in(_rk, 9), 32), (2048,), 38, 99909, jnp.int32), jax.random.randint(jax.random.fold_in(jax.random.fold_in(_rk, 9), 33), (2048,), 27, 99996, jnp.int32), jax.random.randint(jax.random.fold_in(jax.random.fold_in(_rk, 9), 34), (2048,), 191, 99990, jnp.int32), jax.random.randint(jax.random.fold_in(jax.random.fold_in(_rk, 9), 35), (2048,), 51, 12473, jnp.int32), jax.random.randint(jax.random.fold_in(jax.random.fold_in(_rk, 9), 36), (2048,), 200, 99935, jnp.int32), jax.random.randint(jax.random.fold_in(jax.random.fold_in(_rk, 9), 37), (2048,), 30, 99963, jnp.int32), jax.random.randint(jax.random.fold_in(jax.random.fold_in(_rk, 9), 38), (2048,), 181, 99945, jnp.int32), jax.random.randint(jax.random.fold_in(jax.random.fold_in(_rk, 9), 39), (2048,), 8, 99999, jnp.int32), jax.random.randint(jax.random.fold_in(jax.random.fold_in(_rk, 9), 40), (2048,), 233, 99989, jnp.int32), jax.random.randint(jax.random.fold_in(jax.random.fold_in(_rk, 9), 41), (2048,), 70, 99995, jnp.int32), jax.random.randint(jax.random.fold_in(jax.random.fold_in(_rk, 9), 42), (2048,), 21, 99924, jnp.int32), jax.random.randint(jax.random.fold_in(jax.random.fold_in(_rk, 9), 43), (2048,), 136, 99998, jnp.int32), jax.random.randint(jax.random.fold_in(jax.random.fold_in(_rk, 9), 44), (2048,), 12, 99954, jnp.int32), jax.random.randint(jax.random.fold_in(jax.random.fold_in(_rk, 9), 45), (2048,), 41, 99956, jnp.int32), jax.random.randint(jax.random.fold_in(jax.random.fold_in(_rk, 9), 46), (2048,), 21, 99603, jnp.int32), jax.random.randint(jax.random.fold_in(jax.random.fold_in(_rk, 9), 47), (2048,), 67, 99884, jnp.int32), jax.random.randint(jax.random.fold_in(jax.random.fold_in(_rk, 9), 48), (2048,), 83, 99991, jnp.int32), jax.random.randint(jax.random.fold_in(jax.random.fold_in(_rk, 9), 49), (2048,), 28, 99989, jnp.int32), jax.random.randint(jax.random.fold_in(jax.random.fold_in(_rk, 9), 50), (2048,), 63, 99982, jnp.int32), jax.random.randint(jax.random.fold_in(jax.random.fold_in(_rk, 9), 51), (2048,), 1, 99636, jnp.int32), jax.random.randint(jax.random.fold_in(jax.random.fold_in(_rk, 9), 52), (2048,), 41, 99945, jnp.int32), jax.random.randint(jax.random.fold_in(jax.random.fold_in(_rk, 9), 53), (2048,), 196, 99970, jnp.int32), jax.random.randint(jax.random.fold_in(jax.random.fold_in(_rk, 9), 54), (2048,), 45, 99999, jnp.int32), jax.random.randint(jax.random.fold_in(jax.random.fold_in(_rk, 9), 55), (2048,), 163, 99950, jnp.int32), jax.random.randint(jax.random.fold_in(jax.random.fold_in(_rk, 9), 56), (2048,), 91, 99940, jnp.int32), jax.random.randint(jax.random.fold_in(jax.random.fold_in(_rk, 9), 57), (2048,), 150, 99965, jnp.int32), jax.random.randint(jax.random.fold_in(jax.random.fold_in(_rk, 9), 58), (2048,), 230, 99982, jnp.int32), jax.random.randint(jax.random.fold_in(jax.random.fold_in(_rk, 9), 59), (2048,), 64, 99969, jnp.int32), jax.random.randint(jax.random.fold_in(jax.random.fold_in(_rk, 9), 60), (2048,), 154, 99884, jnp.int32), jax.random.randint(jax.random.fold_in(jax.random.fold_in(_rk, 9), 61), (2048,), 52, 99945, jnp.int32), jax.random.randint(jax.random.fold_in(jax.random.fold_in(_rk, 9), 62), (2048,), 3, 99997, jnp.int32), jax.random.randint(jax.random.fold_in(jax.random.fold_in(_rk, 9), 63), (2048,), 15, 99925, jnp.int32), jax.random.randint(jax.random.fold_in(jax.random.fold_in(_rk, 9), 64), (2048,), 22, 99822, jnp.int32), jax.random.randint(jax.random.fold_in(jax.random.fold_in(_rk, 9), 65), (2048,), 91, 99897, jnp.int32), jax.random.randint(jax.random.fold_in(jax.random.fold_in(_rk, 9), 66), (2048,), 20, 12488, jnp.int32), jax.random.randint(jax.random.fold_in(jax.random.fold_in(_rk, 9), 67), (2048,), 71, 99989, jnp.int32), jax.random.randint(jax.random.fold_in(jax.random.fold_in(_rk, 9), 68), (2048,), 79, 99981, jnp.int32), jax.random.randint(jax.random.fold_in(jax.random.fold_in(_rk, 9), 69), (2048,), 156, 99986, jnp.int32), jax.random.randint(jax.random.fold_in(jax.random.fold_in(_rk, 9), 70), (2048,), 53, 99893, jnp.int32), jax.random.randint(jax.random.fold_in(jax.random.fold_in(_rk, 9), 71), (2048,), 52, 99739, jnp.int32), jax.random.randint(jax.random.fold_in(jax.random.fold_in(_rk, 9), 72), (2048,), 52, 99943, jnp.int32), jax.random.randint(jax.random.fold_in(jax.random.fold_in(_rk, 9), 73), (2048,), 656, 99981, jnp.int32), jax.random.randint(jax.random.fold_in(jax.random.fold_in(_rk, 9), 74), (2048,), 44, 99905, jnp.int32), jax.random.randint(jax.random.fold_in(jax.random.fold_in(_rk, 9), 75), (2048,), 73, 99810, jnp.int32), jax.random.randint(jax.random.fold_in(jax.random.fold_in(_rk, 9), 76), (2048,), 12, 99902, jnp.int32), jax.random.randint(jax.random.fold_in(jax.random.fold_in(_rk, 9), 77), (2048,), 2, 99978, jnp.int32), jax.random.randint(jax.random.fold_in(jax.random.fold_in(_rk, 9), 78), (2048,), 777, 99573, jnp.int32), jax.random.randint(jax.random.fold_in(jax.random.fold_in(_rk, 9), 79), (2048,), 0, 99974, jnp.int32), jax.random.randint(jax.random.fold_in(jax.random.fold_in(_rk, 9), 80), (2048,), 74, 99967, jnp.int32), jax.random.randint(jax.random.fold_in(jax.random.fold_in(_rk, 9), 81), (2048,), 68, 99891, jnp.int32), jax.random.randint(jax.random.fold_in(jax.random.fold_in(_rk, 9), 82), (2048,), 71, 99970, jnp.int32), jax.random.randint(jax.random.fold_in(jax.random.fold_in(_rk, 9), 83), (2048,), 8, 99967, jnp.int32), jax.random.randint(jax.random.fold_in(jax.random.fold_in(_rk, 9), 84), (2048,), 82, 12498, jnp.int32), jax.random.randint(jax.random.fold_in(jax.random.fold_in(_rk, 9), 85), (2048,), 133, 99950, jnp.int32), jax.random.randint(jax.random.fold_in(jax.random.fold_in(_rk, 9), 86), (2048,), 7, 99599, jnp.int32), jax.random.randint(jax.random.fold_in(jax.random.fold_in(_rk, 9), 87), (2048,), 66, 12487, jnp.int32), jax.random.randint(jax.random.fold_in(jax.random.fold_in(_rk, 9), 88), (2048,), 154, 99657, jnp.int32), jax.random.randint(jax.random.fold_in(jax.random.fold_in(_rk, 9), 89), (2048,), 156, 99999, jnp.int32), jax.random.randint(jax.random.fold_in(jax.random.fold_in(_rk, 9), 90), (2048,), 8, 99969, jnp.int32), jax.random.randint(jax.random.fold_in(jax.random.fold_in(_rk, 9), 91), (2048,), 67, 99859, jnp.int32), jax.random.randint(jax.random.fold_in(jax.random.fold_in(_rk, 9), 92), (2048,), 311, 99942, jnp.int32), jax.random.randint(jax.random.fold_in(jax.random.fold_in(_rk, 9), 93), (2048,), 6, 99898, jnp.int32), jax.random.randint(jax.random.fold_in(jax.random.fold_in(_rk, 9), 94), (2048,), 68, 99847, jnp.int32), jax.random.randint(jax.random.fold_in(jax.random.fold_in(_rk, 9), 95), (2048,), 7, 99434, jnp.int32), jax.random.randint(jax.random.fold_in(jax.random.fold_in(_rk, 9), 96), (2048,), 99, 99995, jnp.int32), jax.random.randint(jax.random.fold_in(jax.random.fold_in(_rk, 9), 97), (2048,), 64, 99853, jnp.int32), jax.random.randint(jax.random.fold_in(jax.random.fold_in(_rk, 9), 98), (2048,), 110, 99785, jnp.int32), jax.random.randint(jax.random.fold_in(jax.random.fold_in(_rk, 9), 99), (2048,), 390, 99868, jnp.int32), jax.random.randint(jax.random.fold_in(jax.random.fold_in(_rk, 9), 100), (2048,), 102, 99915, jnp.int32), jax.random.randint(jax.random.fold_in(jax.random.fold_in(_rk, 9), 101), (2048,), 60, 99998, jnp.int32), jax.random.randint(jax.random.fold_in(jax.random.fold_in(_rk, 9), 102), (2048,), 140, 99948, jnp.int32), jax.random.randint(jax.random.fold_in(jax.random.fold_in(_rk, 9), 103), (2048,), 400, 99891, jnp.int32), jax.random.randint(jax.random.fold_in(jax.random.fold_in(_rk, 9), 104), (2048,), 11, 99905, jnp.int32), jax.random.randint(jax.random.fold_in(jax.random.fold_in(_rk, 9), 105), (2048,), 14, 99978, jnp.int32), jax.random.randint(jax.random.fold_in(jax.random.fold_in(_rk, 9), 106), (2048,), 17, 99716, jnp.int32), jax.random.randint(jax.random.fold_in(jax.random.fold_in(_rk, 9), 107), (2048,), 44, 99994, jnp.int32), jax.random.randint(jax.random.fold_in(jax.random.fold_in(_rk, 9), 108), (2048,), 244, 99917, jnp.int32), jax.random.randint(jax.random.fold_in(jax.random.fold_in(_rk, 9), 109), (2048,), 263, 99996, jnp.int32), jax.random.randint(jax.random.fold_in(jax.random.fold_in(_rk, 9), 110), (2048,), 14, 99986, jnp.int32), jax.random.randint(jax.random.fold_in(jax.random.fold_in(_rk, 9), 111), (2048,), 174, 99908, jnp.int32), jax.random.randint(jax.random.fold_in(jax.random.fold_in(_rk, 9), 112), (2048,), 30, 99814, jnp.int32), jax.random.randint(jax.random.fold_in(jax.random.fold_in(_rk, 9), 113), (2048,), 4, 99938, jnp.int32), jax.random.randint(jax.random.fold_in(jax.random.fold_in(_rk, 9), 114), (2048,), 84, 99854, jnp.int32), jax.random.randint(jax.random.fold_in(jax.random.fold_in(_rk, 9), 115), (2048,), 116, 99980, jnp.int32), jax.random.randint(jax.random.fold_in(jax.random.fold_in(_rk, 9), 116), (2048,), 45, 99892, jnp.int32), jax.random.randint(jax.random.fold_in(jax.random.fold_in(_rk, 9), 117), (2048,), 1, 12499, jnp.int32), jax.random.randint(jax.random.fold_in(jax.random.fold_in(_rk, 9), 118), (2048,), 55, 99447, jnp.int32), jax.random.randint(jax.random.fold_in(jax.random.fold_in(_rk, 9), 119), (2048,), 86, 99949, jnp.int32), jax.random.randint(jax.random.fold_in(jax.random.fold_in(_rk, 9), 120), (2048,), 118, 99956, jnp.int32), jax.random.randint(jax.random.fold_in(jax.random.fold_in(_rk, 9), 121), (2048,), 37, 99978, jnp.int32), jax.random.randint(jax.random.fold_in(jax.random.fold_in(_rk, 9), 122), (2048,), 33, 99853, jnp.int32), jax.random.randint(jax.random.fold_in(jax.random.fold_in(_rk, 9), 123), (2048,), 1, 99795, jnp.int32), jax.random.randint(jax.random.fold_in(jax.random.fold_in(_rk, 9), 124), (2048,), 62, 99980, jnp.int32), jax.random.randint(jax.random.fold_in(jax.random.fold_in(_rk, 9), 125), (2048,), 26, 99985, jnp.int32), jax.random.randint(jax.random.fold_in(jax.random.fold_in(_rk, 9), 126), (2048,), 27, 99958, jnp.int32), jax.random.randint(jax.random.fold_in(jax.random.fold_in(_rk, 9), 127), (2048,), 53, 99849, jnp.int32), jax.random.randint(jax.random.fold_in(jax.random.fold_in(_rk, 9), 128), (2048,), 5, 99935, jnp.int32), jax.random.randint(jax.random.fold_in(jax.random.fold_in(_rk, 9), 129), (2048,), 36, 99895, jnp.int32), jax.random.randint(jax.random.fold_in(jax.random.fold_in(_rk, 9), 130), (2048,), 103, 99761, jnp.int32), jax.random.randint(jax.random.fold_in(jax.random.fold_in(_rk, 9), 131), (2048,), 41, 99830, jnp.int32), jax.random.randint(jax.random.fold_in(jax.random.fold_in(_rk, 9), 132), (2048,), 124, 99879, jnp.int32), jax.random.randint(jax.random.fold_in(jax.random.fold_in(_rk, 9), 133), (2048,), 24, 99962, jnp.int32), jax.random.randint(jax.random.fold_in(jax.random.fold_in(_rk, 9), 134), (2048,), 148, 99979, jnp.int32), jax.random.randint(jax.random.fold_in(jax.random.fold_in(_rk, 9), 135), (2048,), 94, 99894, jnp.int32), jax.random.randint(jax.random.fold_in(jax.random.fold_in(_rk, 9), 136), (2048,), 307, 99910, jnp.int32), jax.random.randint(jax.random.fold_in(jax.random.fold_in(_rk, 9), 137), (2048,), 61, 99995, jnp.int32), jax.random.randint(jax.random.fold_in(jax.random.fold_in(_rk, 9), 138), (2048,), 282, 99985, jnp.int32), jax.random.randint(jax.random.fold_in(jax.random.fold_in(_rk, 9), 139), (2048,), 110, 99903, jnp.int32), jax.random.randint(jax.random.fold_in(jax.random.fold_in(_rk, 9), 140), (2048,), 154, 99763, jnp.int32), jax.random.randint(jax.random.fold_in(jax.random.fold_in(_rk, 9), 141), (2048,), 18, 12473, jnp.int32), jax.random.randint(jax.random.fold_in(jax.random.fold_in(_rk, 9), 142), (2048,), 210, 99787, jnp.int32), jax.random.randint(jax.random.fold_in(jax.random.fold_in(_rk, 9), 143), (2048,), 55, 99967, jnp.int32), jax.random.randint(jax.random.fold_in(jax.random.fold_in(_rk, 9), 144), (2048,), 114, 12492, jnp.int32), jax.random.randint(jax.random.fold_in(jax.random.fold_in(_rk, 9), 145), (2048,), 54, 99993, jnp.int32), jax.random.randint(jax.random.fold_in(jax.random.fold_in(_rk, 9), 146), (2048,), 30, 99956, jnp.int32), jax.random.randint(jax.random.fold_in(jax.random.fold_in(_rk, 9), 147), (2048,), 105, 99998, jnp.int32), jax.random.randint(jax.random.fold_in(jax.random.fold_in(_rk, 9), 148), (2048,), 122, 99786, jnp.int32), jax.random.randint(jax.random.fold_in(jax.random.fold_in(_rk, 9), 149), (2048,), 10, 12475, jnp.int32), jax.random.randint(jax.random.fold_in(jax.random.fold_in(_rk, 9), 150), (2048,), 3, 99892, jnp.int32), jax.random.randint(jax.random.fold_in(jax.random.fold_in(_rk, 9), 151), (2048,), 245, 99974, jnp.int32), jax.random.randint(jax.random.fold_in(jax.random.fold_in(_rk, 9), 152), (2048,), 219, 99639, jnp.int32), jax.random.randint(jax.random.fold_in(jax.random.fold_in(_rk, 9), 153), (2048,), 67, 99846, jnp.int32), jax.random.randint(jax.random.fold_in(jax.random.fold_in(_rk, 9), 154), (2048,), 70, 99862, jnp.int32), jax.random.randint(jax.random.fold_in(jax.random.fold_in(_rk, 9), 155), (2048,), 144, 12487, jnp.int32), jax.random.randint(jax.random.fold_in(jax.random.fold_in(_rk, 9), 156), (2048,), 116, 12469, jnp.int32), jax.random.randint(jax.random.fold_in(jax.random.fold_in(_rk, 9), 157), (2048,), 26, 99861, jnp.int32), jax.random.randint(jax.random.fold_in(jax.random.fold_in(_rk, 9), 158), (2048,), 15, 99919, jnp.int32), jax.random.randint(jax.random.fold_in(jax.random.fold_in(_rk, 9), 159), (2048,), 28, 12482, jnp.int32), jax.random.randint(jax.random.fold_in(jax.random.fold_in(_rk, 9), 160), (2048,), 62, 99987, jnp.int32), jax.random.randint(jax.random.fold_in(jax.random.fold_in(_rk, 9), 161), (2048,), 103, 99881, jnp.int32), jax.random.randint(jax.random.fold_in(jax.random.fold_in(_rk, 9), 162), (2048,), 55, 99985, jnp.int32), jax.random.randint(jax.random.fold_in(jax.random.fold_in(_rk, 9), 163), (2048,), 4, 99892, jnp.int32), jax.random.randint(jax.random.fold_in(jax.random.fold_in(_rk, 9), 164), (2048,), 13, 99787, jnp.int32), jax.random.randint(jax.random.fold_in(jax.random.fold_in(_rk, 9), 165), (2048,), 6, 12464, jnp.int32), jax.random.randint(jax.random.fold_in(jax.random.fold_in(_rk, 9), 166), (2048,), 171, 12493, jnp.int32), jax.random.randint(jax.random.fold_in(jax.random.fold_in(_rk, 9), 167), (2048,), 269, 99972, jnp.int32), jax.random.randint(jax.random.fold_in(jax.random.fold_in(_rk, 9), 168), (2048,), 554, 99985, jnp.int32), jax.random.randint(jax.random.fold_in(jax.random.fold_in(_rk, 9), 169), (2048,), 22, 99972, jnp.int32), jax.random.randint(jax.random.fold_in(jax.random.fold_in(_rk, 9), 170), (2048,), 9, 99876, jnp.int32), jax.random.randint(jax.random.fold_in(jax.random.fold_in(_rk, 9), 171), (2048,), 45, 99890, jnp.int32), jax.random.randint(jax.random.fold_in(jax.random.fold_in(_rk, 9), 172), (2048,), 182, 99945, jnp.int32), jax.random.randint(jax.random.fold_in(jax.random.fold_in(_rk, 9), 173), (2048,), 110, 99819, jnp.int32), jax.random.randint(jax.random.fold_in(jax.random.fold_in(_rk, 9), 174), (2048,), 85, 99981, jnp.int32), jax.random.randint(jax.random.fold_in(jax.random.fold_in(_rk, 9), 175), (2048,), 275, 12475, jnp.int32), jax.random.randint(jax.random.fold_in(jax.random.fold_in(_rk, 9), 176), (2048,), 114, 99957, jnp.int32), jax.random.randint(jax.random.fold_in(jax.random.fold_in(_rk, 9), 177), (2048,), 61, 99954, jnp.int32), jax.random.randint(jax.random.fold_in(jax.random.fold_in(_rk, 9), 178), (2048,), 13, 99995, jnp.int32), jax.random.randint(jax.random.fold_in(jax.random.fold_in(_rk, 9), 179), (2048,), 78, 99998, jnp.int32), jax.random.randint(jax.random.fold_in(jax.random.fold_in(_rk, 9), 180), (2048,), 108, 12498, jnp.int32), jax.random.randint(jax.random.fold_in(jax.random.fold_in(_rk, 9), 181), (2048,), 26, 12496, jnp.int32), jax.random.randint(jax.random.fold_in(jax.random.fold_in(_rk, 9), 182), (2048,), 200, 99645, jnp.int32), jax.random.randint(jax.random.fold_in(jax.random.fold_in(_rk, 9), 183), (2048,), 68, 99932, jnp.int32), jax.random.randint(jax.random.fold_in(jax.random.fold_in(_rk, 9), 184), (2048,), 95, 99996, jnp.int32), jax.random.randint(jax.random.fold_in(jax.random.fold_in(_rk, 9), 185), (2048,), 30, 99997, jnp.int32), jax.random.randint(jax.random.fold_in(jax.random.fold_in(_rk, 9), 186), (2048,), 1, 12485, jnp.int32), jax.random.randint(jax.random.fold_in(jax.random.fold_in(_rk, 9), 187), (2048,), 48, 99987, jnp.int32), jax.random.randint(jax.random.fold_in(jax.random.fold_in(_rk, 9), 188), (2048,), 19, 12496, jnp.int32), jax.random.randint(jax.random.fold_in(jax.random.fold_in(_rk, 9), 189), (2048,), 16, 99953, jnp.int32), jax.random.randint(jax.random.fold_in(jax.random.fold_in(_rk, 9), 190), (2048,), 1, 99802, jnp.int32), jax.random.randint(jax.random.fold_in(jax.random.fold_in(_rk, 9), 191), (2048,), 8, 99839, jnp.int32), jax.random.randint(jax.random.fold_in(jax.random.fold_in(_rk, 9), 192), (2048,), 10, 99779, jnp.int32), jax.random.randint(jax.random.fold_in(jax.random.fold_in(_rk, 9), 193), (2048,), 95, 99996, jnp.int32), jax.random.randint(jax.random.fold_in(jax.random.fold_in(_rk, 9), 194), (2048,), 94, 12493, jnp.int32), jax.random.randint(jax.random.fold_in(jax.random.fold_in(_rk, 9), 195), (2048,), 161, 99902, jnp.int32), jax.random.randint(jax.random.fold_in(jax.random.fold_in(_rk, 9), 196), (2048,), 70, 99873, jnp.int32), jax.random.randint(jax.random.fold_in(jax.random.fold_in(_rk, 9), 197), (2048,), 264, 99991, jnp.int32), jax.random.randint(jax.random.fold_in(jax.random.fold_in(_rk, 9), 198), (2048,), 232, 99947, jnp.int32), jax.random.randint(jax.random.fold_in(jax.random.fold_in(_rk, 9), 199), (2048,), 169, 99692, jnp.int32)], axis=1)
        r_ipv_item_cat = jnp.stack([jax.random.randint(jax.random.fold_in(jax.random.fold_in(_rk, 10), 0), (2048,), 0, 1000, jnp.int32), jax.random.randint(jax.random.fold_in(jax.random.fold_in(_rk, 10), 1), (2048,), 0, 1000, jnp.int32), jax.random.randint(jax.random.fold_in(jax.random.fold_in(_rk, 10), 2), (2048,), 1, 1000, jnp.int32), jax.random.randint(jax.random.fold_in(jax.random.fold_in(_rk, 10), 3), (2048,), 1, 997, jnp.int32), jax.random.randint(jax.random.fold_in(jax.random.fold_in(_rk, 10), 4), (2048,), 2, 999, jnp.int32), jax.random.randint(jax.random.fold_in(jax.random.fold_in(_rk, 10), 5), (2048,), 0, 1000, jnp.int32), jax.random.randint(jax.random.fold_in(jax.random.fold_in(_rk, 10), 6), (2048,), 2, 1000, jnp.int32), jax.random.randint(jax.random.fold_in(jax.random.fold_in(_rk, 10), 7), (2048,), 1, 1000, jnp.int32), jax.random.randint(jax.random.fold_in(jax.random.fold_in(_rk, 10), 8), (2048,), 0, 1000, jnp.int32), jax.random.randint(jax.random.fold_in(jax.random.fold_in(_rk, 10), 9), (2048,), 2, 999, jnp.int32), jax.random.randint(jax.random.fold_in(jax.random.fold_in(_rk, 10), 10), (2048,), 1, 994, jnp.int32), jax.random.randint(jax.random.fold_in(jax.random.fold_in(_rk, 10), 11), (2048,), 5, 1000, jnp.int32), jax.random.randint(jax.random.fold_in(jax.random.fold_in(_rk, 10), 12), (2048,), 2, 1000, jnp.int32), jax.random.randint(jax.random.fold_in(jax.random.fold_in(_rk, 10), 13), (2048,), 0, 1000, jnp.int32), jax.random.randint(jax.random.fold_in(jax.random.fold_in(_rk, 10), 14), (2048,), 0, 1000, jnp.int32), jax.random.randint(jax.random.fold_in(jax.random.fold_in(_rk, 10), 15), (2048,), 1, 998, jnp.int32), jax.random.randint(jax.random.fold_in(jax.random.fold_in(_rk, 10), 16), (2048,), 1, 997, jnp.int32), jax.random.randint(jax.random.fold_in(jax.random.fold_in(_rk, 10), 17), (2048,), 0, 999, jnp.int32), jax.random.randint(jax.random.fold_in(jax.random.fold_in(_rk, 10), 18), (2048,), 2, 1000, jnp.int32), jax.random.randint(jax.random.fold_in(jax.random.fold_in(_rk, 10), 19), (2048,), 1, 1000, jnp.int32), jax.random.randint(jax.random.fold_in(jax.random.fold_in(_rk, 10), 20), (2048,), 0, 1000, jnp.int32), jax.random.randint(jax.random.fold_in(jax.random.fold_in(_rk, 10), 21), (2048,), 1, 999, jnp.int32), jax.random.randint(jax.random.fold_in(jax.random.fold_in(_rk, 10), 22), (2048,), 0, 1000, jnp.int32), jax.random.randint(jax.random.fold_in(jax.random.fold_in(_rk, 10), 23), (2048,), 0, 999, jnp.int32), jax.random.randint(jax.random.fold_in(jax.random.fold_in(_rk, 10), 24), (2048,), 0, 1000, jnp.int32), jax.random.randint(jax.random.fold_in(jax.random.fold_in(_rk, 10), 25), (2048,), 0, 1000, jnp.int32), jax.random.randint(jax.random.fold_in(jax.random.fold_in(_rk, 10), 26), (2048,), 1, 999, jnp.int32), jax.random.randint(jax.random.fold_in(jax.random.fold_in(_rk, 10), 27), (2048,), 1, 999, jnp.int32), jax.random.randint(jax.random.fold_in(jax.random.fold_in(_rk, 10), 28), (2048,), 0, 1000, jnp.int32), jax.random.randint(jax.random.fold_in(jax.random.fold_in(_rk, 10), 29), (2048,), 5, 999, jnp.int32), jax.random.randint(jax.random.fold_in(jax.random.fold_in(_rk, 10), 30), (2048,), 1, 999, jnp.int32), jax.random.randint(jax.random.fold_in(jax.random.fold_in(_rk, 10), 31), (2048,), 0, 999, jnp.int32), jax.random.randint(jax.random.fold_in(jax.random.fold_in(_rk, 10), 32), (2048,), 3, 1000, jnp.int32), jax.random.randint(jax.random.fold_in(jax.random.fold_in(_rk, 10), 33), (2048,), 1, 1000, jnp.int32), jax.random.randint(jax.random.fold_in(jax.random.fold_in(_rk, 10), 34), (2048,), 0, 1000, jnp.int32), jax.random.randint(jax.random.fold_in(jax.random.fold_in(_rk, 10), 35), (2048,), 0, 1000, jnp.int32), jax.random.randint(jax.random.fold_in(jax.random.fold_in(_rk, 10), 36), (2048,), 0, 1000, jnp.int32), jax.random.randint(jax.random.fold_in(jax.random.fold_in(_rk, 10), 37), (2048,), 0, 999, jnp.int32), jax.random.randint(jax.random.fold_in(jax.random.fold_in(_rk, 10), 38), (2048,), 1, 999, jnp.int32), jax.random.randint(jax.random.fold_in(jax.random.fold_in(_rk, 10), 39), (2048,), 0, 1000, jnp.int32), jax.random.randint(jax.random.fold_in(jax.random.fold_in(_rk, 10), 40), (2048,), 0, 1000, jnp.int32), jax.random.randint(jax.random.fold_in(jax.random.fold_in(_rk, 10), 41), (2048,), 0, 1000, jnp.int32), jax.random.randint(jax.random.fold_in(jax.random.fold_in(_rk, 10), 42), (2048,), 0, 1000, jnp.int32), jax.random.randint(jax.random.fold_in(jax.random.fold_in(_rk, 10), 43), (2048,), 0, 1000, jnp.int32), jax.random.randint(jax.random.fold_in(jax.random.fold_in(_rk, 10), 44), (2048,), 1, 999, jnp.int32), jax.random.randint(jax.random.fold_in(jax.random.fold_in(_rk, 10), 45), (2048,), 0, 997, jnp.int32), jax.random.randint(jax.random.fold_in(jax.random.fold_in(_rk, 10), 46), (2048,), 1, 1000, jnp.int32), jax.random.randint(jax.random.fold_in(jax.random.fold_in(_rk, 10), 47), (2048,), 0, 999, jnp.int32), jax.random.randint(jax.random.fold_in(jax.random.fold_in(_rk, 10), 48), (2048,), 0, 1000, jnp.int32), jax.random.randint(jax.random.fold_in(jax.random.fold_in(_rk, 10), 49), (2048,), 1, 1000, jnp.int32), jax.random.randint(jax.random.fold_in(jax.random.fold_in(_rk, 10), 50), (2048,), 2, 999, jnp.int32), jax.random.randint(jax.random.fold_in(jax.random.fold_in(_rk, 10), 51), (2048,), 1, 1000, jnp.int32), jax.random.randint(jax.random.fold_in(jax.random.fold_in(_rk, 10), 52), (2048,), 0, 999, jnp.int32), jax.random.randint(jax.random.fold_in(jax.random.fold_in(_rk, 10), 53), (2048,), 0, 1000, jnp.int32), jax.random.randint(jax.random.fold_in(jax.random.fold_in(_rk, 10), 54), (2048,), 0, 999, jnp.int32), jax.random.randint(jax.random.fold_in(jax.random.fold_in(_rk, 10), 55), (2048,), 0, 1000, jnp.int32), jax.random.randint(jax.random.fold_in(jax.random.fold_in(_rk, 10), 56), (2048,), 0, 1000, jnp.int32), jax.random.randint(jax.random.fold_in(jax.random.fold_in(_rk, 10), 57), (2048,), 0, 999, jnp.int32), jax.random.randint(jax.random.fold_in(jax.random.fold_in(_rk, 10), 58), (2048,), 2, 1000, jnp.int32), jax.random.randint(jax.random.fold_in(jax.random.fold_in(_rk, 10), 59), (2048,), 1, 999, jnp.int32), jax.random.randint(jax.random.fold_in(jax.random.fold_in(_rk, 10), 60), (2048,), 0, 999, jnp.int32), jax.random.randint(jax.random.fold_in(jax.random.fold_in(_rk, 10), 61), (2048,), 0, 999, jnp.int32), jax.random.randint(jax.random.fold_in(jax.random.fold_in(_rk, 10), 62), (2048,), 0, 998, jnp.int32), jax.random.randint(jax.random.fold_in(jax.random.fold_in(_rk, 10), 63), (2048,), 0, 1000, jnp.int32), jax.random.randint(jax.random.fold_in(jax.random.fold_in(_rk, 10), 64), (2048,), 0, 1000, jnp.int32), jax.random.randint(jax.random.fold_in(jax.random.fold_in(_rk, 10), 65), (2048,), 0, 998, jnp.int32), jax.random.randint(jax.random.fold_in(jax.random.fold_in(_rk, 10), 66), (2048,), 1, 1000, jnp.int32), jax.random.randint(jax.random.fold_in(jax.random.fold_in(_rk, 10), 67), (2048,), 2, 1000, jnp.int32), jax.random.randint(jax.random.fold_in(jax.random.fold_in(_rk, 10), 68), (2048,), 1, 1000, jnp.int32), jax.random.randint(jax.random.fold_in(jax.random.fold_in(_rk, 10), 69), (2048,), 2, 997, jnp.int32), jax.random.randint(jax.random.fold_in(jax.random.fold_in(_rk, 10), 70), (2048,), 0, 1000, jnp.int32), jax.random.randint(jax.random.fold_in(jax.random.fold_in(_rk, 10), 71), (2048,), 1, 998, jnp.int32), jax.random.randint(jax.random.fold_in(jax.random.fold_in(_rk, 10), 72), (2048,), 0, 1000, jnp.int32), jax.random.randint(jax.random.fold_in(jax.random.fold_in(_rk, 10), 73), (2048,), 1, 1000, jnp.int32), jax.random.randint(jax.random.fold_in(jax.random.fold_in(_rk, 10), 74), (2048,), 0, 998, jnp.int32), jax.random.randint(jax.random.fold_in(jax.random.fold_in(_rk, 10), 75), (2048,), 3, 1000, jnp.int32), jax.random.randint(jax.random.fold_in(jax.random.fold_in(_rk, 10), 76), (2048,), 1, 999, jnp.int32), jax.random.randint(jax.random.fold_in(jax.random.fold_in(_rk, 10), 77), (2048,), 0, 1000, jnp.int32), jax.random.randint(jax.random.fold_in(jax.random.fold_in(_rk, 10), 78), (2048,), 0, 1000, jnp.int32), jax.random.randint(jax.random.fold_in(jax.random.fold_in(_rk, 10), 79), (2048,), 0, 1000, jnp.int32), jax.random.randint(jax.random.fold_in(jax.random.fold_in(_rk, 10), 80), (2048,), 0, 999, jnp.int32), jax.random.randint(jax.random.fold_in(jax.random.fold_in(_rk, 10), 81), (2048,), 0, 999, jnp.int32), jax.random.randint(jax.random.fold_in(jax.random.fold_in(_rk, 10), 82), (2048,), 0, 1000, jnp.int32), jax.random.randint(jax.random.fold_in(jax.random.fold_in(_rk, 10), 83), (2048,), 0, 1000, jnp.int32), jax.random.randint(jax.random.fold_in(jax.random.fold_in(_rk, 10), 84), (2048,), 0, 1000, jnp.int32), jax.random.randint(jax.random.fold_in(jax.random.fold_in(_rk, 10), 85), (2048,), 1, 1000, jnp.int32), jax.random.randint(jax.random.fold_in(jax.random.fold_in(_rk, 10), 86), (2048,), 0, 999, jnp.int32), jax.random.randint(jax.random.fold_in(jax.random.fold_in(_rk, 10), 87), (2048,), 0, 998, jnp.int32), jax.random.randint(jax.random.fold_in(jax.random.fold_in(_rk, 10), 88), (2048,), 0, 1000, jnp.int32), jax.random.randint(jax.random.fold_in(jax.random.fold_in(_rk, 10), 89), (2048,), 0, 997, jnp.int32), jax.random.randint(jax.random.fold_in(jax.random.fold_in(_rk, 10), 90), (2048,), 0, 1000, jnp.int32), jax.random.randint(jax.random.fold_in(jax.random.fold_in(_rk, 10), 91), (2048,), 0, 1000, jnp.int32), jax.random.randint(jax.random.fold_in(jax.random.fold_in(_rk, 10), 92), (2048,), 0, 1000, jnp.int32), jax.random.randint(jax.random.fold_in(jax.random.fold_in(_rk, 10), 93), (2048,), 0, 1000, jnp.int32), jax.random.randint(jax.random.fold_in(jax.random.fold_in(_rk, 10), 94), (2048,), 0, 1000, jnp.int32), jax.random.randint(jax.random.fold_in(jax.random.fold_in(_rk, 10), 95), (2048,), 1, 1000, jnp.int32), jax.random.randint(jax.random.fold_in(jax.random.fold_in(_rk, 10), 96), (2048,), 0, 1000, jnp.int32), jax.random.randint(jax.random.fold_in(jax.random.fold_in(_rk, 10), 97), (2048,), 0, 1000, jnp.int32), jax.random.randint(jax.random.fold_in(jax.random.fold_in(_rk, 10), 98), (2048,), 0, 1000, jnp.int32), jax.random.randint(jax.random.fold_in(jax.random.fold_in(_rk, 10), 99), (2048,), 2, 999, jnp.int32), jax.random.randint(jax.random.fold_in(jax.random.fold_in(_rk, 10), 100), (2048,), 2, 1000, jnp.int32), jax.random.randint(jax.random.fold_in(jax.random.fold_in(_rk, 10), 101), (2048,), 1, 1000, jnp.int32), jax.random.randint(jax.random.fold_in(jax.random.fold_in(_rk, 10), 102), (2048,), 1, 1000, jnp.int32), jax.random.randint(jax.random.fold_in(jax.random.fold_in(_rk, 10), 103), (2048,), 1, 997, jnp.int32), jax.random.randint(jax.random.fold_in(jax.random.fold_in(_rk, 10), 104), (2048,), 0, 1000, jnp.int32), jax.random.randint(jax.random.fold_in(jax.random.fold_in(_rk, 10), 105), (2048,), 0, 999, jnp.int32), jax.random.randint(jax.random.fold_in(jax.random.fold_in(_rk, 10), 106), (2048,), 2, 1000, jnp.int32), jax.random.randint(jax.random.fold_in(jax.random.fold_in(_rk, 10), 107), (2048,), 1, 1000, jnp.int32), jax.random.randint(jax.random.fold_in(jax.random.fold_in(_rk, 10), 108), (2048,), 0, 1000, jnp.int32), jax.random.randint(jax.random.fold_in(jax.random.fold_in(_rk, 10), 109), (2048,), 0, 999, jnp.int32), jax.random.randint(jax.random.fold_in(jax.random.fold_in(_rk, 10), 110), (2048,), 0, 998, jnp.int32), jax.random.randint(jax.random.fold_in(jax.random.fold_in(_rk, 10), 111), (2048,), 2, 999, jnp.int32), jax.random.randint(jax.random.fold_in(jax.random.fold_in(_rk, 10), 112), (2048,), 1, 999, jnp.int32), jax.random.randint(jax.random.fold_in(jax.random.fold_in(_rk, 10), 113), (2048,), 0, 999, jnp.int32), jax.random.randint(jax.random.fold_in(jax.random.fold_in(_rk, 10), 114), (2048,), 0, 1000, jnp.int32), jax.random.randint(jax.random.fold_in(jax.random.fold_in(_rk, 10), 115), (2048,), 0, 999, jnp.int32), jax.random.randint(jax.random.fold_in(jax.random.fold_in(_rk, 10), 116), (2048,), 0, 1000, jnp.int32), jax.random.randint(jax.random.fold_in(jax.random.fold_in(_rk, 10), 117), (2048,), 0, 999, jnp.int32), jax.random.randint(jax.random.fold_in(jax.random.fold_in(_rk, 10), 118), (2048,), 0, 999, jnp.int32), jax.random.randint(jax.random.fold_in(jax.random.fold_in(_rk, 10), 119), (2048,), 0, 1000, jnp.int32), jax.random.randint(jax.random.fold_in(jax.random.fold_in(_rk, 10), 120), (2048,), 0, 1000, jnp.int32), jax.random.randint(jax.random.fold_in(jax.random.fold_in(_rk, 10), 121), (2048,), 4, 1000, jnp.int32), jax.random.randint(jax.random.fold_in(jax.random.fold_in(_rk, 10), 122), (2048,), 0, 1000, jnp.int32), jax.random.randint(jax.random.fold_in(jax.random.fold_in(_rk, 10), 123), (2048,), 0, 998, jnp.int32), jax.random.randint(jax.random.fold_in(jax.random.fold_in(_rk, 10), 124), (2048,), 0, 1000, jnp.int32), jax.random.randint(jax.random.fold_in(jax.random.fold_in(_rk, 10), 125), (2048,), 0, 1000, jnp.int32), jax.random.randint(jax.random.fold_in(jax.random.fold_in(_rk, 10), 126), (2048,), 1, 999, jnp.int32), jax.random.randint(jax.random.fold_in(jax.random.fold_in(_rk, 10), 127), (2048,), 0, 1000, jnp.int32), jax.random.randint(jax.random.fold_in(jax.random.fold_in(_rk, 10), 128), (2048,), 0, 1000, jnp.int32), jax.random.randint(jax.random.fold_in(jax.random.fold_in(_rk, 10), 129), (2048,), 0, 1000, jnp.int32), jax.random.randint(jax.random.fold_in(jax.random.fold_in(_rk, 10), 130), (2048,), 0, 998, jnp.int32), jax.random.randint(jax.random.fold_in(jax.random.fold_in(_rk, 10), 131), (2048,), 0, 1000, jnp.int32), jax.random.randint(jax.random.fold_in(jax.random.fold_in(_rk, 10), 132), (2048,), 0, 999, jnp.int32), jax.random.randint(jax.random.fold_in(jax.random.fold_in(_rk, 10), 133), (2048,), 1, 1000, jnp.int32), jax.random.randint(jax.random.fold_in(jax.random.fold_in(_rk, 10), 134), (2048,), 1, 1000, jnp.int32), jax.random.randint(jax.random.fold_in(jax.random.fold_in(_rk, 10), 135), (2048,), 0, 998, jnp.int32), jax.random.randint(jax.random.fold_in(jax.random.fold_in(_rk, 10), 136), (2048,), 0, 1000, jnp.int32), jax.random.randint(jax.random.fold_in(jax.random.fold_in(_rk, 10), 137), (2048,), 0, 1000, jnp.int32), jax.random.randint(jax.random.fold_in(jax.random.fold_in(_rk, 10), 138), (2048,), 0, 998, jnp.int32), jax.random.randint(jax.random.fold_in(jax.random.fold_in(_rk, 10), 139), (2048,), 1, 999, jnp.int32), jax.random.randint(jax.random.fold_in(jax.random.fold_in(_rk, 10), 140), (2048,), 1, 1000, jnp.int32), jax.random.randint(jax.random.fold_in(jax.random.fold_in(_rk, 10), 141), (2048,), 0, 999, jnp.int32), jax.random.randint(jax.random.fold_in(jax.random.fold_in(_rk, 10), 142), (2048,), 0, 1000, jnp.int32), jax.random.randint(jax.random.fold_in(jax.random.fold_in(_rk, 10), 143), (2048,), 0, 1000, jnp.int32), jax.random.randint(jax.random.fold_in(jax.random.fold_in(_rk, 10), 144), (2048,), 0, 999, jnp.int32), jax.random.randint(jax.random.fold_in(jax.random.fold_in(_rk, 10), 145), (2048,), 3, 1000, jnp.int32), jax.random.randint(jax.random.fold_in(jax.random.fold_in(_rk, 10), 146), (2048,), 1, 1000, jnp.int32), jax.random.randint(jax.random.fold_in(jax.random.fold_in(_rk, 10), 147), (2048,), 3, 1000, jnp.int32), jax.random.randint(jax.random.fold_in(jax.random.fold_in(_rk, 10), 148), (2048,), 0, 1000, jnp.int32), jax.random.randint(jax.random.fold_in(jax.random.fold_in(_rk, 10), 149), (2048,), 0, 1000, jnp.int32), jax.random.randint(jax.random.fold_in(jax.random.fold_in(_rk, 10), 150), (2048,), 0, 999, jnp.int32), jax.random.randint(jax.random.fold_in(jax.random.fold_in(_rk, 10), 151), (2048,), 2, 1000, jnp.int32), jax.random.randint(jax.random.fold_in(jax.random.fold_in(_rk, 10), 152), (2048,), 0, 1000, jnp.int32), jax.random.randint(jax.random.fold_in(jax.random.fold_in(_rk, 10), 153), (2048,), 1, 1000, jnp.int32), jax.random.randint(jax.random.fold_in(jax.random.fold_in(_rk, 10), 154), (2048,), 1, 1000, jnp.int32), jax.random.randint(jax.random.fold_in(jax.random.fold_in(_rk, 10), 155), (2048,), 0, 1000, jnp.int32), jax.random.randint(jax.random.fold_in(jax.random.fold_in(_rk, 10), 156), (2048,), 1, 1000, jnp.int32), jax.random.randint(jax.random.fold_in(jax.random.fold_in(_rk, 10), 157), (2048,), 0, 999, jnp.int32), jax.random.randint(jax.random.fold_in(jax.random.fold_in(_rk, 10), 158), (2048,), 3, 1000, jnp.int32), jax.random.randint(jax.random.fold_in(jax.random.fold_in(_rk, 10), 159), (2048,), 0, 1000, jnp.int32), jax.random.randint(jax.random.fold_in(jax.random.fold_in(_rk, 10), 160), (2048,), 0, 1000, jnp.int32), jax.random.randint(jax.random.fold_in(jax.random.fold_in(_rk, 10), 161), (2048,), 1, 1000, jnp.int32), jax.random.randint(jax.random.fold_in(jax.random.fold_in(_rk, 10), 162), (2048,), 1, 1000, jnp.int32), jax.random.randint(jax.random.fold_in(jax.random.fold_in(_rk, 10), 163), (2048,), 0, 1000, jnp.int32), jax.random.randint(jax.random.fold_in(jax.random.fold_in(_rk, 10), 164), (2048,), 1, 999, jnp.int32), jax.random.randint(jax.random.fold_in(jax.random.fold_in(_rk, 10), 165), (2048,), 2, 1000, jnp.int32), jax.random.randint(jax.random.fold_in(jax.random.fold_in(_rk, 10), 166), (2048,), 0, 999, jnp.int32), jax.random.randint(jax.random.fold_in(jax.random.fold_in(_rk, 10), 167), (2048,), 2, 1000, jnp.int32), jax.random.randint(jax.random.fold_in(jax.random.fold_in(_rk, 10), 168), (2048,), 1, 998, jnp.int32), jax.random.randint(jax.random.fold_in(jax.random.fold_in(_rk, 10), 169), (2048,), 0, 1000, jnp.int32), jax.random.randint(jax.random.fold_in(jax.random.fold_in(_rk, 10), 170), (2048,), 0, 1000, jnp.int32), jax.random.randint(jax.random.fold_in(jax.random.fold_in(_rk, 10), 171), (2048,), 0, 997, jnp.int32), jax.random.randint(jax.random.fold_in(jax.random.fold_in(_rk, 10), 172), (2048,), 0, 1000, jnp.int32), jax.random.randint(jax.random.fold_in(jax.random.fold_in(_rk, 10), 173), (2048,), 0, 999, jnp.int32), jax.random.randint(jax.random.fold_in(jax.random.fold_in(_rk, 10), 174), (2048,), 0, 1000, jnp.int32), jax.random.randint(jax.random.fold_in(jax.random.fold_in(_rk, 10), 175), (2048,), 0, 999, jnp.int32), jax.random.randint(jax.random.fold_in(jax.random.fold_in(_rk, 10), 176), (2048,), 1, 1000, jnp.int32), jax.random.randint(jax.random.fold_in(jax.random.fold_in(_rk, 10), 177), (2048,), 0, 1000, jnp.int32), jax.random.randint(jax.random.fold_in(jax.random.fold_in(_rk, 10), 178), (2048,), 1, 1000, jnp.int32), jax.random.randint(jax.random.fold_in(jax.random.fold_in(_rk, 10), 179), (2048,), 1, 1000, jnp.int32), jax.random.randint(jax.random.fold_in(jax.random.fold_in(_rk, 10), 180), (2048,), 1, 1000, jnp.int32), jax.random.randint(jax.random.fold_in(jax.random.fold_in(_rk, 10), 181), (2048,), 1, 1000, jnp.int32), jax.random.randint(jax.random.fold_in(jax.random.fold_in(_rk, 10), 182), (2048,), 0, 1000, jnp.int32), jax.random.randint(jax.random.fold_in(jax.random.fold_in(_rk, 10), 183), (2048,), 1, 1000, jnp.int32), jax.random.randint(jax.random.fold_in(jax.random.fold_in(_rk, 10), 184), (2048,), 0, 1000, jnp.int32), jax.random.randint(jax.random.fold_in(jax.random.fold_in(_rk, 10), 185), (2048,), 0, 1000, jnp.int32), jax.random.randint(jax.random.fold_in(jax.random.fold_in(_rk, 10), 186), (2048,), 2, 1000, jnp.int32), jax.random.randint(jax.random.fold_in(jax.random.fold_in(_rk, 10), 187), (2048,), 2, 1000, jnp.int32), jax.random.randint(jax.random.fold_in(jax.random.fold_in(_rk, 10), 188), (2048,), 0, 1000, jnp.int32), jax.random.randint(jax.random.fold_in(jax.random.fold_in(_rk, 10), 189), (2048,), 0, 1000, jnp.int32), jax.random.randint(jax.random.fold_in(jax.random.fold_in(_rk, 10), 190), (2048,), 0, 1000, jnp.int32), jax.random.randint(jax.random.fold_in(jax.random.fold_in(_rk, 10), 191), (2048,), 0, 1000, jnp.int32), jax.random.randint(jax.random.fold_in(jax.random.fold_in(_rk, 10), 192), (2048,), 0, 996, jnp.int32), jax.random.randint(jax.random.fold_in(jax.random.fold_in(_rk, 10), 193), (2048,), 0, 1000, jnp.int32), jax.random.randint(jax.random.fold_in(jax.random.fold_in(_rk, 10), 194), (2048,), 1, 1000, jnp.int32), jax.random.randint(jax.random.fold_in(jax.random.fold_in(_rk, 10), 195), (2048,), 0, 1000, jnp.int32), jax.random.randint(jax.random.fold_in(jax.random.fold_in(_rk, 10), 196), (2048,), 1, 1000, jnp.int32), jax.random.randint(jax.random.fold_in(jax.random.fold_in(_rk, 10), 197), (2048,), 0, 999, jnp.int32), jax.random.randint(jax.random.fold_in(jax.random.fold_in(_rk, 10), 198), (2048,), 1, 999, jnp.int32), jax.random.randint(jax.random.fold_in(jax.random.fold_in(_rk, 10), 199), (2048,), 0, 998, jnp.int32)], axis=1)
        return (r_num_feat1, r_num_feat2, r_score, r_user_id, r_cand_item_id, r_cand_item_cat, r_exp_item_id, r_exp_item_cat, r_ipv_item_id, r_ipv_item_cat)
    r_num_feat1, r_num_feat2, r_score, r_user_id, r_cand_item_id, r_cand_item_cat, r_exp_item_id, r_exp_item_cat, r_ipv_item_id, r_ipv_item_cat = _rec_inputs()

    def _L0_rec_setup():
        import jax, jax.numpy as jnp
        import numpy as np
        B, L = (1024, 200)
        N_ITEM, N_CAT, N_USER = (12500, 1000, 12500)
        D_ID, D_CAT, D_USER = (64, 32, 32)
        D_ITEM = D_ID + D_CAT
        CAT_SIZE = 2 + D_USER + 3 * D_ITEM
        H1, H2 = (200, 80)
        BN_EPS = 1e-05

        def _attention_pool(seq, tgt, w1, b1, w2, b2):
            t = jnp.broadcast_to(tgt[:, None, :], seq.shape)
            cat = jnp.concatenate([seq, t, seq - t, seq * t], axis=-1)
            h = jax.nn.relu(cat @ w1 + b1)
            logits = h @ w2 + b2
            w = jax.nn.softmax(logits, axis=1)
            return jnp.sum(w * seq, axis=1)

        def _bn_eval(x, g, b, m, v):
            return (x - m) * jax.lax.rsqrt(v + BN_EPS) * g + b
        key = jax.random.key(seed)
        ks = jax.random.split(key, 32)
        inp = {}
        inp['num_feat1'] = jax.random.normal(ks[0], (B,), jnp.float32)
        inp['num_feat2'] = jax.random.normal(ks[1], (B,), jnp.float32)
        inp['score'] = jax.random.uniform(ks[2], (B,), jnp.float32, 0.05, 0.95)
        inp['user_id'] = jax.random.randint(ks[3], (B,), 0, N_USER)
        inp['cand_item_id'] = jax.random.randint(ks[4], (B,), 0, N_ITEM)
        inp['cand_item_cat'] = jax.random.randint(ks[5], (B,), 0, N_CAT)
        inp['exp_item_id'] = jax.random.randint(ks[6], (B, L), 0, N_ITEM)
        inp['exp_item_cat'] = jax.random.randint(ks[7], (B, L), 0, N_CAT)
        inp['ipv_item_id'] = jax.random.randint(ks[8], (B, L), 0, N_ITEM)
        inp['ipv_item_cat'] = jax.random.randint(ks[9], (B, L), 0, N_CAT)
        s = 0.02
        inp['emb_item_id'] = jax.random.normal(ks[10], (N_ITEM, D_ID), jnp.float32) * s
        inp['emb_item_cat'] = jax.random.normal(ks[11], (N_CAT, D_CAT), jnp.float32) * s
        inp['emb_user'] = jax.random.normal(ks[12], (N_USER, D_USER), jnp.float32) * s
        inp['att_w1'] = jax.random.normal(ks[13], (4 * D_ITEM, D_ITEM), jnp.float32) * s
        inp['att_b1'] = jnp.zeros((D_ITEM,), jnp.float32)
        inp['att_w2'] = jax.random.normal(ks[14], (D_ITEM, 1), jnp.float32) * s
        inp['att_b2'] = jnp.zeros((1,), jnp.float32)
        inp['fc1_w'] = jax.random.normal(ks[15], (CAT_SIZE, H1), jnp.float32) * s
        inp['fc1_b'] = jnp.zeros((H1,), jnp.float32)
        inp['bn1_g'] = jnp.ones((H1,), jnp.float32)
        inp['bn1_b'] = jnp.zeros((H1,), jnp.float32)
        inp['bn1_m'] = jax.random.normal(ks[16], (H1,), jnp.float32) * 0.1
        inp['bn1_v'] = jax.random.uniform(ks[17], (H1,), jnp.float32, 0.5, 1.5)
        inp['fc2_w'] = jax.random.normal(ks[18], (H1, H2), jnp.float32) * s
        inp['fc2_b'] = jnp.zeros((H2,), jnp.float32)
        inp['bn2_g'] = jnp.ones((H2,), jnp.float32)
        inp['bn2_b'] = jnp.zeros((H2,), jnp.float32)
        inp['bn2_m'] = jax.random.normal(ks[19], (H2,), jnp.float32) * 0.1
        inp['bn2_v'] = jax.random.uniform(ks[20], (H2,), jnp.float32, 0.5, 1.5)
        inp['fc3_w'] = jax.random.normal(ks[21], (H2, 1), jnp.float32) * s
        inp['fc3_b'] = jnp.zeros((1,), jnp.float32)
        return inp
    _L0_rec_all = _L0_rec_setup()
    _L0_rec_in = {k: v for k, v in _L0_rec_all.items() if k in ('emb_item_id', 'emb_item_cat', 'emb_user', 'att_w1', 'att_b1', 'att_w2', 'att_b2', 'fc1_w', 'fc1_b', 'bn1_g', 'bn1_b', 'bn1_m', 'bn1_v', 'fc2_w', 'fc2_b', 'bn2_g', 'bn2_b', 'bn2_m', 'bn2_v', 'fc3_w', 'fc3_b')}
    del _L0_rec_all
    return {'r_num_feat1': r_num_feat1, 'r_num_feat2': r_num_feat2, 'r_score': r_score, 'r_user_id': r_user_id, 'r_cand_item_id': r_cand_item_id, 'r_cand_item_cat': r_cand_item_cat, 'r_exp_item_id': r_exp_item_id, 'r_exp_item_cat': r_exp_item_cat, 'r_ipv_item_id': r_ipv_item_id, 'r_ipv_item_cat': r_ipv_item_cat, 'L0_rec_emb_item_id': _L0_rec_in['emb_item_id'], 'L0_rec_emb_item_cat': _L0_rec_in['emb_item_cat'], 'L0_rec_emb_user': _L0_rec_in['emb_user'], 'L0_rec_att_w1': _L0_rec_in['att_w1'], 'L0_rec_att_b1': _L0_rec_in['att_b1'], 'L0_rec_att_w2': _L0_rec_in['att_w2'], 'L0_rec_att_b2': _L0_rec_in['att_b2'], 'L0_rec_fc1_w': _L0_rec_in['fc1_w'], 'L0_rec_fc1_b': _L0_rec_in['fc1_b'], 'L0_rec_bn1_g': _L0_rec_in['bn1_g'], 'L0_rec_bn1_b': _L0_rec_in['bn1_b'], 'L0_rec_bn1_m': _L0_rec_in['bn1_m'], 'L0_rec_bn1_v': _L0_rec_in['bn1_v'], 'L0_rec_fc2_w': _L0_rec_in['fc2_w'], 'L0_rec_fc2_b': _L0_rec_in['fc2_b'], 'L0_rec_bn2_g': _L0_rec_in['bn2_g'], 'L0_rec_bn2_b': _L0_rec_in['bn2_b'], 'L0_rec_bn2_m': _L0_rec_in['bn2_m'], 'L0_rec_bn2_v': _L0_rec_in['bn2_v'], 'L0_rec_fc3_w': _L0_rec_in['fc3_w'], 'L0_rec_fc3_b': _L0_rec_in['fc3_b']}

def reference(r_num_feat1, r_num_feat2, r_score, r_user_id, r_cand_item_id, r_cand_item_cat, r_exp_item_id, r_exp_item_cat, r_ipv_item_id, r_ipv_item_cat, L0_rec_emb_item_id, L0_rec_emb_item_cat, L0_rec_emb_user, L0_rec_att_w1, L0_rec_att_b1, L0_rec_att_w2, L0_rec_att_b2, L0_rec_fc1_w, L0_rec_fc1_b, L0_rec_bn1_g, L0_rec_bn1_b, L0_rec_bn1_m, L0_rec_bn1_v, L0_rec_fc2_w, L0_rec_fc2_b, L0_rec_bn2_g, L0_rec_bn2_b, L0_rec_bn2_m, L0_rec_bn2_v, L0_rec_fc3_w, L0_rec_fc3_b):
    import jax
    import jax.numpy as jnp

    def _L0_rec_ref(num_feat1, num_feat2, score, emb_item_id, emb_item_cat, emb_user, att_w1, att_b1, att_w2, att_b2, fc1_w, fc1_b, bn1_g, bn1_b, bn1_m, bn1_v, fc2_w, fc2_b, bn2_g, bn2_b, bn2_m, bn2_v, fc3_w, fc3_b, user_id, cand_item_id, cand_item_cat, exp_item_id, exp_item_cat, ipv_item_id, ipv_item_cat):
        import jax, jax.numpy as jnp
        import numpy as np
        B, L = (1024, 200)
        N_ITEM, N_CAT, N_USER = (12500, 1000, 12500)
        D_ID, D_CAT, D_USER = (64, 32, 32)
        D_ITEM = D_ID + D_CAT
        CAT_SIZE = 2 + D_USER + 3 * D_ITEM
        H1, H2 = (200, 80)
        BN_EPS = 1e-05

        def _attention_pool(seq, tgt, w1, b1, w2, b2):
            t = jnp.broadcast_to(tgt[:, None, :], seq.shape)
            cat = jnp.concatenate([seq, t, seq - t, seq * t], axis=-1)
            h = jax.nn.relu(cat @ w1 + b1)
            logits = h @ w2 + b2
            w = jax.nn.softmax(logits, axis=1)
            return jnp.sum(w * seq, axis=1)

        def _bn_eval(x, g, b, m, v):
            return (x - m) * jax.lax.rsqrt(v + BN_EPS) * g + b
        user = emb_user[user_id]
        cand = jnp.concatenate([emb_item_id[cand_item_id], emb_item_cat[cand_item_cat]], axis=-1)
        exp_seq = jnp.concatenate([emb_item_id[exp_item_id], emb_item_cat[exp_item_cat]], axis=-1)
        ipv_seq = jnp.concatenate([emb_item_id[ipv_item_id], emb_item_cat[ipv_item_cat]], axis=-1)
        exp_out = _attention_pool(exp_seq, cand, att_w1, att_b1, att_w2, att_b2)
        ipv_out = _attention_pool(ipv_seq, cand, att_w1, att_b1, att_w2, att_b2)
        x = jnp.concatenate([num_feat1[:, None], num_feat2[:, None], user, cand, exp_out, ipv_out], axis=1)
        h = jax.nn.relu(_bn_eval(x @ fc1_w + fc1_b, bn1_g, bn1_b, bn1_m, bn1_v))
        h = jax.nn.relu(_bn_eval(h @ fc2_w + fc2_b, bn2_g, bn2_b, bn2_m, bn2_v))
        mlp_out = h @ fc3_w + fc3_b
        score_logits = -jnp.log(1.0 / score[:, None] - 1.0)
        return jax.nn.sigmoid(mlp_out + score_logits)
    y = _L0_rec_ref(r_num_feat1, r_num_feat2, r_score, L0_rec_emb_item_id, L0_rec_emb_item_cat, L0_rec_emb_user, L0_rec_att_w1, L0_rec_att_b1, L0_rec_att_w2, L0_rec_att_b2, L0_rec_fc1_w, L0_rec_fc1_b, L0_rec_bn1_g, L0_rec_bn1_b, L0_rec_bn1_m, L0_rec_bn1_v, L0_rec_fc2_w, L0_rec_fc2_b, L0_rec_bn2_g, L0_rec_bn2_b, L0_rec_bn2_m, L0_rec_bn2_v, L0_rec_fc3_w, L0_rec_fc3_b, r_user_id, r_cand_item_id, r_cand_item_cat, r_exp_item_id, r_exp_item_cat, r_ipv_item_id, r_ipv_item_cat)
    return y

_drawn_inputs = setup_inputs


def setup_inputs(seed=0):
    import zlib

    import numpy as np

    out = dict(_drawn_inputs(seed))
    spreads = {'L0_rec_att_b1': (0.0, 2.0),
     'L0_rec_fc1_b': (0.0, 0.8),
     'L0_rec_bn1_g': (1.0, 0.6),
     'L0_rec_bn1_b': (0.0, 0.8),
     'L0_rec_fc2_b': (0.0, 0.8),
     'L0_rec_bn2_g': (1.0, 0.6),
     'L0_rec_bn2_b': (0.0, 0.8)}
    factors = {'r_num_feat1': 8.0,
     'r_num_feat2': 8.0,
     'L0_rec_emb_item_id': 8.0,
     'L0_rec_emb_item_cat': 26.691,
     'L0_rec_emb_user': 8.0,
     'L0_rec_att_w1': 64.0,
     'L0_rec_att_w2': 64.0,
     'L0_rec_fc1_w': 8.0,
     'L0_rec_bn1_m': 8.0,
     'L0_rec_bn1_v': 8.0,
     'L0_rec_fc2_w': 8.0,
     'L0_rec_bn2_m': 8.0,
     'L0_rec_bn2_v': 8.0,
     'L0_rec_fc3_w': 8.0}
    for name, (base, spread) in spreads.items():
        noise = np.random.default_rng([zlib.crc32(name.encode()), seed]).standard_normal(out[name].shape)
        drawn = base * np.exp(spread * noise) if base else spread * noise
        out[name] = jnp.asarray(drawn.astype(out[name].dtype))
    for name, factor in factors.items():
        out[name] = (out[name] * factor).astype(out[name].dtype)
    return out
```

```python
import concourse.bass as bass
from concourse import mybir
from contextlib import ExitStack

B, L = 2048, 200
D_ID, D_CAT, D_USER = 64, 32, 32
D = D_ID + D_CAT
H1, H2 = 200, 80
BN_EPS = 1e-5
P = 128
SEQS = 2
GB = 16
QUARTERS = P // (SEQS * GB)
LQ = L // QUARTERS
SQ = SEQS * QUARTERS
GROUPS = B // GB
ROW = SEQS * L
TB = 4
BATCHES = [(a, min(TB, LQ - a)) for a in range(0, LQ, TB)]
NB = len(BATCHES)
LC = 10
NC = LQ // LC
CH = B // P
EARLY = 4
H1C = H1 // 2
NT = 512


def build(nc, feat1, feat2, score, user_id, cand_id, cand_cat, seq_id, seq_cat,
          emb_id, emb_cat, emb_user, att_w1, att_b1, att_w2, att_b2,
          fc1_w, fc1_b, bn1_g, bn1_b, bn1_m, bn1_v, fc2_w, fc2_b, bn2_g, bn2_b, bn2_m, bn2_v,
          fc3_w, fc3_b, out):
    f32, i32 = mybir.dt.float32, mybir.dt.int32
    ALU, ACT, AX = mybir.AluOpType, mybir.ActivationFunctionType, mybir.AxisListType.X
    N_ID, N_CAT, N_USER = emb_id.shape[0], emb_cat.shape[0], emb_user.shape[0]
    ctx = ExitStack()
    with ctx:
        def sb(name, shape, dt=f32):
            return ctx.enter_context(nc.sbuf_tensor(name, shape, dt))

        def pb(name, shape):
            return ctx.enter_context(nc.psum_tensor(name, shape, f32))

        def sem(name):
            return ctx.enter_context(nc.semaphore(name))

        ident = sb("ident", [P, P])
        spread = sb("spread", [GB, SQ, P])
        gather_lanes = sb("gather_lanes", [P, SEQS * GB])
        w1_abcd = sb("w1_abcd", [D, 4, D])
        w_seq = sb("w_seq", [D, D])
        w_tgt = sb("w_tgt", [D, D])
        b1 = sb("b1", [D, 1])
        w2 = sb("w2", [D, 1])
        w2_cols = sb("w2_cols", [D, GB, GB])
        b2 = sb("b2", [GB, 1])
        idx_small = sb("idx_small", [P, 3, CH], i32)
        idx_neg = sb("idx_neg", [P, 3, CH])
        idx_wrapped = sb("idx_wrapped", [P, 3, CH])
        idx_fixed = sb("idx_fixed", [P, 3, CH], i32)
        cand_rows = sb("cand_rows", [P, CH, D])
        user_rows = sb("user_rows", [P, CH, D_USER])
        candT = sb("candT", [D, B])
        tgtT = sb("tgtT", [D, B])
        userT = sb("userT", [D_USER, B])
        poolT = sb("poolT", [D, SEQS, B])
        idx_raw = [sb(f"idx_raw{u}", [P, 2, LQ], i32) for u in range(2)]
        grp_neg = sb("grp_neg", [P, 2, LQ])
        grp_wrapped = sb("grp_wrapped", [P, 2, LQ])
        idx = [sb(f"idx{u}", [P, 2, LQ], i32) for u in range(2)]
        rows = [sb(f"rows{u}", [P, LQ, D]) for u in range(2)]
        seqT = [sb(f"seqT{u}", [D, GB, SQ, LQ]) for u in range(2)]
        w_row = [sb(f"w_row{u}", [D, GB, D]) for u in range(2)]
        hid = [sb(f"hid{u}", [D, ROW]) for u in range(2)]
        logit = sb("logit", [GB, SEQS, L])
        neg_max = sb("neg_max", [GB, SEQS])
        expd = sb("expd", [GB, SEQS, L])
        exp_sum = sb("exp_sum", [GB, SEQS])
        inv_sum = sb("inv_sum", [GB, SEQS])
        prob = sb("prob", [GB, SEQS, L])
        lane_w = sb("lane_w", [P, LQ])
        weighted = sb("weighted", [P, LC, D])
        partial = sb("partial", [P, NC, D])
        pooled = sb("pooled", [P, D])
        featT = sb("featT", [2, B])
        fc1_f = sb("fc1_f", [2, H1])
        fc1_u = sb("fc1_u", [D_USER, H1])
        fc1_x = sb("fc1_x", [D, 3, H1])
        fc2_s = sb("fc2_s", [H1C, 2, H2])
        fc3_s = sb("fc3_s", [H2, 1])
        fc3_bias = sb("fc3_bias", [P, 1])
        bn1 = sb("bn1", [H1C, 5, 2])
        bn2 = sb("bn2", [H2, 5, 1])
        bn1_w = sb("bn1_w", [H1C, 6, 2])
        bn2_w = sb("bn2_w", [H2, 6, 1])
        h1T = sb("h1T", [H1C, 2, NT])
        h2T = sb("h2T", [H2, B])
        score_s = sb("score_s", [P, CH])
        fin = sb("fin", [P, 8, CH])

        tp = [pb(f"tp{u}", [P, TB, P]) for u in range(2)]
        hp = [pb(f"hp{u}", [P, 512]) for u in range(2)]
        lp = pb("lp", [P, 512])
        sp_w = pb("sp_w", [P, 512])
        sp_p = pb("sp_p", [P, 512])
        sp_m = pb("sp_m", [P, 512])

        consts_made = sem("consts_made")
        att_loaded = sem("att_loaded")
        mlp_loaded = sem("mlp_loaded")
        small_loaded = sem("small_loaded")
        small_fixed = sem("small_fixed")
        small_gathered = sem("small_gathered")
        setup_step = sem("setup_step")
        att_ready = sem("att_ready")
        candT_put = sem("candT_put")
        candT_taken = sem("candT_taken")
        tgt_put = sem("tgt_put")
        tgt_taken = sem("tgt_taken")
        idx_loaded = [sem(f"idx_loaded{u}") for u in range(2)]
        idx_step = sem("idx_step")
        idx_ready = sem("idx_ready")
        gathered = [[sem(f"gathered{u}_{j}") for j in range(NB)] for u in range(2)]
        tp_put = sem("tp_put")
        tp_taken = sem("tp_taken")
        w_row_ready = sem("w_row_ready")
        hid_put = sem("hid_put")
        hid_ready = sem("hid_ready")
        logit_add = sem("logit_add")
        logit_ready = sem("logit_ready")
        max_ready = sem("max_ready")
        exp_ready = sem("exp_ready")
        inv_ready = sem("inv_ready")
        prob_ready = sem("prob_ready")
        spread_put = sem("spread_put")
        lane_w_ready = sem("lane_w_ready")
        chunk_weighted = sem("chunk_weighted")
        chunk_pooled = sem("chunk_pooled")
        pooled_ready = sem("pooled_ready")
        pool_put = sem("pool_put")
        poolT_ready = sem("poolT_ready")
        bn_step = sem("bn_step")
        bn_sqrt = sem("bn_sqrt")
        bn_ready = sem("bn_ready")
        h1_put = sem("h1_put")
        h1_ready = sem("h1_ready")
        h2_put = sem("h2_put")
        h2_ready = sem("h2_ready")
        y_put = sem("y_put")
        fin_exp_in = sem("fin_exp_in")
        fin_exp = sem("fin_exp")
        fin_step = sem("fin_step")
        out_stored = sem("out_stored")

        block = ctx.enter_context(nc.Block())

        def groups(eng, body):
            body(0, 0, 0)
            body(1, 1, 0)
            with eng.Fori(1, GROUPS // 2) as t:
                body(2 * t, 0, t)
                body(2 * t + 1, 1, t)
            body(GROUPS, 0, GROUPS // 2)

        @block.sync
        def _(sp):
            def col(v):
                return v.rearrange("(n a) -> n a", a=1)

            sp.dma_start(idx_small[:, 0, :], cand_id.rearrange("(p c) -> p c", c=CH)).then_inc(small_loaded, 16)
            sp.dma_start(idx_small[:, 1, :], cand_cat.rearrange("(p c) -> p c", c=CH)).then_inc(small_loaded, 16)
            sp.dma_start(idx_small[:, 2, :], user_id.rearrange("(p c) -> p c", c=CH)).then_inc(small_loaded, 16)

            def load_idx(g, u):
                sp.dma_start(idx_raw[u][:, 0, :], seq_id[bass.ds(g * P, P), :]).then_inc(idx_loaded[u], 16)
                sp.dma_start(idx_raw[u][:, 1, :], seq_cat[bass.ds(g * P, P), :]).then_inc(idx_loaded[u], 16)

            load_idx(0, 0)
            load_idx(1, 1)
            sp.dma_start(w1_abcd[:, :, :], att_w1.rearrange("(a p) n -> p a n", p=D)).then_inc(att_loaded, 16)
            sp.dma_start(b1[:, :], col(att_b1)).then_inc(att_loaded, 16)
            sp.dma_start(w2[:, :], att_w2).then_inc(att_loaded, 16)
            sp.dma_start(b2[:, :], att_b2.rearrange("(a n) -> a n", a=1).to_broadcast([GB, 1])).then_inc(att_loaded, 16)
            sp.dma_start(featT[0:1, :], feat1.rearrange("(a n) -> a n", a=1)).then_inc(mlp_loaded, 16)
            sp.dma_start(featT[1:2, :], feat2.rearrange("(a n) -> a n", a=1)).then_inc(mlp_loaded, 16)
            sp.dma_start(fc1_f[:, :], fc1_w[0:2, :]).then_inc(mlp_loaded, 16)
            sp.dma_start(fc1_u[:, :], fc1_w[2:2 + D_USER, :]).then_inc(mlp_loaded, 16)
            sp.dma_start(fc1_x[:, :, :], fc1_w[2 + D_USER:, :].rearrange("(a p) n -> p a n", p=D)).then_inc(mlp_loaded, 16)
            sp.dma_start(fc2_s[:, :, :], fc2_w.rearrange("(a p) n -> p a n", p=H1C)).then_inc(mlp_loaded, 16)
            sp.dma_start(fc3_s[:, :], fc3_w).then_inc(mlp_loaded, 16)
            sp.dma_start(fc3_bias[:, :], fc3_b.rearrange("(a n) -> a n", a=1).to_broadcast([P, 1])).then_inc(mlp_loaded, 16)
            sp.dma_start(score_s[:, :], score.rearrange("(p c) -> p c", c=CH)).then_inc(mlp_loaded, 16)
            for n, v in enumerate((fc1_b, bn1_g, bn1_b, bn1_m, bn1_v)):
                for c in range(2):
                    sp.dma_start(bn1[:, n, c:c + 1], col(v)[c * H1C:(c + 1) * H1C, :]).then_inc(mlp_loaded, 16)
            for n, v in enumerate((fc2_b, bn2_g, bn2_b, bn2_m, bn2_v)):
                sp.dma_start(bn2[:, n, :], col(v)).then_inc(mlp_loaded, 16)
            with sp.Fori(1, GROUPS // 2) as t:
                for u in range(2):
                    g = 2 * t + u
                    sp.wait_ge(idx_ready, g - 1)
                    load_idx(g, u)
            sp.wait_ge(fin_step, 6)
            sp.dma_start(out.rearrange("(p c) a -> p (c a)", c=CH), fin[:, 7, :]).then_inc(out_stored, 16)
            sp.wait_ge(out_stored, 16)

        MLP_LOADS = 16 * (9 + 10 + 5)

        @block.gpsimd
        def _(pool):
            def gather(dst, table, at):
                return pool.indirect_dma_start(out=dst, out_offset=None, in_=table,
                                               in_offset=bass.IndirectOffsetOnAxis(ap=at, axis=0))

            pool.memset(ident[:, :], 0.0).then_inc(consts_made, 1)
            pool.memset(spread[:, :, :], 0.0).then_inc(consts_made, 1)
            pool.wait_ge(consts_made, 2)
            pool.affine_select(out=ident[:, :], in_=ident[:, :], compare_op=ALU.not_equal, fill=1.0, base=0,
                               pattern=[[-1, P]], channel_multiplier=1).then_inc(consts_made, 1)
            pool.affine_select(out=spread[:, :, :], in_=spread[:, :, :], compare_op=ALU.not_equal, fill=1.0, base=0,
                               pattern=[[-GB, SQ], [1, P]], channel_multiplier=-1).then_inc(consts_made, 1)
            pool.wait_ge(small_fixed, 1)
            for c in range(CH):
                gather(cand_rows[:, c, 0:D_ID], emb_id, idx_fixed[:, 0, c:c + 1]).then_inc(small_gathered, 16)
                gather(cand_rows[:, c, D_ID:D], emb_cat, idx_fixed[:, 1, c:c + 1]).then_inc(small_gathered, 16)
                gather(user_rows[:, c, :], emb_user, idx_fixed[:, 2, c:c + 1]).then_inc(small_gathered, 16)

            def body(g, u, t):
                if isinstance(g, int) and g >= GROUPS:
                    return
                pool.wait_ge(idx_ready, g + 1)
                pool.nop(nofuse=True)
                need = 0
                for j, (a, n) in enumerate(BATCHES):
                    chunks = (a + n + LC - 1) // LC
                    if chunks > need and not (isinstance(g, int) and g < 2):
                        pool.wait_ge(chunk_pooled, NC * (g - 2) + chunks)
                        pool.nop(nofuse=True)
                        need = chunks
                    for l in range(a, a + n):
                        gather(rows[u][:, l, 0:D_ID], emb_id, idx[u][:, 0, l:l + 1]).then_inc(gathered[u][j], 16)
                        gather(rows[u][:, l, D_ID:D], emb_cat, idx[u][:, 1, l:l + 1]).then_inc(gathered[u][j], 16)

            groups(pool, body)

        @block.tensor
        def _(pe):
            pe.wait_ge(consts_made, 4)
            pe.wait_ge(small_gathered, 16 * 3 * CH)
            for c in range(0, CH, TB):
                k = c // TB
                if k >= 2:
                    pe.wait_ge(candT_taken, k - 1)
                for i in range(TB):
                    last = nc.tensor.transpose(tp[k % 2][0:D, i, :], cand_rows[:, c + i, :], ident[:, :])
                last.then_inc(candT_put, 1)
            for c in range(0, CH, TB):
                k = (CH + c) // TB
                pe.wait_ge(candT_taken, k - 1)
                for i in range(TB):
                    last = nc.tensor.transpose(tp[k % 2][0:D_USER, i, :], user_rows[:, c + i, :], ident[:, :])
                last.then_inc(candT_put, 1)
            pe.wait_ge(att_ready, 1)
            pe.wait_ge(candT_taken, CH // TB)
            for k in range(B // NT):
                if k >= 2:
                    pe.wait_ge(tgt_taken, k - 1)
                nc.tensor.matmul(hp[k % 2][0:D, :], w_tgt[:, :], candT[:, k * NT:(k + 1) * NT],
                                 start=True, stop=True).then_inc(tgt_put, 1)
            pe.wait_ge(candT_taken, 2 * CH // TB)
            pe.wait_ge(tgt_taken, B // NT)

            def body(g, u, t):
                first = isinstance(g, int) and g == 0
                last_one = isinstance(g, int) and g == GROUPS
                v = 1 - u
                if not first:
                    b = g - 1
                    pe.wait_ge(w_row_ready, b + 1)
                    pe.wait_ge(tp_taken, NB * (b + 1))
                    for i in range(GB + 1):
                        if i < GB:
                            if not (isinstance(b, int) and b == 0 and i < 2):
                                pe.wait_ge(hid_ready, GB * b + i - 1)
                            nc.tensor.matmul(hp[i % 2][0:D, 0:ROW], w_row[v][:, i, :],
                                             seqT[v][:, i, :, :].rearrange("d q l -> d (q l)"),
                                             start=True, stop=True).then_inc(hid_put, 1)
                        if i >= 1:
                            pe.wait_ge(hid_ready, GB * b + i)
                            if i == 1 and not (isinstance(b, int) and b == 0):
                                pe.wait_ge(logit_ready, b)
                            nc.tensor.matmul(lp[0:GB, 0:ROW], w2_cols[:, i - 1, :], hid[(i - 1) % 2][:, :],
                                             start=(i == 1), stop=(i == GB)).then_inc(logit_add, 1)

                def spread_weights():
                    pe.wait_ge(prob_ready, b + 1)
                    if not (isinstance(b, int) and b == 0):
                        pe.wait_ge(lane_w_ready, b)
                    for q in range(SQ):
                        last = nc.tensor.matmul(sp_w[:, 0:LQ], spread[:, q, :],
                                                prob[:, q // QUARTERS, (q % QUARTERS) * LQ:(q % QUARTERS + 1) * LQ],
                                                start=(q == 0), stop=(q == SQ - 1))
                    last.then_inc(spread_put, 1)

                def gather_pooled():
                    pe.wait_ge(pooled_ready, b + 1)
                    if not (isinstance(b, int) and b == 0):
                        pe.wait_ge(poolT_ready, b)
                    nc.tensor.matmul(sp_p[0:D, 0:SEQS * GB], pooled[:, :], gather_lanes[:, :],
                                     start=True, stop=True).then_inc(pool_put, 1)

                if not last_one:
                    for j, (a, n) in enumerate(BATCHES):
                        if j == EARLY and not first:
                            spread_weights()
                        k = NB * g + j
                        tile = tp[(u + j) % 2]
                        pe.wait_ge(gathered[u][j], 32 * n * (t + 1))
                        if not (isinstance(g, int) and g == 0 and j < 2):
                            pe.wait_ge(tp_taken, k - 1)
                        for i in range(n):
                            last = nc.tensor.transpose(tile[0:D, i, :], rows[u][:, a + i, :], ident[:, :])
                        last.then_inc(tp_put, 1)
                elif not first:
                    spread_weights()
                if not first:
                    gather_pooled()

            groups(pe, body)

            pe.wait_ge(mlp_loaded, MLP_LOADS)
            pe.wait_ge(poolT_ready, GROUPS)
            for k in range(B // NT):
                s = slice(k * NT, (k + 1) * NT)
                for c in range(2):
                    if k:
                        pe.wait_ge(h1_ready, 2 * (k - 1) + c + 1)
                    m = slice(c * H1C, (c + 1) * H1C)
                    parts = [(fc1_f[:, m], featT[:, s]), (fc1_u[:, m], userT[:, s]), (fc1_x[:, 0, m], candT[:, s]),
                             (fc1_x[:, 1, m], poolT[:, 0, s]), (fc1_x[:, 2, m], poolT[:, 1, s])]
                    for n, (w, x) in enumerate(parts):
                        last = nc.tensor.matmul(hp[c][0:H1C, :], w, x, start=(n == 0), stop=(n == len(parts) - 1))
                    last.then_inc(h1_put, 1)
                pe.wait_ge(h1_ready, 2 * (k + 1))
                if k:
                    pe.wait_ge(h2_ready, k)
                for c in range(2):
                    last = nc.tensor.matmul(lp[0:H2, :], fc2_s[:, c, :], h1T[:, c, :], start=(c == 0), stop=(c == 1))
                last.then_inc(h2_put, 1)
            pe.wait_ge(h2_ready, B // NT)
            for c in range(CH):
                last = nc.tensor.matmul(sp_m[:, c:c + 1], h2T[:, c::CH], fc3_s[:, :], start=True, stop=True)
            last.then_inc(y_put, 1)

        @block.scalar
        def _(act):
            for k in range(2 * CH // TB):
                act.wait_ge(candT_put, k + 1)
                w, dst = (D, candT) if k < CH // TB else (D_USER, userT)
                c = k * TB % CH
                act.activation(dst[:, :].rearrange("d (p c) -> d c p", c=CH)[:, c:c + TB, :],
                               tp[k % 2][0:w, :, :], ACT.Copy).then_inc(candT_taken, 1)
            act.wait_ge(att_loaded, 64)
            for k in range(B // NT):
                act.wait_ge(tgt_put, k + 1)
                act.activation(tgtT[:, k * NT:(k + 1) * NT], hp[k % 2][0:D, :], ACT.Identity,
                               bias=b1[:, :]).then_inc(tgt_taken, 1)
            act.wait_ge(tgt_taken, B // NT)

            def body(g, u, t):
                first = isinstance(g, int) and g == 0
                last_one = isinstance(g, int) and g == GROUPS
                b = g - 1
                if not first:
                    for i in range(GB):
                        act.wait_ge(hid_put, GB * b + i + 1)
                        if not (isinstance(b, int) and b == 0 and i < 2):
                            act.wait_ge(logit_add, GB * b + i - 1)
                        act.activation(hid[i % 2][:, :], hp[i % 2][0:D, 0:ROW], ACT.Relu,
                                       bias=tgtT[:, bass.ds(b * GB + i, 1)]).then_inc(hid_ready, 1)
                    act.wait_ge(max_ready, b + 1)
                    if not (isinstance(b, int) and b == 0):
                        act.wait_ge(prob_ready, b)
                    for s in range(SEQS):
                        act.activation(expd[:, s, :], logit[:, s, :], ACT.Exp, bias=neg_max[:, s:s + 1],
                                       accum_out=exp_sum[:, s:s + 1]).then_inc(exp_ready, 1)

                def lane_weights():
                    act.wait_ge(spread_put, b + 1)
                    if not (isinstance(b, int) and b == 0):
                        act.wait_ge(pooled_ready, b)
                    act.activation(lane_w[:, :], sp_w[:, 0:LQ], ACT.Copy).then_inc(lane_w_ready, 1)

                if not last_one:
                    for j, (a, n) in enumerate(BATCHES):
                        if j == EARLY and not first:
                            lane_weights()
                        act.wait_ge(tp_put, NB * g + j + 1)
                        if j == 0 and not (isinstance(g, int) and g < 2):
                            act.wait_ge(hid_put, GB * (g - 1))
                        act.activation(seqT[u][:, :, :, a:a + n].rearrange("d b q l -> d q b l"),
                                       tp[(u + j) % 2][0:D, 0:n, :].rearrange("d l (q b) -> d q b l", q=SQ),
                                       ACT.Copy).then_inc(tp_taken, 1)
                elif not first:
                    lane_weights()
                if not first:
                    act.wait_ge(pool_put, b + 1)
                    act.activation(poolT[:, :, bass.ds(b * GB, GB)],
                                   sp_p[0:D, 0:SEQS * GB].rearrange("d (s b) -> d s b", s=SEQS),
                                   ACT.Copy).then_inc(poolT_ready, 1)

            groups(act, body)

            act.wait_ge(bn_step, 1)
            act.activation(bn1_w[:, 1, :], bn1_w[:, 0, :], ACT.Sqrt).then_inc(bn_sqrt, 1)
            act.activation(bn2_w[:, 1, :], bn2_w[:, 0, :], ACT.Sqrt).then_inc(bn_sqrt, 1)
            act.wait_ge(bn_ready, 1)
            for k in range(B // NT):
                for c in range(2):
                    act.wait_ge(h1_put, 2 * k + c + 1)
                    if k:
                        act.wait_ge(h2_put, k)
                    act.activation(h1T[:, c, :], hp[c][0:H1C, :], ACT.Relu, bias=bn1_w[:, 5, c:c + 1],
                                   scale=bn1_w[:, 3, c:c + 1]).then_inc(h1_ready, 1)
                act.wait_ge(h2_put, k + 1)
                act.activation(h2T[:, k * NT:(k + 1) * NT], lp[0:H2, :], ACT.Relu, bias=bn2_w[:, 5, :],
                               scale=bn2_w[:, 3, :]).then_inc(h2_ready, 1)
            act.wait_ge(fin_exp_in, 1)
            act.activation(fin[:, 1, :], fin[:, 0, :], ACT.Exp, scale=-1.0).then_inc(fin_exp, 1)

        @block.vector
        def _(dve):
            steps = [0]

            def link(ins, s=setup_step):
                steps[0] += 1
                ins.then_inc(s, 1)
                dve.wait_ge(s, steps[0])

            dve.wait_ge(small_loaded, 48)
            sizes = (N_ID, N_CAT, N_USER)
            for n, size in enumerate(sizes):
                last = nc.vector.tensor_scalar(idx_neg[:, n, :], idx_small[:, n, :], 0.0, float(size), ALU.is_lt, ALU.mult)
            link(last)
            link(nc.vector.tensor_tensor(idx_wrapped[:, :, :], idx_small[:, :, :], idx_neg[:, :, :], ALU.add))
            for n, size in enumerate(sizes):
                last = nc.vector.tensor_scalar(idx_fixed[:, n, :], idx_wrapped[:, n, :], 0.0, float(size - 1), ALU.max, ALU.min)
            last.then_inc(small_fixed, 1)

            def fix_idx(g, u):
                dve.wait_ge(idx_loaded[u], 16 * (g - u) + 32)
                for n, size in enumerate((N_ID, N_CAT)):
                    last = nc.vector.tensor_scalar(grp_neg[:, n, :], idx_raw[u][:, n, :], 0.0, float(size), ALU.is_lt, ALU.mult)
                last.then_inc(idx_step, 1)
                dve.wait_ge(idx_step, 2 * g + 1)
                nc.vector.tensor_tensor(grp_wrapped[:, :, :], idx_raw[u][:, :, :], grp_neg[:, :, :], ALU.add).then_inc(idx_step, 1)
                dve.wait_ge(idx_step, 2 * g + 2)
                if not (isinstance(g, int) and g < 2):
                    dve.wait_ge(tp_put, NB * (g - 1))
                for n, size in enumerate((N_ID, N_CAT)):
                    last = nc.vector.tensor_scalar(idx[u][:, n, :], grp_wrapped[:, n, :], 0.0, float(size - 1), ALU.max, ALU.min)
                last.then_inc(idx_ready, 1)

            fix_idx(0, 0)
            dve.wait_ge(att_loaded, 64)
            nc.vector.memset(w2_cols[:, :, :], 0.0).then_inc(setup_step, 1)
            nc.vector.tensor_tensor(w_seq[:, :], w1_abcd[:, 0, :], w1_abcd[:, 2, :], ALU.add)
            steps[0] += 1
            dve.wait_ge(setup_step, steps[0])
            nc.vector.tensor_copy(w2_cols[:, :, :].rearrange("d a b -> d (a b)")[:, 0::GB + 1],
                                  w2[:, :].to_broadcast([D, GB]))
            dve.wait_ge(consts_made, 4)
            nc.vector.tensor_reduce(gather_lanes[:, :].rearrange("p (s b) -> p s b", s=SEQS),
                                    ident[:, :].rearrange("p (s q b) -> p s b q", s=SEQS, q=QUARTERS), AX, ALU.add)
            nc.vector.tensor_tensor(w_tgt[:, :], w1_abcd[:, 1, :], w1_abcd[:, 2, :], ALU.subtract).then_inc(att_ready, 1)
            dve.wait_ge(att_ready, 1)
            dve.wait_ge(candT_taken, CH // TB)

            def body(g, u, t):
                first = isinstance(g, int) and g == 0
                last_one = isinstance(g, int) and g == GROUPS
                b = g - 1
                v = 1 - u
                if not last_one:
                    if not (isinstance(g, int) and g < 2):
                        dve.wait_ge(hid_put, GB * (g - 1))
                    for i in range(GB):
                        last = nc.vector.scalar_tensor_tensor(
                            out=w_row[u][:, i, :], in0=w1_abcd[:, 3, :], scalar=candT[:, bass.ds(g * GB + i, 1)],
                            in1=w_seq[:, :], op0=ALU.mult, op1=ALU.add)
                    last.then_inc(w_row_ready, 1)
                if not first:
                    dve.wait_ge(logit_add, GB * (b + 1))
                    nc.vector.tensor_scalar(logit[:, :, :].rearrange("b s l -> b (s l)"), lp[0:GB, 0:ROW], b2[:, :], None,
                                            ALU.add).then_inc(logit_ready, 1)
                    dve.wait_ge(logit_ready, b + 1)
                    nc.vector.tensor_reduce(neg_max[:, :], logit[:, :, :], AX, ALU.max, negate=True).then_inc(max_ready, 1)
                    dve.wait_ge(exp_ready, SEQS * (b + 1))
                    nc.vector.reciprocal(inv_sum[:, :], exp_sum[:, :]).then_inc(inv_ready, 1)
                    dve.wait_ge(inv_ready, b + 1)
                    if not (isinstance(b, int) and b == 0):
                        dve.wait_ge(spread_put, b)
                    for s in range(SEQS):
                        last = nc.vector.tensor_scalar(prob[:, s, :], expd[:, s, :], inv_sum[:, s:s + 1], None, ALU.mult)
                    last.then_inc(prob_ready, 1)
                if not last_one and not (isinstance(g, int) and g == GROUPS - 1):
                    fix_idx(g + 1, v)
                if not first:
                    dve.wait_ge(lane_w_ready, b + 1)
                    for c in range(NC):
                        if not (isinstance(b, int) and b == 0 and c == 0):
                            dve.wait_ge(chunk_pooled, NC * b + c)
                        ls = slice(c * LC, (c + 1) * LC)
                        nc.vector.tensor_tensor(weighted[:, :, :], rows[v][:, ls, :],
                                                lane_w[:, ls].unsqueeze(2).to_broadcast([P, LC, D]),
                                                ALU.mult).then_inc(chunk_weighted, 1)
                        dve.wait_ge(chunk_weighted, NC * b + c + 1)
                        nc.vector.tensor_reduce(partial[:, c, :], weighted[:, :, :].rearrange("p l d -> p d l"), AX,
                                                ALU.add).then_inc(chunk_pooled, 1)
                    dve.wait_ge(chunk_pooled, NC * (b + 1))
                    if not (isinstance(b, int) and b == 0):
                        dve.wait_ge(pool_put, b)
                    nc.vector.tensor_reduce(pooled[:, :], partial[:, :, :].rearrange("p c d -> p d c"), AX,
                                            ALU.add).then_inc(pooled_ready, 1)

            body(0, 0, 0)
            body(1, 1, 0)
            with dve.Fori(1, GROUPS // 2 - 1) as t:
                body(2 * t, 0, t)
                body(2 * t + 1, 1, t)
            body(GROUPS - 2, 0, GROUPS // 2 - 1)
            body(GROUPS - 1, 1, GROUPS // 2 - 1)
            body(GROUPS, 0, GROUPS // 2)

            dve.wait_ge(mlp_loaded, MLP_LOADS)
            for src, w in ((bn1, bn1_w), (bn2, bn2_w)):
                last = nc.vector.tensor_scalar(w[:, 0, :], src[:, 4, :], BN_EPS, None, ALU.add)
            last.then_inc(bn_step, 1)
            dve.wait_ge(bn_sqrt, 2)
            steps[0] = 1
            for src, w in ((bn1, bn1_w), (bn2, bn2_w)):
                link(nc.vector.reciprocal(w[:, 2, :], w[:, 1, :]), bn_step)
                link(nc.vector.tensor_tensor(w[:, 3, :], w[:, 2, :], src[:, 1, :], ALU.mult), bn_step)
                link(nc.vector.tensor_tensor(w[:, 4, :], src[:, 0, :], src[:, 3, :], ALU.subtract), bn_step)
                link(nc.vector.tensor_tensor(w[:, 2, :], w[:, 4, :], w[:, 3, :], ALU.mult), bn_step)
                link(nc.vector.tensor_tensor(w[:, 5, :], w[:, 2, :], src[:, 2, :], ALU.add), bn_step)
            nc.vector.memset(fin[:, 7, :], 0.0).then_inc(bn_ready, 1)
            dve.wait_ge(bn_ready, 1)
            dve.wait_ge(y_put, 1)
            nc.vector.tensor_scalar(fin[:, 0, :], sp_m[:, 0:CH], fc3_bias[:, :], None, ALU.add).then_inc(fin_exp_in, 1)
            dve.wait_ge(fin_exp, 1)
            steps[0] = 0
            link(nc.vector.tensor_scalar(fin[:, 2, :], fin[:, 1, :], 1e-37, 1e37, ALU.max, ALU.min), fin_step)
            link(nc.vector.tensor_scalar(fin[:, 3, :], score_s[:, :], -1.0, 1.0, ALU.mult, ALU.add), fin_step)
            link(nc.vector.tensor_tensor(fin[:, 4, :], fin[:, 2, :], fin[:, 3, :], ALU.mult), fin_step)
            link(nc.vector.tensor_tensor(fin[:, 5, :], fin[:, 4, :], score_s[:, :], ALU.add), fin_step)
            link(nc.vector.reciprocal(fin[:, 6, :], fin[:, 5, :]), fin_step)
            nc.vector.tensor_tensor(fin[:, 7, :], fin[:, 6, :], score_s[:, :], ALU.mult).then_inc(fin_step, 1)


def kernel(**inputs):
    import numpy as np
    import concourse.bacc as bacc
    from concourse.bass_utils import run_bass_kernel_spmd

    def lanes(exp, ipv):
        x = np.stack([np.asarray(exp), np.asarray(ipv)]).reshape(SEQS, GROUPS, GB, QUARTERS, LQ)
        return x.transpose(1, 0, 3, 2, 4).reshape(GROUPS * P, LQ)

    nc = bacc.Bacc("TRN2", target_bir_lowering=False, num_devices=1)
    given = {n: inputs[n] for n in ("r_num_feat1", "r_num_feat2", "r_score", "r_user_id", "r_cand_item_id", "r_cand_item_cat")}
    given["seq_item_id"] = lanes(inputs["r_exp_item_id"], inputs["r_ipv_item_id"])
    given["seq_item_cat"] = lanes(inputs["r_exp_item_cat"], inputs["r_ipv_item_cat"])
    for n in ("emb_item_id", "emb_item_cat", "emb_user", "att_w1", "att_b1", "att_w2", "att_b2",
              "fc1_w", "fc1_b", "bn1_g", "bn1_b", "bn1_m", "bn1_v",
              "fc2_w", "fc2_b", "bn2_g", "bn2_b", "bn2_m", "bn2_v", "fc3_w", "fc3_b"):
        given[n] = inputs["L0_rec_" + n]
    arrays, args = {}, []
    for n, a in given.items():
        a = np.ascontiguousarray(a)
        arrays[f"in_{n}"] = a
        args.append(nc.dram_tensor(f"in_{n}", a.shape, mybir.dt.from_np(a.dtype), kind="ExternalInput").ap())
    args.append(nc.dram_tensor("out_0", (B, 1), mybir.dt.float32, kind="ExternalOutput").ap())
    build(nc, *args)
    r = run_bass_kernel_spmd(nc, [arrays], core_ids=[0])
    return r.results[0]["out_0"]
```

```python
import concourse.bass as bass
from concourse import mybir
from contextlib import ExitStack

B, L = 2048, 200
D_ID, D_CAT, D_USER = 64, 32, 32
D = D_ID + D_CAT
H1, H2 = 200, 80
BN_EPS = 1e-5
P = 128
SEQS = 2
GB = 16
QUARTERS = P // (SEQS * GB)
LQ = L // QUARTERS
SQ = SEQS * QUARTERS
GROUPS = B // GB
ROW = SEQS * L
TB = 4
BATCHES = [(a, min(TB, LQ - a)) for a in range(0, LQ, TB)]
NB = len(BATCHES)
LC = 10
NC = LQ // LC
PARTS = 3
TBLOCK = 2
OB = 3
OBLOCKS = [BATCHES[m:m + TBLOCK] for m in range(0, NB, TBLOCK)]
NO = len(OBLOCKS)
BEHIND = {1: [(3, 0)], 2: [(3, 1)], 3: [(4, 0), ("p", 0)], 4: [(4, 1), ("p", 1)], 5: [(5, 0), ("w", 0)],
          6: [(5, 1), ("a", 0)], 7: [(6, 0), ("w", 1)], 8: [(6, 1), ("a", 1)], 9: [("w", 2), ("p", 2)],
          10: [("a", 2)], 11: [("p", 3)]}
TAIL = 3
COLS = 4
HB = 8
PEEL = 4
AHEAD = 2
PIECES = 8
CH = B // P
EARLY = 3
H1C = H1 // 2
NT = 512


def build(nc, feat1, feat2, score, user_id, cand_id, cand_cat, seq_id, seq_cat,
          emb_id, emb_cat, emb_user, att_w1, att_b1, att_w2, att_b2,
          fc1_w, fc1_b, bn1_g, bn1_b, bn1_m, bn1_v, fc2_w, fc2_b, bn2_g, bn2_b, bn2_m, bn2_v,
          fc3_w, fc3_b, out):
    f32, i32 = mybir.dt.float32, mybir.dt.int32
    ALU, ACT, AX = mybir.AluOpType, mybir.ActivationFunctionType, mybir.AxisListType.X
    bf16, f16 = mybir.dt.bfloat16, mybir.dt.float16
    N_ID, N_CAT, N_USER = emb_id.shape[0], emb_cat.shape[0], emb_user.shape[0]
    CC = -(-N_CAT // P)
    FULL = N_CAT // P
    assert N_CAT <= 2048
    PW = B * SQ * LQ // (PIECES * P)
    cat_fixed = nc.dram_tensor("cat_fixed", (GROUPS, LQ * P), f16, kind="Internal").ap()
    ctx = ExitStack()
    with ctx:
        def sb(name, shape, dt=f32):
            return ctx.enter_context(nc.sbuf_tensor(name, shape, dt))

        def pb(name, shape):
            return ctx.enter_context(nc.psum_tensor(name, shape, f32))

        def sem(name):
            return ctx.enter_context(nc.semaphore(name))

        ident = sb("ident", [P, P])
        shift = sb("shift", [P, 2 * P - GB])
        gather_lanes = sb("gather_lanes", [P, SEQS * GB])
        w1_abcd = sb("w1_abcd", [D, 4, D])
        w_seq = sb("w_seq", [D, D])
        w_tgt = sb("w_tgt", [D, D])
        b1 = sb("b1", [D, 1])
        w2 = sb("w2", [D, 1])
        w2_cols = sb("w2_cols", [D, GB // COLS, P // COLS])
        b2 = sb("b2", [P, 1])
        idx_small = sb("idx_small", [P, 3, CH], i32)
        idx_neg = sb("idx_neg", [P, 3, CH])
        idx_wrapped = sb("idx_wrapped", [P, 3, CH])
        idx_fixed = sb("idx_fixed", [P, 3, CH], i32)
        candT = sb("candT", [D, B])
        tgtT = sb("tgtT", [D, B])
        user_rows = sb("user_rows", [P, CH, D_USER])
        late = sb("late", [P, SEQS * B])
        poolT = late[0:D, :].rearrange("d (s b) -> d s b", s=SEQS)
        assert 5 * PW <= SEQS * B
        cat_raw = [late[:, n * PW:(n + 1) * PW].bitcast(i32) for n in range(2)]
        cat_neg = late[:, 2 * PW:3 * PW]
        cat_wrapped = late[:, 3 * PW:4 * PW]
        cat_ok = [late[:, 4 * PW + n * PW // 2:4 * PW + (n + 1) * PW // 2].bitcast(f16) for n in range(2)]
        table_row = sb("table_row", [P, CC])
        table_row_i = sb("table_row_i", [P, CC], i32)
        cat_parts = sb("cat_parts", [P, CC, PARTS, D_CAT], bf16)
        cat_of = [sb(f"cat_of{u}", [P, LQ * P], f16) for u in range(2)]
        onehot = [sb(f"onehot{n}", [P, CC, TBLOCK * TB * P], bf16) for n in range(OB)]
        idx_raw = [sb(f"idx_raw{u}", [P, LQ], i32) for u in range(2)]
        grp_neg = sb("grp_neg", [P, LQ])
        grp_wrapped = sb("grp_wrapped", [P, LQ])
        idx = [sb(f"idx{u}", [P, LQ], i32) for u in range(2)]
        rows = [sb(f"rows{u}", [P, LQ, D]) for u in range(2)]
        cand_rows = rows[1][:, 0:CH, :]
        cat_table = rows[1][:, 2 * CH:2 * CH + CC, 0:D_CAT]
        cat_left = [rows[1][:, 2 * CH:2 * CH + CC, (1 + n) * D_CAT:(2 + n) * D_CAT] for n in range(2)]
        seq_area = sb("seq_area", [P, GB * SQ * LQ])
        seqT = seq_area[0:D, :].rearrange("d (b q l) -> d b q l", b=GB, q=SQ)
        w_row = sb("w_row", [D, GB, D])
        hid = sb("hid", [D, HB, ROW])
        neg_max = sb("neg_max", [P, SEQS])
        exp_sum = sb("exp_sum", [P, SEQS])
        inv_sum = sb("inv_sum", [P, SEQS])
        prob = sb("prob", [P, SEQS, L])
        lane_w = sb("lane_w", [P, LQ])
        weighted = sb("weighted", [P, LC, D])
        partial = sb("partial", [P, NC, D])
        pooled = sb("pooled", [P, D])
        used = [0]

        def behind_seq(lanes, width):
            used[0] += width
            assert used[0] <= GB * SQ * LQ
            return seq_area[0:lanes, used[0] - width:used[0]]

        smallT = behind_seq(D_USER + 2, B)
        fc1_s = behind_seq(D_USER + 2, H1)
        fc1_x = behind_seq(D, 3 * H1).rearrange("p (a n) -> p a n", a=3)
        fc2_s = behind_seq(H1C, 2 * H2).rearrange("p (a n) -> p a n", a=2)
        h1T = behind_seq(H1C, 2 * NT).rearrange("p (c n) -> p c n", c=2)
        fc3_s = sb("fc3_s", [H2, 1])
        fc3_bias = sb("fc3_bias", [P, 1])
        bn1 = sb("bn1", [H1C, 5, 2])
        bn2 = sb("bn2", [H2, 5, 1])
        bn1_w = sb("bn1_w", [H1C, 6, 2])
        bn2_w = sb("bn2_w", [H2, 6, 1])
        h2T = tgtT[0:H2, :]
        score_s = sb("score_s", [P, CH])
        fin = sb("fin", [P, 8, CH])

        tp = [pb(f"tp{u}", [P, TB, P]) for u in range(2)]
        hp = [pb(f"hp{u}", [P, 512]) for u in range(2)]
        lp = pb("lp", [P, 512])
        cp = [pb(f"cp{u}", [P, 512]) for u in range(2)]
        misc = pb("misc", [P, 512])
        sp_w, sp_p, sp_m = misc[:, 0:LQ], misc[0:D, 64:64 + SEQS * GB], misc[:, 96:96 + CH]

        consts_made = sem("consts_made")
        att_loaded = sem("att_loaded")
        mlp_loaded = sem("mlp_loaded")
        small_loaded = sem("small_loaded")
        cat_raw_loaded = [sem(f"cat_raw_loaded{n}") for n in range(2)]
        cat_step = sem("cat_step")
        cat_piece_ready = sem("cat_piece_ready")
        cat_stored = [sem(f"cat_stored{n}") for n in range(PIECES)]
        table_loaded = sem("table_loaded")
        table_cleared = sem("table_cleared")
        rows_numbered = sem("rows_numbered")
        table_ready = sem("table_ready")
        cat_spread = [sem(f"cat_spread{u}") for u in range(2)]
        onehot_ready = sem("onehot_ready")
        cat_put = sem("cat_put")
        cat_taken = sem("cat_taken")
        shift_ready = sem("shift_ready")
        small_fixed = sem("small_fixed")
        small_gathered = sem("small_gathered")
        late_loaded = sem("late_loaded")
        user_put = sem("user_put")
        user_taken = sem("user_taken")
        setup_step = sem("setup_step")
        att_ready = sem("att_ready")
        candT_put = sem("candT_put")
        candT_taken = sem("candT_taken")
        tgt_put = sem("tgt_put")
        tgt_taken = sem("tgt_taken")
        idx_loaded = [sem(f"idx_loaded{u}") for u in range(2)]
        idx_step = sem("idx_step")
        idx_ready = sem("idx_ready")
        gathered = [[sem(f"gathered{u}_{j}") for j in range(NB)] for u in range(2)]
        tp_put = sem("tp_put")
        tp_taken = sem("tp_taken")
        w_row_ready = sem("w_row_ready")
        hid_put = sem("hid_put")
        hid_ready = sem("hid_ready")
        logit_add = sem("logit_add")
        logit_ready = sem("logit_ready")
        max_ready = sem("max_ready")
        exp_ready = sem("exp_ready")
        inv_ready = sem("inv_ready")
        prob_ready = sem("prob_ready")
        spread_put = sem("spread_put")
        lane_w_ready = sem("lane_w_ready")
        chunk_weighted = sem("chunk_weighted")
        chunk_pooled = sem("chunk_pooled")
        pooled_ready = sem("pooled_ready")
        pool_put = sem("pool_put")
        poolT_ready = sem("poolT_ready")
        bn_step = sem("bn_step")
        bn_sqrt = sem("bn_sqrt")
        bn_ready = sem("bn_ready")
        h1_put = sem("h1_put")
        h1_ready = sem("h1_ready")
        h2_put = sem("h2_put")
        h2_ready = sem("h2_ready")
        y_put = sem("y_put")
        fin_exp_in = sem("fin_exp_in")
        fin_exp = sem("fin_exp")
        fin_step = sem("fin_step")
        out_stored = sem("out_stored")

        block = ctx.enter_context(nc.Block())

        def groups(eng, body):
            for g in range(PEEL):
                body(g, g % 2, g // 2)
            with eng.Fori(PEEL // 2, GROUPS // 2) as t:
                body(2 * t, 0, t)
                body(2 * t + 1, 1, t)
            body(GROUPS, 0, GROUPS // 2)

        @block.sync
        def _(sp):
            def col(v):
                return v.rearrange("(n a) -> n a", a=1)

            sp.dma_start(idx_small[:, 0, :], cand_id.rearrange("(p c) -> p c", c=CH)).then_inc(small_loaded, 16)
            sp.dma_start(idx_small[:, 1, :], cand_cat.rearrange("(p c) -> p c", c=CH)).then_inc(small_loaded, 16)
            sp.dma_start(idx_small[:, 2, :], user_id.rearrange("(p c) -> p c", c=CH)).then_inc(small_loaded, 16)

            def load_idx(g, u):
                sp.dma_start(idx_raw[u][:, :], seq_id[bass.ds(g * P, P), :]).then_inc(idx_loaded[u], 16)

            def spread_cat(g, u):
                sp.dma_start(cat_of[u][:, :], cat_fixed[bass.ds(g, 1), :].to_broadcast([P, LQ * P])).then_inc(cat_spread[u], 16)

            def load_piece(n):
                if n >= 2:
                    sp.wait_ge(cat_piece_ready, n - 1)
                sp.dma_start(cat_raw[n % 2], seq_cat[n * P:(n + 1) * P, :]).then_inc(cat_raw_loaded[n % 2], 16)

            def store_piece(n):
                sp.wait_ge(cat_piece_ready, n + 1)
                k = GROUPS // PIECES
                sp.dma_start(cat_fixed[n * k:(n + 1) * k, :].rearrange("g (r c) -> (g r) c", c=PW),
                             cat_ok[n % 2]).then_inc(cat_stored[n], 16)

            load_piece(0)
            load_idx(0, 0)
            load_piece(1)
            load_idx(1, 1)
            sp.wait_ge(table_cleared, 1)
            sp.dma_start(cat_table[:, 0:FULL, :], emb_cat[0:FULL * P, :].rearrange("(c p) d -> p c d", p=P)).then_inc(table_loaded, 16)
            if N_CAT > FULL * P:
                sp.dma_start(cat_table[0:N_CAT - FULL * P, FULL, :], emb_cat[FULL * P:, :]).then_inc(table_loaded, 16)
            store_piece(0)
            sp.wait_ge(cat_stored[0], 16)
            spread_cat(0, 0)
            spread_cat(1, 1)
            sp.dma_start(w1_abcd[:, :, :], att_w1.rearrange("(a p) n -> p a n", p=D)).then_inc(att_loaded, 16)
            sp.dma_start(b1[:, :], col(att_b1)).then_inc(att_loaded, 16)
            sp.dma_start(w2[:, :], att_w2).then_inc(att_loaded, 16)
            sp.dma_start(b2[:, :], att_b2.rearrange("(a n) -> a n", a=1).to_broadcast([P, 1])).then_inc(att_loaded, 16)
            sp.dma_start(fc3_s[:, :], fc3_w).then_inc(mlp_loaded, 16)
            sp.dma_start(fc3_bias[:, :], fc3_b.rearrange("(a n) -> a n", a=1).to_broadcast([P, 1])).then_inc(mlp_loaded, 16)
            sp.dma_start(score_s[:, :], score.rearrange("(p c) -> p c", c=CH)).then_inc(mlp_loaded, 16)
            for n, v in enumerate((fc1_b, bn1_g, bn1_b, bn1_m, bn1_v)):
                for c in range(2):
                    sp.dma_start(bn1[:, n, c:c + 1], col(v)[c * H1C:(c + 1) * H1C, :]).then_inc(mlp_loaded, 16)
            for n, v in enumerate((fc2_b, bn2_g, bn2_b, bn2_m, bn2_v)):
                sp.dma_start(bn2[:, n, :], col(v)).then_inc(mlp_loaded, 16)
            for n in range(2, PIECES):
                load_piece(n)
                store_piece(n - 1)
            store_piece(PIECES - 1)
            for n in range(1, PIECES):
                sp.wait_ge(cat_stored[n], 16)
            with sp.Fori(1, GROUPS // 2) as t:
                for u in range(2):
                    g = 2 * t + u
                    sp.wait_ge(idx_ready, g - 1)
                    load_idx(g, u)
                    sp.wait_ge(onehot_ready, NO * (g - 1))
                    spread_cat(g, u)
            sp.wait_ge(hid_put, GB * GROUPS)
            sp.dma_start(smallT[D_USER:D_USER + 1, :], feat1.rearrange("(a n) -> a n", a=1)).then_inc(late_loaded, 16)
            sp.dma_start(smallT[D_USER + 1:D_USER + 2, :], feat2.rearrange("(a n) -> a n", a=1)).then_inc(late_loaded, 16)
            sp.dma_start(fc1_s[D_USER:D_USER + 2, :], fc1_w[0:2, :]).then_inc(late_loaded, 16)
            sp.dma_start(fc1_s[0:D_USER, :], fc1_w[2:2 + D_USER, :]).then_inc(late_loaded, 16)
            sp.dma_start(fc1_x[:, :, :], fc1_w[2 + D_USER:, :].rearrange("(a p) n -> p a n", p=D)).then_inc(late_loaded, 16)
            sp.dma_start(fc2_s[:, :, :], fc2_w.rearrange("(a p) n -> p a n", p=H1C)).then_inc(late_loaded, 16)
            sp.wait_ge(fin_step, 6)
            sp.dma_start(out.rearrange("(p c) a -> p (c a)", c=CH), fin[:, 7, :]).then_inc(out_stored, 16)
            sp.wait_ge(out_stored, 16)

        MLP_LOADS = 16 * (3 + 10 + 5)
        LATE_LOADS = 16 * 6

        @block.gpsimd
        def _(pool):
            def gather(dst, table, at):
                return pool.indirect_dma_start(out=dst, out_offset=None, in_=table,
                                               in_offset=bass.IndirectOffsetOnAxis(ap=at, axis=0))

            pool.memset(ident[:, :], 0.0).then_inc(consts_made, 1)
            pool.memset(shift[:, :], 0.0).then_inc(consts_made, 1)
            pool.wait_ge(consts_made, 1)
            pool.affine_select(out=ident[:, :], in_=ident[:, :], compare_op=ALU.not_equal, fill=1.0, base=0,
                               pattern=[[-1, P]], channel_multiplier=1).then_inc(consts_made, 1)
            pool.iota(table_row_i[:, :], pattern=[[P, CC]], base=0, channel_multiplier=1).then_inc(rows_numbered, 1)
            pool.wait_ge(small_fixed, 1)
            for c in range(CH):
                gather(cand_rows[:, c, 0:D_ID], emb_id, idx_fixed[:, 0, c:c + 1]).then_inc(small_gathered, 16)
                gather(cand_rows[:, c, D_ID:D], emb_cat, idx_fixed[:, 1, c:c + 1]).then_inc(small_gathered, 16)
                gather(user_rows[:, c, :], emb_user, idx_fixed[:, 2, c:c + 1]).then_inc(small_gathered, 16)

            def body(g, u, t):
                if isinstance(g, int) and g >= GROUPS:
                    return
                pool.wait_ge(idx_ready, g + 1)
                pool.nop(nofuse=True)
                if isinstance(g, int) and g == 1:
                    pool.wait_ge(candT_put, CH // TB)
                    pool.nop(nofuse=True)
                    pool.wait_ge(table_ready, 1)
                    pool.nop(nofuse=True)
                need = 0
                for j, (a, n) in enumerate(BATCHES):
                    chunks = (a + n + LC - 1) // LC
                    if chunks > need and not (isinstance(g, int) and g < 2):
                        pool.wait_ge(chunk_pooled, NC * (g - 2) + chunks)
                        pool.nop(nofuse=True)
                        need = chunks
                    for l in range(a, a + n):
                        gather(rows[u][:, l, 0:D_ID], emb_id, idx[u][:, l:l + 1]).then_inc(gathered[u][j], 16)

            groups(pool, body)

        @block.tensor
        def _(pe):
            pe.wait_ge(table_ready, 1)
            pe.wait_ge(shift_ready, 1)
            pe.wait_ge(consts_made, 3)
            pe.wait_ge(small_gathered, 16 * 3 * CH)
            for c in range(0, CH, TB):
                k = c // TB
                if k >= 2:
                    pe.wait_ge(candT_taken, k - 1)
                for i in range(TB):
                    last = nc.tensor.transpose(tp[k % 2][0:D, i, :], cand_rows[:, c + i, :], ident[:, :])
                last.then_inc(candT_put, 1)
            pe.wait_ge(att_ready, 1)
            pe.wait_ge(candT_taken, CH // TB)
            for k in range(B // NT):
                if k >= 2:
                    pe.wait_ge(tgt_taken, k - 1)
                nc.tensor.matmul(hp[k % 2][0:D, :], w_tgt[:, :], candT[:, k * NT:(k + 1) * NT],
                                 start=True, stop=True).then_inc(tgt_put, 1)
            pe.wait_ge(tgt_taken, B // NT)

            def add_logits(b, k):
                pe.wait_ge(hid_ready, GB * b + COLS * (k + 1))
                if k == 0 and not (isinstance(b, int) and b == 0):
                    pe.wait_ge(logit_ready, b)
                for c in range(COLS):
                    m = P // COLS
                    last = nc.tensor.matmul(lp[c * m:(c + 1) * m, 0:ROW], w2_cols[:, k, :], hid[:, (COLS * k + c) % HB, :],
                                            start=(k == 0), stop=(k == GB // COLS - 1))
                last.then_inc(logit_add, 1)

            def body(g, u, t):
                first = isinstance(g, int) and g == 0
                second = isinstance(g, int) and g == 1
                last_one = isinstance(g, int) and g == GROUPS
                b = g - 1
                if not first:
                    pe.wait_ge(w_row_ready, b + 1)
                    pe.wait_ge(tp_taken, NB * (b + 1))
                    for i in range(GB):
                        if not (isinstance(b, int) and b == 0 and i < 2):
                            pe.wait_ge(hid_ready, GB * b + i - 1)
                        nc.tensor.matmul(hp[i % 2][0:D, 0:ROW], w_row[:, i, :],
                                         seqT[:, i, :, :].rearrange("d q l -> d (q l)"),
                                         start=True, stop=True).then_inc(hid_put, 1)
                        if i >= COLS and i % COLS == 0:
                            add_logits(b, i // COLS - 1)

                def look_up(j):
                    a, n = BATCHES[j]
                    m = j // TBLOCK
                    pe.wait_ge(onehot_ready, NO * g + m + 1)
                    if not (isinstance(g, int) and g == 0 and j < 2):
                        pe.wait_ge(cat_taken, NB * g + j - 1)
                    for i in range(n):
                        at = (a + i - OBLOCKS[m][0][0]) * P
                        for c in range(CC):
                            last = nc.tensor.matmul(cp[(u + j) % 2][:, i * PARTS * D_CAT:(i + 1) * PARTS * D_CAT],
                                                    onehot[m % OB][:, c, at:at + P],
                                                    cat_parts[:, c, :, :].rearrange("p k d -> p (k d)"),
                                                    start=(c == 0), stop=(c == CC - 1))
                    last.then_inc(cat_put, 1)

                def spread_weights():
                    pe.wait_ge(prob_ready, b + 1)
                    if not second:
                        pe.wait_ge(poolT_ready, g - 1)
                    if not (isinstance(b, int) and b == 0):
                        pe.wait_ge(lane_w_ready, b)
                    for q in range(SQ):
                        last = nc.tensor.matmul(sp_w, shift[:, P - GB * (q + 1):2 * P - GB * (q + 1)],
                                                prob[:, q // QUARTERS, (q % QUARTERS) * LQ:(q % QUARTERS + 1) * LQ],
                                                start=(q == 0), stop=(q == SQ - 1))
                    last.then_inc(spread_put, 1)

                def gather_pooled(b):
                    pe.wait_ge(pooled_ready, b + 1)
                    if not (isinstance(b, int) and b == 0):
                        pe.wait_ge(poolT_ready, b)
                    nc.tensor.matmul(sp_p, pooled[:, :], gather_lanes[:, :], start=True, stop=True).then_inc(pool_put, 1)

                if not last_one:
                    look_up(0)
                if not first:
                    add_logits(b, GB // COLS - 1)
                if not last_one:
                    for j in range(1, AHEAD):
                        look_up(j)
                if not first and not second:
                    gather_pooled(g - 2)
                if not last_one:
                    for j, (a, n) in enumerate(BATCHES):
                        if j == EARLY and not first:
                            spread_weights()
                        if j + AHEAD < NB:
                            look_up(j + AHEAD)
                        k = NB * g + j
                        tile = tp[(u + j) % 2]
                        pe.wait_ge(gathered[u][j], 16 * n * (t + 1))
                        pe.wait_ge(cat_taken, k + 1)
                        if not (isinstance(g, int) and g == 0 and j < 2):
                            pe.wait_ge(tp_taken, k - 1)
                        for i in range(n):
                            last = nc.tensor.transpose(tile[0:D, i, :], rows[u][:, a + i, :], ident[:, :])
                        last.then_inc(tp_put, 1)
                else:
                    for k in range(CH // TB):
                        if k >= 2:
                            pe.wait_ge(user_taken, k - 1)
                        else:
                            pe.wait_ge(tp_taken, NB * GROUPS)
                        for i in range(TB):
                            last = nc.tensor.transpose(tp[k % 2][0:D_USER, i, :], user_rows[:, k * TB + i, :], ident[:, :])
                        last.then_inc(user_put, 1)
                    spread_weights()
                    gather_pooled(b)

            groups(pe, body)

            pe.wait_ge(mlp_loaded, MLP_LOADS)
            pe.wait_ge(late_loaded, LATE_LOADS)
            pe.wait_ge(user_taken, CH // TB)
            pe.wait_ge(poolT_ready, GROUPS)
            for k in range(B // NT):
                s = slice(k * NT, (k + 1) * NT)
                for c in range(2):
                    if k:
                        pe.wait_ge(h1_ready, 2 * (k - 1) + c + 1)
                    m = slice(c * H1C, (c + 1) * H1C)
                    parts = [(fc1_s[:, m], smallT[:, s]), (fc1_x[:, 0, m], candT[:, s]),
                             (fc1_x[:, 1, m], poolT[:, 0, s]), (fc1_x[:, 2, m], poolT[:, 1, s])]
                    for n, (w, x) in enumerate(parts):
                        last = nc.tensor.matmul(hp[c][0:H1C, :], w, x, start=(n == 0), stop=(n == len(parts) - 1))
                    last.then_inc(h1_put, 1)
                pe.wait_ge(h1_ready, 2 * (k + 1))
                if k:
                    pe.wait_ge(h2_ready, k)
                for c in range(2):
                    last = nc.tensor.matmul(lp[0:H2, :], fc2_s[:, c, :], h1T[:, c, :], start=(c == 0), stop=(c == 1))
                last.then_inc(h2_put, 1)
            pe.wait_ge(h2_ready, B // NT)
            for c in range(CH):
                last = nc.tensor.matmul(sp_m[:, c:c + 1], h2T[:, c::CH], fc3_s[:, :], start=True, stop=True)
            last.then_inc(y_put, 1)

        @block.scalar
        def _(act):
            def take_small(k, dst, w, put, taken):
                act.wait_ge(put, k + 1)
                act.activation(dst.rearrange("d (p c) -> d c p", c=CH)[:, k * TB:(k + 1) * TB, :],
                               tp[k % 2][0:w, :, :], ACT.Copy).then_inc(taken, 1)

            for k in range(CH // TB):
                take_small(k, candT[:, :], D, candT_put, candT_taken)
            act.wait_ge(att_loaded, 64)
            for k in range(B // NT):
                act.wait_ge(tgt_put, k + 1)
                act.activation(tgtT[:, k * NT:(k + 1) * NT], hp[k % 2][0:D, :], ACT.Identity,
                               bias=b1[:, :]).then_inc(tgt_taken, 1)
            act.wait_ge(tgt_taken, B // NT)

            def body(g, u, t):
                first = isinstance(g, int) and g == 0
                last_one = isinstance(g, int) and g == GROUPS
                b = g - 1
                if not first:
                    for i in range(GB):
                        act.wait_ge(hid_put, GB * b + i + 1)
                        if not (isinstance(b, int) and b == 0 and i < HB):
                            act.wait_ge(logit_add, GB // COLS * b + (i - HB) // COLS + 1)
                        act.activation(hid[:, i % HB, :], hp[i % 2][0:D, 0:ROW], ACT.Relu,
                                       bias=tgtT[:, bass.ds(b * GB + i, 1)]).then_inc(hid_ready, 1)
                    act.wait_ge(logit_add, GB // COLS * (b + 1))
                    if not (isinstance(b, int) and b == 0):
                        act.wait_ge(spread_put, b)
                    act.activation(prob[:, :, :].rearrange("b s l -> b (s l)"), lp[:, 0:ROW], ACT.Identity,
                                   bias=b2[:, :]).then_inc(logit_ready, 1)
                    act.wait_ge(max_ready, b + 1)
                    for s in range(SEQS):
                        act.activation(prob[:, s, :], prob[:, s, :], ACT.Exp, bias=neg_max[:, s:s + 1],
                                       accum_out=exp_sum[:, s:s + 1]).then_inc(exp_ready, 1)

                def norm_weights():
                    act.wait_ge(inv_ready, b + 1)
                    for s in range(SEQS):
                        last = act.activation(prob[:, s, :], prob[:, s, :], ACT.Copy, scale=inv_sum[:, s:s + 1])
                    last.then_inc(prob_ready, 1)

                def lane_weights():
                    act.wait_ge(spread_put, b + 1)
                    if not (isinstance(b, int) and b == 0):
                        act.wait_ge(pooled_ready, b)
                    act.activation(lane_w[:, :], sp_w, ACT.Copy).then_inc(lane_w_ready, 1)

                def keep_pooled(b):
                    act.wait_ge(pool_put, b + 1)
                    act.activation(poolT[:, :, bass.ds(b * GB, GB)], sp_p.rearrange("d (s b) -> d s b", s=SEQS),
                                   ACT.Copy).then_inc(poolT_ready, 1)

                if not last_one:
                    for j, (a, n) in enumerate(BATCHES):
                        if j == 1 and not first:
                            norm_weights()
                        if j == 2 and not (isinstance(g, int) and g < 2):
                            if isinstance(g, int) and g == 2:
                                for k in range(PIECES):
                                    act.wait_ge(cat_stored[k], 16)
                            keep_pooled(g - 2)
                        if j == EARLY and not first:
                            lane_weights()
                        act.wait_ge(tp_put, NB * g + j + 1)
                        if j == 0 and not first:
                            act.wait_ge(hid_put, GB * g)
                        act.activation(seqT[:, :, :, a:a + n].rearrange("d b q l -> d q b l"),
                                       tp[(u + j) % 2][0:D, 0:n, :].rearrange("d l (q b) -> d q b l", q=SQ),
                                       ACT.Copy).then_inc(tp_taken, 1)
                else:
                    norm_weights()
                    keep_pooled(g - 2)
                    act.wait_ge(hid_put, GB * GROUPS)
                    for k in range(CH // TB):
                        take_small(k, smallT[0:D_USER, :], D_USER, user_put, user_taken)
                    lane_weights()
                    keep_pooled(b)

            groups(act, body)

            act.wait_ge(bn_step, 1)
            act.activation(bn1_w[:, 1, :], bn1_w[:, 0, :], ACT.Sqrt).then_inc(bn_sqrt, 1)
            act.activation(bn2_w[:, 1, :], bn2_w[:, 0, :], ACT.Sqrt).then_inc(bn_sqrt, 1)
            act.wait_ge(bn_ready, 1)
            for k in range(B // NT):
                for c in range(2):
                    act.wait_ge(h1_put, 2 * k + c + 1)
                    if k:
                        act.wait_ge(h2_put, k)
                    act.activation(h1T[:, c, :], hp[c][0:H1C, :], ACT.Relu, bias=bn1_w[:, 5, c:c + 1],
                                   scale=bn1_w[:, 3, c:c + 1]).then_inc(h1_ready, 1)
                act.wait_ge(h2_put, k + 1)
                act.activation(h2T[:, k * NT:(k + 1) * NT], lp[0:H2, :], ACT.Relu, bias=bn2_w[:, 5, :],
                               scale=bn2_w[:, 3, :]).then_inc(h2_ready, 1)
            act.wait_ge(fin_exp_in, 1)
            act.activation(fin[:, 1, :], fin[:, 0, :], ACT.Exp, scale=-1.0).then_inc(fin_exp, 1)

        @block.vector
        def _(dve):
            steps = [0]

            def link(ins, s=setup_step):
                steps[0] += 1
                ins.then_inc(s, 1)
                dve.wait_ge(s, steps[0])

            dve.wait_ge(small_loaded, 48)
            sizes = (N_ID, N_CAT, N_USER)
            for n, size in enumerate(sizes):
                last = nc.vector.tensor_scalar(idx_neg[:, n, :], idx_small[:, n, :], 0.0, float(size), ALU.is_lt, ALU.mult)
            link(last)
            link(nc.vector.tensor_tensor(idx_wrapped[:, :, :], idx_small[:, :, :], idx_neg[:, :, :], ALU.add))
            for n, size in enumerate(sizes):
                last = nc.vector.tensor_scalar(idx_fixed[:, n, :], idx_wrapped[:, n, :], 0.0, float(size - 1), ALU.max, ALU.min)
            last.then_inc(small_fixed, 1)

            def fix_idx(g, u):
                dve.wait_ge(idx_loaded[u], 8 * (g - u) + 16)
                nc.vector.tensor_scalar(grp_neg[:, :], idx_raw[u][:, :], 0.0, float(N_ID), ALU.is_lt, ALU.mult).then_inc(idx_step, 1)
                dve.wait_ge(idx_step, 2 * g + 1)
                nc.vector.tensor_tensor(grp_wrapped[:, :], idx_raw[u][:, :], grp_neg[:, :], ALU.add).then_inc(idx_step, 1)
                dve.wait_ge(idx_step, 2 * g + 2)
                if not (isinstance(g, int) and g < 2):
                    dve.wait_ge(tp_put, NB * (g - 1))
                nc.vector.tensor_scalar(idx[u][:, :], grp_wrapped[:, :], 0.0, float(N_ID - 1), ALU.max, ALU.min).then_inc(idx_ready, 1)

            fix_idx(0, 0)

            def fix_piece(n):
                dve.wait_ge(cat_raw_loaded[n % 2], 16 * (n // 2 + 1))
                nc.vector.tensor_scalar(cat_neg, cat_raw[n % 2], 0.0, float(N_CAT), ALU.is_lt, ALU.mult).then_inc(cat_step, 1)
                dve.wait_ge(cat_step, 2 * n + 1)
                nc.vector.tensor_tensor(cat_wrapped, cat_raw[n % 2], cat_neg, ALU.add).then_inc(cat_step, 1)
                dve.wait_ge(cat_step, 2 * n + 2)
                if n >= 2:
                    dve.wait_ge(cat_stored[n - 2], 16)
                nc.vector.tensor_scalar(cat_ok[n % 2], cat_wrapped, 0.0, float(N_CAT - 1), ALU.max, ALU.min).then_inc(cat_piece_ready, 1)

            nc.vector.memset(cat_table[:, :, :], 0.0).then_inc(table_cleared, 1)
            fix_piece(0)
            dve.wait_ge(table_loaded, 16 * (1 + (N_CAT > FULL * P)))
            link(nc.vector.tensor_copy(cat_parts[:, :, 0, :], cat_table[:, :, :]))
            link(nc.vector.tensor_tensor(cat_left[0], cat_table[:, :, :], cat_parts[:, :, 0, :], ALU.subtract))
            link(nc.vector.tensor_copy(cat_parts[:, :, 1, :], cat_left[0]))
            link(nc.vector.tensor_tensor(cat_left[1], cat_left[0], cat_parts[:, :, 1, :], ALU.subtract))
            dve.wait_ge(rows_numbered, 1)
            nc.vector.tensor_copy(table_row[:, :], table_row_i[:, :])
            nc.vector.tensor_copy(cat_parts[:, :, 2, :], cat_left[1]).then_inc(table_ready, 1)
            dve.wait_ge(table_ready, 1)
            for n in range(1, PIECES):
                fix_piece(n)
            dve.wait_ge(att_loaded, 64)
            link(nc.vector.memset(w2_cols[:, :, :], 0.0))
            nc.vector.tensor_copy(w2_cols[:, :, :].rearrange("d a b -> d (a b)")[:, 0::P // COLS + 1],
                                  w2[:, :].to_broadcast([D, GB // COLS]))
            nc.vector.tensor_tensor(w_seq[:, :], w1_abcd[:, 0, :], w1_abcd[:, 2, :], ALU.add)
            dve.wait_ge(consts_made, 3)
            nc.vector.tensor_reduce(gather_lanes[:, :].rearrange("p (s b) -> p s b", s=SEQS),
                                    ident[:, :].rearrange("p (s q b) -> p s b q", s=SEQS, q=QUARTERS), AX, ALU.add)
            nc.vector.tensor_copy(shift[:, P - GB:P].rearrange("p (k c) -> p k c", c=COLS),
                                  ident[:, :].rearrange("p (c k) -> p k c", c=COLS)[:, 0:GB // COLS, :]).then_inc(shift_ready, 1)
            nc.vector.tensor_tensor(w_tgt[:, :], w1_abcd[:, 1, :], w1_abcd[:, 2, :], ALU.subtract).then_inc(att_ready, 1)
            dve.wait_ge(att_ready, 1)
            dve.wait_ge(candT_taken, CH // TB)

            def body(g, u, t):
                first = isinstance(g, int) and g == 0
                last_one = isinstance(g, int) and g == GROUPS
                b = g - 1
                v = 1 - u

                def make_onehot(m, halves=(0, 1)):
                    if m == 0:
                        dve.wait_ge(cat_spread[u], 16 * (t + 1))
                    k = NO * g + m
                    if m >= OB:
                        dve.wait_ge(cat_put, NB * g + TBLOCK * (m - OB + 1))
                    elif not first:
                        dve.wait_ge(cat_put, NB * g)
                    lo = OBLOCKS[m][0][0] * P
                    w = sum(n for _, n in OBLOCKS[m]) * P
                    for c in range(halves[0] * CC // 2, (halves[-1] + 1) * CC // 2):
                        last = nc.vector.tensor_scalar(onehot[m % OB][:, c, 0:w], cat_of[u][:, lo:lo + w],
                                                       table_row[:, c:c + 1], None, ALU.is_equal)
                    if halves[-1] == 1:
                        last.then_inc(onehot_ready, 1)

                def take_cat(j):
                    a, n = BATCHES[j]
                    dve.wait_ge(cat_put, NB * g + j + 1)
                    nc.vector.tensor_reduce(rows[u][:, a:a + n, D_ID:D],
                                            cp[(u + j) % 2][:, 0:n * PARTS * D_CAT].rearrange(
                                                "p (l k d) -> p l d k", k=PARTS, d=D_CAT), AX, ALU.add).then_inc(cat_taken, 1)

                def weight_chunk(b, v, c):
                    if c == 0:
                        dve.wait_ge(lane_w_ready, b + 1)
                    if not (isinstance(b, int) and b == 0 and c == 0):
                        dve.wait_ge(chunk_pooled, NC * b + c)
                    ls = slice(c * LC, (c + 1) * LC)
                    nc.vector.tensor_tensor(weighted[:, :, :], rows[v][:, ls, :],
                                            lane_w[:, ls].unsqueeze(2).to_broadcast([P, LC, D]),
                                            ALU.mult).then_inc(chunk_weighted, 1)

                def add_chunk(b, c):
                    dve.wait_ge(chunk_weighted, NC * b + c + 1)
                    nc.vector.tensor_reduce(partial[:, c, :], weighted[:, :, :].rearrange("p l d -> p d l"), AX,
                                            ALU.add).then_inc(chunk_pooled, 1)

                def make_right_sides(quarter):
                    if quarter == 0 and not first:
                        dve.wait_ge(hid_put, GB * g)
                    for i in range(quarter * GB // 4, (quarter + 1) * GB // 4):
                        last = nc.vector.scalar_tensor_tensor(
                            out=w_row[:, i, :], in0=w1_abcd[:, 3, :], scalar=candT[:, bass.ds(g * GB + i, 1)],
                            in1=w_seq[:, :], op0=ALU.mult, op1=ALU.add)
                    if quarter == 3:
                        last.then_inc(w_row_ready, 1)

                def behind(j):
                    for kind, n in BEHIND.get(j, []):
                        if kind == "p":
                            make_right_sides(n)
                        elif kind == "w" and not first:
                            weight_chunk(b, v, n)
                        elif kind == "a" and not first:
                            add_chunk(b, n)
                        elif isinstance(kind, int):
                            make_onehot(kind, (n,))

                def finish_pooling(b):
                    dve.wait_ge(chunk_pooled, NC * (b + 1))
                    if not (isinstance(b, int) and b == 0):
                        dve.wait_ge(pool_put, b)
                    nc.vector.tensor_reduce(pooled[:, :], partial[:, :, :].rearrange("p c d -> p d c"), AX,
                                            ALU.add).then_inc(pooled_ready, 1)

                if not last_one:
                    make_onehot(0)
                    make_onehot(1)
                if not (isinstance(g, int) and g < 2):
                    for c in range(TAIL, NC):
                        weight_chunk(g - 2, u, c)
                        add_chunk(g - 2, c)
                    finish_pooling(g - 2)
                if not last_one:
                    for m in range(2, OB):
                        make_onehot(m)
                    for j in range(AHEAD):
                        take_cat(j)
                        behind(j)
                if not first:
                    dve.wait_ge(logit_ready, b + 1)
                    nc.vector.tensor_reduce(neg_max[:, :], prob[:, :, :], AX, ALU.max, negate=True).then_inc(max_ready, 1)
                if not last_one:
                    take_cat(AHEAD)
                    behind(AHEAD)
                if not first:
                    dve.wait_ge(exp_ready, SEQS * (b + 1))
                    nc.vector.reciprocal(inv_sum[:, :], exp_sum[:, :]).then_inc(inv_ready, 1)
                if not last_one and not (isinstance(g, int) and g == GROUPS - 1):
                    fix_idx(g + 1, v)
                if not last_one:
                    for j in range(AHEAD + 1, NB):
                        take_cat(j)
                        behind(j)
                else:
                    for c in range(NC):
                        weight_chunk(b, v, c)
                        add_chunk(b, c)
                    finish_pooling(b)

            for g in range(PEEL):
                body(g, g % 2, g // 2)
            with dve.Fori(PEEL // 2, GROUPS // 2 - 1) as t:
                body(2 * t, 0, t)
                body(2 * t + 1, 1, t)
            body(GROUPS - 2, 0, GROUPS // 2 - 1)
            body(GROUPS - 1, 1, GROUPS // 2 - 1)
            body(GROUPS, 0, GROUPS // 2)

            dve.wait_ge(mlp_loaded, MLP_LOADS)
            for src, w in ((bn1, bn1_w), (bn2, bn2_w)):
                last = nc.vector.tensor_scalar(w[:, 0, :], src[:, 4, :], BN_EPS, None, ALU.add)
            last.then_inc(bn_step, 1)
            dve.wait_ge(bn_sqrt, 2)
            steps[0] = 1
            for src, w in ((bn1, bn1_w), (bn2, bn2_w)):
                link(nc.vector.reciprocal(w[:, 2, :], w[:, 1, :]), bn_step)
                link(nc.vector.tensor_tensor(w[:, 3, :], w[:, 2, :], src[:, 1, :], ALU.mult), bn_step)
                link(nc.vector.tensor_tensor(w[:, 4, :], src[:, 0, :], src[:, 3, :], ALU.subtract), bn_step)
                link(nc.vector.tensor_tensor(w[:, 2, :], w[:, 4, :], w[:, 3, :], ALU.mult), bn_step)
                link(nc.vector.tensor_tensor(w[:, 5, :], w[:, 2, :], src[:, 2, :], ALU.add), bn_step)
            nc.vector.memset(fin[:, 7, :], 0.0).then_inc(bn_ready, 1)
            dve.wait_ge(bn_ready, 1)
            dve.wait_ge(y_put, 1)
            nc.vector.tensor_scalar(fin[:, 0, :], sp_m[:, 0:CH], fc3_bias[:, :], None, ALU.add).then_inc(fin_exp_in, 1)
            dve.wait_ge(fin_exp, 1)
            steps[0] = 0
            link(nc.vector.tensor_scalar(fin[:, 2, :], fin[:, 1, :], 1e-37, 1e37, ALU.max, ALU.min), fin_step)
            link(nc.vector.tensor_scalar(fin[:, 3, :], score_s[:, :], -1.0, 1.0, ALU.mult, ALU.add), fin_step)
            link(nc.vector.tensor_tensor(fin[:, 4, :], fin[:, 2, :], fin[:, 3, :], ALU.mult), fin_step)
            link(nc.vector.tensor_tensor(fin[:, 5, :], fin[:, 4, :], score_s[:, :], ALU.add), fin_step)
            link(nc.vector.reciprocal(fin[:, 6, :], fin[:, 5, :]), fin_step)
            nc.vector.tensor_tensor(fin[:, 7, :], fin[:, 6, :], score_s[:, :], ALU.mult).then_inc(fin_step, 1)


def kernel(**inputs):
    import numpy as np
    import concourse.bacc as bacc
    from concourse.bass_utils import run_bass_kernel_spmd

    def lanes(exp, ipv):
        x = np.stack([np.asarray(exp), np.asarray(ipv)]).reshape(SEQS, GROUPS, GB, QUARTERS, LQ)
        return x.transpose(1, 0, 3, 2, 4).reshape(GROUPS * P, LQ)

    nc = bacc.Bacc("TRN2", target_bir_lowering=False, num_devices=1)
    given = {n: inputs[n] for n in ("r_num_feat1", "r_num_feat2", "r_score", "r_user_id", "r_cand_item_id", "r_cand_item_cat")}
    given["seq_item_id"] = lanes(inputs["r_exp_item_id"], inputs["r_ipv_item_id"])
    cats = lanes(inputs["r_exp_item_cat"], inputs["r_ipv_item_cat"]).reshape(GROUPS, P, LQ).transpose(0, 2, 1)
    given["seq_item_cat"] = cats.reshape(PIECES * P, -1)
    for n in ("emb_item_id", "emb_item_cat", "emb_user", "att_w1", "att_b1", "att_w2", "att_b2",
              "fc1_w", "fc1_b", "bn1_g", "bn1_b", "bn1_m", "bn1_v",
              "fc2_w", "fc2_b", "bn2_g", "bn2_b", "bn2_m", "bn2_v", "fc3_w", "fc3_b"):
        given[n] = inputs["L0_rec_" + n]
    arrays, args = {}, []
    for n, a in given.items():
        a = np.ascontiguousarray(a)
        arrays[f"in_{n}"] = a
        args.append(nc.dram_tensor(f"in_{n}", a.shape, mybir.dt.from_np(a.dtype), kind="ExternalInput").ap())
    args.append(nc.dram_tensor("out_0", (B, 1), mybir.dt.float32, kind="ExternalOutput").ap())
    build(nc, *args)
    r = run_bass_kernel_spmd(nc, [arrays], core_ids=[0])
    return r.results[0]["out_0"]
```

```python
import concourse.bass as bass
from concourse import mybir
from contextlib import ExitStack

B, L = 2048, 200
D_ID, D_CAT, D_USER = 64, 32, 32
D = D_ID + D_CAT
H1, H2 = 200, 80
BN_EPS = 1e-5
P = 128
SEQS = 2
GB = 16
QUARTERS = P // (SEQS * GB)
LQ = L // QUARTERS
SQ = SEQS * QUARTERS
GROUPS = B // GB
ROW = SEQS * L
TB = 4
BATCHES = [(a, min(TB, LQ - a)) for a in range(0, LQ, TB)]
NB = len(BATCHES)
LC = 10
NC = LQ // LC
PARTS = 3
TBLOCK = 2
OB = 3
LO = 32
LOOKUPS = [(a, min(n, LO - a)) for a, n in BATCHES if a < LO]
NOH = len(LOOKUPS)
FIRST_CAT = LO // TB
OBLOCKS = [LOOKUPS[m:m + TBLOCK] for m in range(0, NOH, TBLOCK)]
NO = len(OBLOCKS)
BEHIND = {1: [(3, 0)], 2: [(3, 1)], 3: [("s", 0), ("p", 0)], 4: [("s", 1), ("w", 0), ("s", 2), ("a", 0)],
          5: [("w", 1), ("s", 3), ("a", 1)], 6: [("c", 0), ("s", 4), ("p", 1)],
          7: [("p", 2), ("s", 5), ("p", 3)] + [("s", k) for k in range(6, 17)]}
PREPARE = 4
KEY = 1024
WB = 2
ROUNDS = -(-LQ // 8)
SORT_STEPS = 4 + 2 * ROUNDS - 1
SPARED = [(16, 18), (18, 20), (20, 22), (22, 24), (24, 32), (32, LQ)]
ALWAYS = SPARED[0][0] // TB
TAIL = 2
COLS = 4
HB = 8
PEEL = 4
AHEAD = 2
CH = B // P
EARLY = 3
H1C = H1 // 2
NT = 512


def build(nc, feat1, feat2, score, user_id, cand_id, cand_cat, seq_id, seq_cat,
          emb_id, emb_cat, emb_user, att_w1, att_b1, att_w2, att_b2,
          fc1_w, fc1_b, bn1_g, bn1_b, bn1_m, bn1_v, fc2_w, fc2_b, bn2_g, bn2_b, bn2_m, bn2_v,
          fc3_w, fc3_b, out):
    f32, i32 = mybir.dt.float32, mybir.dt.int32
    ALU, ACT, AX = mybir.AluOpType, mybir.ActivationFunctionType, mybir.AxisListType.X
    bf16, f16 = mybir.dt.bfloat16, mybir.dt.float16
    N_ID, N_CAT, N_USER = emb_id.shape[0], emb_cat.shape[0], emb_user.shape[0]
    CC = -(-N_CAT // P)
    FULL = N_CAT // P
    assert LO % TB == 0 or LO // TB == NOH - 1
    assert N_CAT <= KEY <= 2048 and N_ID * KEY < 1 << 24
    cat_turned = nc.dram_tensor("cat_turned", (GROUPS, LO * P), f16, kind="Internal").ap()
    ctx = ExitStack()
    with ctx:
        def sb(name, shape, dt=f32):
            return ctx.enter_context(nc.sbuf_tensor(name, shape, dt))

        def pb(name, shape):
            return ctx.enter_context(nc.psum_tensor(name, shape, f32))

        def sem(name):
            return ctx.enter_context(nc.semaphore(name))

        ident = sb("ident", [P, P])
        shift = sb("shift", [P, 2 * P - GB])
        gather_lanes = sb("gather_lanes", [P, SEQS * GB])
        w_prod = sb("w_prod", [D, D])
        w_seq = sb("w_seq", [D, D])
        w_tgt = sb("w_tgt", [D, D])
        b1 = sb("b1", [D, 1])
        w2 = sb("w2", [D, 1])
        w2_cols = sb("w2_cols", [D, GB // COLS, P // COLS])
        b2 = sb("b2", [P, 1])
        idx_small = sb("idx_small", [P, 3, CH], i32)
        idx_neg = sb("idx_neg", [P, 3, CH])
        idx_wrapped = sb("idx_wrapped", [P, 3, CH])
        idx_fixed = sb("idx_fixed", [P, 3, CH], i32)
        candT = sb("candT", [D, B])
        tgtT = sb("tgtT", [D, B])
        poolT = sb("poolT", [D, SEQS, B])
        table_row = sb("table_row", [P, CC])
        table_row_i = sb("table_row_i", [P, CC], i32)
        cat_parts = sb("cat_parts", [P, CC, PARTS, D_CAT], bf16)
        cat_of = [sb(f"cat_of{u}", [P, LO * P], f16) for u in range(2)]
        onehot = [sb(f"onehot{n}", [P, CC, TBLOCK * TB * P], bf16) for n in range(OB)]
        idx_raw = [sb(f"idx_raw{u}", [P, 2, LQ], i32) for u in range(2)]
        grp_neg = sb("grp_neg", [P, 2, LQ])
        grp_wrapped = sb("grp_wrapped", [P, 2, LQ])
        grp_ok = grp_neg
        keys = [sb("keys0", [P, LQ]), grp_wrapped[:, 0, :]]
        sorted_keys = sb("sorted_keys", [P, ROUNDS * 8])
        key_i = sb("key_i", [P, LQ], i32)
        key_hi = sb("key_hi", [P, LQ], i32)
        is_other = grp_neg[:, 1, :]
        cat_lane = sb("cat_lane", [P, LQ])
        cat16 = sb("cat16", [LO, P], f16)
        cat_idx = [sb(f"cat_idx{u}", [P, LQ - LO], i32) for u in range(2)]
        others = sb("others", [P, 1])
        steps_needed = [sb(f"steps_needed{u}", [1, 1], i32) for u in range(2)]
        last_item = sb("last_item", [P, D_ID])
        idx = [sb(f"idx{u}", [P, LQ], i32) for u in range(2)]
        rows = [sb(f"rows{u}", [P, LQ, D]) for u in range(2)]
        user_rows = rows[0][:, 0:CH, 0:D_USER]
        cand_rows = rows[1][:, 0:CH, :]
        cat_table = rows[1][:, 2 * CH:2 * CH + CC, 0:D_CAT]
        cat_left = [rows[1][:, 2 * CH:2 * CH + CC, (1 + n) * D_CAT:(2 + n) * D_CAT] for n in range(2)]
        seq_area = sb("seq_area", [P, GB * SQ * LQ])
        seqT = seq_area[0:D, :].rearrange("d (b q l) -> d b q l", b=GB, q=SQ)
        w_row = sb("w_row", [D, GB, D])
        hid = sb("hid", [D, HB, ROW])
        neg_max = sb("neg_max", [P, SEQS])
        exp_sum = sb("exp_sum", [P, SEQS])
        inv_sum = sb("inv_sum", [P, SEQS])
        prob = sb("prob", [P, SEQS, L])
        lane_w = sb("lane_w", [P, LQ])
        weighted = [sb(f"weighted{n}", [P, LC, D]) for n in range(WB)]
        w1_abc = weighted[1][0:D, 0:3, :]
        partial = sb("partial", [P, NC, D])
        pooled = sb("pooled", [P, D])
        used = [0]

        def behind_seq(lanes, width):
            used[0] += width
            assert used[0] <= GB * SQ * LQ
            return seq_area[0:lanes, used[0] - width:used[0]]

        smallT = behind_seq(D_USER + 2, B)
        fc1_s = behind_seq(D_USER + 2, H1)
        fc1_x = behind_seq(D, 3 * H1).rearrange("p (a n) -> p a n", a=3)
        fc2_s = behind_seq(H1C, 2 * H2).rearrange("p (a n) -> p a n", a=2)
        h1T = behind_seq(H1C, 2 * NT).rearrange("p (c n) -> p c n", c=2)
        fc3_s = sb("fc3_s", [H2, 1])
        fc3_bias = sb("fc3_bias", [P, 1])
        bn1 = sb("bn1", [H1C, 5, 2])
        bn2 = sb("bn2", [H2, 5, 1])
        bn1_w = sb("bn1_w", [H1C, 6, 2])
        bn2_w = sb("bn2_w", [H2, 6, 1])
        h2T = tgtT[0:H2, :]
        score_s = sb("score_s", [P, CH])
        fin = sb("fin", [P, 8, CH])

        tp = [pb(f"tp{u}", [P, TB, P]) for u in range(2)]
        hp = [pb(f"hp{u}", [P, 512]) for u in range(2)]
        lp = pb("lp", [P, 512])
        cp = [pb(f"cp{u}", [P, 512]) for u in range(2)]
        misc = pb("misc", [P, 512])
        hid_banks = cp + hp
        turned, lane_counts = misc[0:LO, P:2 * P], misc[0:1, 2 * P:3 * P]
        sp_w, sp_p, sp_m = misc[:, 0:LQ], misc[0:D, 64:64 + SEQS * GB], misc[:, 96:96 + CH]

        consts_made = sem("consts_made")
        att_loaded = sem("att_loaded")
        mlp_loaded = sem("mlp_loaded")
        small_loaded = sem("small_loaded")
        sort_step = sem("sort_step")
        sorted_ready = sem("sorted_ready")
        cat_lane_ready = sem("cat_lane_ready")
        turned_put = sem("turned_put")
        cat16_ready = sem("cat16_ready")
        cat_stored = sem("cat_stored")
        count_ready = sem("count_ready")
        last_item_loaded = sem("last_item_loaded")
        table_loaded = sem("table_loaded")
        table_cleared = sem("table_cleared")
        rows_numbered = sem("rows_numbered")
        table_ready = sem("table_ready")
        cat_spread = [sem(f"cat_spread{u}") for u in range(2)]
        onehot_ready = sem("onehot_ready")
        cat_put = sem("cat_put")
        cat_taken = sem("cat_taken")
        shift_ready = sem("shift_ready")
        small_fixed = sem("small_fixed")
        small_gathered = sem("small_gathered")
        user_gathered = sem("user_gathered")
        late_loaded = sem("late_loaded")
        user_put = sem("user_put")
        user_taken = sem("user_taken")
        setup_step = sem("setup_step")
        att_ready = sem("att_ready")
        candT_put = sem("candT_put")
        candT_taken = sem("candT_taken")
        tgt_put = sem("tgt_put")
        tgt_taken = sem("tgt_taken")
        idx_loaded = [sem(f"idx_loaded{u}") for u in range(2)]
        idx_step = sem("idx_step")
        idx_ready = sem("idx_ready")
        gathered = [[sem(f"gathered{u}_{j}") for j in range(ALWAYS)] for u in range(2)]
        spared_gathered = [[sem(f"spared_gathered{u}_{k}") for k in range(len(SPARED))] for u in range(2)]
        cats_gathered = [[sem(f"cats_gathered{u}_{j}") for j in range(FIRST_CAT, NB)] for u in range(2)]
        filled = sem("filled")
        tp_put = sem("tp_put")
        tp_taken = sem("tp_taken")
        w_row_ready = sem("w_row_ready")
        hid_put = sem("hid_put")
        hid_ready = sem("hid_ready")
        logit_add = sem("logit_add")
        logit_ready = sem("logit_ready")
        max_ready = sem("max_ready")
        exp_ready = sem("exp_ready")
        inv_ready = sem("inv_ready")
        prob_ready = sem("prob_ready")
        spread_put = sem("spread_put")
        lane_w_ready = sem("lane_w_ready")
        chunk_weighted = sem("chunk_weighted")
        chunk_pooled = sem("chunk_pooled")
        pooled_ready = sem("pooled_ready")
        pool_put = sem("pool_put")
        poolT_ready = sem("poolT_ready")
        bn_step = sem("bn_step")
        bn_sqrt = sem("bn_sqrt")
        bn_ready = sem("bn_ready")
        h1_put = sem("h1_put")
        h1_ready = sem("h1_ready")
        h2_put = sem("h2_put")
        h2_ready = sem("h2_ready")
        y_put = sem("y_put")
        fin_exp_in = sem("fin_exp_in")
        fin_exp = sem("fin_exp")
        fin_step = sem("fin_step")
        out_stored = sem("out_stored")

        block = ctx.enter_context(nc.Block())

        def groups(eng, body):
            for g in range(PEEL):
                body(g, g % 2, g // 2)
            with eng.Fori(PEEL // 2, GROUPS // 2 - 1) as t:
                body(2 * t, 0, t)
                body(2 * t + 1, 1, t)
            for g in range(GROUPS - 2, GROUPS + 1):
                body(g, g % 2, g // 2)

        @block.sync
        def _(sp):
            def col(v):
                return v.rearrange("(n a) -> n a", a=1)

            sp.dma_start(idx_small[:, 0, :], cand_id.rearrange("(p c) -> p c", c=CH)).then_inc(small_loaded, 16)
            sp.dma_start(idx_small[:, 1, :], cand_cat.rearrange("(p c) -> p c", c=CH)).then_inc(small_loaded, 16)
            sp.dma_start(idx_small[:, 2, :], user_id.rearrange("(p c) -> p c", c=CH)).then_inc(small_loaded, 16)

            def load_idx(g, u):
                sp.dma_start(idx_raw[u][:, 0, :], seq_id[bass.ds(g * P, P), :]).then_inc(idx_loaded[u], 16)
                sp.dma_start(idx_raw[u][:, 1, :], seq_cat[bass.ds(g * P, P), :]).then_inc(idx_loaded[u], 16)

            def spread_cat(g, u):
                sp.wait_ge(cat16_ready, g + 1)
                sp.nop(nofuse=True)
                sp.dma_start(cat_turned[bass.ds(g, 1), :].rearrange("a (l p) -> (a l) p", p=P), cat16[:, :]).then_inc(cat_stored, 16)
                sp.wait_ge(cat_stored, 16 * (g + 1))
                sp.nop(nofuse=True)
                if not (isinstance(g, int) and g < 2):
                    sp.wait_ge(onehot_ready, NO * (g - 1))
                    sp.nop(nofuse=True)
                sp.dma_start(cat_of[u][:, :], cat_turned[bass.ds(g, 1), :].to_broadcast([P, LO * P])).then_inc(cat_spread[u], 16)

            load_idx(0, 0)
            load_idx(1, 1)
            sp.wait_ge(table_cleared, 1)
            sp.dma_start(cat_table[:, 0:FULL, :], emb_cat[0:FULL * P, :].rearrange("(c p) d -> p c d", p=P)).then_inc(table_loaded, 16)
            if N_CAT > FULL * P:
                sp.dma_start(cat_table[0:N_CAT - FULL * P, FULL, :], emb_cat[FULL * P:, :]).then_inc(table_loaded, 16)
            sp.dma_start(last_item[:, :], emb_id[N_ID - 1:N_ID, :].to_broadcast([P, D_ID])).then_inc(last_item_loaded, 16)
            sp.dma_start(w1_abc, att_w1[0:3 * D, :].rearrange("(a p) n -> p a n", p=D)).then_inc(att_loaded, 16)
            sp.dma_start(w_prod[:, :], att_w1[3 * D:, :]).then_inc(att_loaded, 16)
            sp.dma_start(b1[:, :], col(att_b1)).then_inc(att_loaded, 16)
            sp.dma_start(w2[:, :], att_w2).then_inc(att_loaded, 16)
            sp.dma_start(b2[:, :], att_b2.rearrange("(a n) -> a n", a=1).to_broadcast([P, 1])).then_inc(att_loaded, 16)
            sp.dma_start(fc3_s[:, :], fc3_w).then_inc(mlp_loaded, 16)
            sp.dma_start(fc3_bias[:, :], fc3_b.rearrange("(a n) -> a n", a=1).to_broadcast([P, 1])).then_inc(mlp_loaded, 16)
            sp.dma_start(score_s[:, :], score.rearrange("(p c) -> p c", c=CH)).then_inc(mlp_loaded, 16)
            for n, v in enumerate((fc1_b, bn1_g, bn1_b, bn1_m, bn1_v)):
                for c in range(2):
                    sp.dma_start(bn1[:, n, c:c + 1], col(v)[c * H1C:(c + 1) * H1C, :]).then_inc(mlp_loaded, 16)
            for n, v in enumerate((fc2_b, bn2_g, bn2_b, bn2_m, bn2_v)):
                sp.dma_start(bn2[:, n, :], col(v)).then_inc(mlp_loaded, 16)

            def feed(g, u, more=True):
                if more:
                    sp.wait_ge(sorted_ready, g + 1)
                    sp.nop(nofuse=True)
                    load_idx(g + 2, u)
                spread_cat(g, u)

            for g in range(2):
                feed(g, g)
            with sp.Fori(1, GROUPS // 2 - 1) as t:
                for u in range(2):
                    feed(2 * t + u, u)
            for g in range(GROUPS - 2, GROUPS):
                feed(g, g % 2, more=False)
            sp.wait_ge(hid_put, GB * GROUPS)
            sp.dma_start(smallT[D_USER:D_USER + 1, :], feat1.rearrange("(a n) -> a n", a=1)).then_inc(late_loaded, 16)
            sp.dma_start(smallT[D_USER + 1:D_USER + 2, :], feat2.rearrange("(a n) -> a n", a=1)).then_inc(late_loaded, 16)
            sp.dma_start(fc1_s[D_USER:D_USER + 2, :], fc1_w[0:2, :]).then_inc(late_loaded, 16)
            sp.dma_start(fc1_s[0:D_USER, :], fc1_w[2:2 + D_USER, :]).then_inc(late_loaded, 16)
            sp.dma_start(fc1_x[:, :, :], fc1_w[2 + D_USER:, :].rearrange("(a p) n -> p a n", p=D)).then_inc(late_loaded, 16)
            sp.dma_start(fc2_s[:, :, :], fc2_w.rearrange("(a p) n -> p a n", p=H1C)).then_inc(late_loaded, 16)
            sp.wait_ge(fin_step, 6)
            sp.dma_start(out.rearrange("(p c) a -> p (c a)", c=CH), fin[:, 7, :]).then_inc(out_stored, 16)
            sp.wait_ge(out_stored, 16)

        MLP_LOADS = 16 * (3 + 10 + 5)
        LATE_LOADS = 16 * 6

        @block.gpsimd
        def _(pool):
            def gather(dst, table, at):
                return pool.indirect_dma_start(out=dst, out_offset=None, in_=table,
                                               in_offset=bass.IndirectOffsetOnAxis(ap=at, axis=0))

            pool.memset(ident[:, :], 0.0).then_inc(consts_made, 1)
            pool.memset(shift[:, :], 0.0).then_inc(consts_made, 1)
            pool.wait_ge(consts_made, 1)
            pool.affine_select(out=ident[:, :], in_=ident[:, :], compare_op=ALU.not_equal, fill=1.0, base=0,
                               pattern=[[-1, P]], channel_multiplier=1).then_inc(consts_made, 1)
            pool.iota(table_row_i[:, :], pattern=[[P, CC]], base=0, channel_multiplier=1).then_inc(rows_numbered, 1)
            pool.wait_ge(last_item_loaded, 16)
            pool.wait_ge(small_fixed, 1)
            for c in range(CH):
                gather(cand_rows[:, c, 0:D_ID], emb_id, idx_fixed[:, 0, c:c + 1]).then_inc(small_gathered, 16)
                gather(cand_rows[:, c, D_ID:D], emb_cat, idx_fixed[:, 1, c:c + 1]).then_inc(small_gathered, 16)

            overwritten = [[pool.alloc_register(f"overwritten{u}_{k}") for k in range(len(SPARED))] for u in range(2)]
            for u in range(2):
                for k in range(len(SPARED)):
                    pool.reg_mov(overwritten[u][k], 1)

            def body(g, u, t):
                if isinstance(g, int) and g == GROUPS:
                    pool.wait_ge(chunk_pooled, NC * (g - 1))
                    pool.nop(nofuse=True)
                    for c in range(CH):
                        gather(user_rows[:, c, :], emb_user, idx_fixed[:, 2, c:c + 1]).then_inc(user_gathered, 16)
                    return
                pool.wait_ge(idx_ready, g + 1)
                pool.nop(nofuse=True)
                if isinstance(g, int) and g == 1:
                    pool.wait_ge(candT_put, CH // TB)
                    pool.nop(nofuse=True)
                    pool.wait_ge(table_ready, 1)
                    pool.nop(nofuse=True)
                pool.wait_ge(count_ready, g + 1)
                pool.nop(nofuse=True)
                needed = pool.value_load(steps_needed[u][0:1, 0:1])
                need = 0

                def wait_for_room(end):
                    nonlocal need
                    chunks = (end + LC - 1) // LC
                    if chunks > need and not (isinstance(g, int) and g < 2):
                        pool.wait_ge(chunk_pooled, NC * (g - 2) + chunks)
                        pool.nop(nofuse=True)
                        need = chunks

                def gather_items(a, end, done):
                    for l in range(a, end):
                        gather(rows[u][:, l, 0:D_ID], emb_id, idx[u][:, l:l + 1]).then_inc(done, 16)

                for j in range(ALWAYS):
                    a, n = BATCHES[j]
                    wait_for_room(a + n)
                    gather_items(a, a + n, gathered[u][j])
                for k, (a, end) in enumerate(SPARED):
                    wait_for_room(end)
                    with pool.If(needed > a):
                        gather_items(a, end, spared_gathered[u][k])
                        pool.reg_mov(overwritten[u][k], 1)
                    with pool.Else(), pool.If_cmp(overwritten[u][k], 1, "IS_EQ"):
                        pool.reg_mov(overwritten[u][k], 0)
                        pool.tensor_copy(rows[u][:, a:end, 0:D_ID],
                                         last_item[:, :].unsqueeze(1).to_broadcast([P, end - a, D_ID])).then_inc(filled, 1)
                for j in range(FIRST_CAT, NB):
                    a, n = BATCHES[j]
                    for l in range(max(a, LO), a + n):
                        gather(rows[u][:, l, D_ID:D], emb_cat, cat_idx[u][:, l - LO:l - LO + 1]).then_inc(
                            cats_gathered[u][j - FIRST_CAT], 16)

            groups(pool, body)

        @block.tensor
        def _(pe):
            pe.wait_ge(consts_made, 3)

            def turn_indices(n):
                pe.wait_ge(cat_lane_ready, n + 1)
                pe.nop(nofuse=True)
                nc.tensor.transpose(turned, cat_lane[:, 0:LO], ident[:, :])
                nc.tensor.transpose(lane_counts, others[:, :], ident[:, :]).then_inc(turned_put, 1)

            turn_indices(0)
            pe.wait_ge(table_ready, 1)
            pe.wait_ge(shift_ready, 1)
            pe.wait_ge(small_gathered, 16 * 2 * CH)
            for c in range(0, CH, TB):
                k = c // TB
                if k >= 2:
                    pe.wait_ge(candT_taken, k - 1)
                for i in range(TB):
                    last = nc.tensor.transpose(tp[k % 2][0:D, i, :], cand_rows[:, c + i, :], ident[:, :])
                last.then_inc(candT_put, 1)
            pe.wait_ge(att_ready, 1)
            pe.wait_ge(candT_taken, CH // TB)
            for k in range(B // NT):
                if k >= 2:
                    pe.wait_ge(tgt_taken, k - 1)
                nc.tensor.matmul(hp[k % 2][0:D, :], w_tgt[:, :], candT[:, k * NT:(k + 1) * NT],
                                 start=True, stop=True).then_inc(tgt_put, 1)
            pe.wait_ge(tgt_taken, B // NT)

            def add_logits(b, k):
                pe.wait_ge(hid_ready, GB * b + COLS * (k + 1))
                if k == 0 and not (isinstance(b, int) and b == 0):
                    pe.wait_ge(logit_ready, b)
                for c in range(COLS):
                    m = P // COLS
                    last = nc.tensor.matmul(lp[c * m:(c + 1) * m, 0:ROW], w2_cols[:, k, :], hid[:, (COLS * k + c) % HB, :],
                                            start=(k == 0), stop=(k == GB // COLS - 1))
                last.then_inc(logit_add, 1)

            counts = [[pe.alloc_register(f"counts{u}_{k}") for k in range(len(SPARED))] for u in range(2)]
            overwritten = [[pe.alloc_register(f"seen_overwritten{u}_{k}") for k in range(len(SPARED))] for u in range(2)]
            for u in range(2):
                for k in range(len(SPARED)):
                    pe.reg_mov(counts[u][k], 0)
                    pe.reg_mov(overwritten[u][k], 1)
            fills = pe.alloc_register("fills")
            pe.reg_mov(fills, 0)

            def body(g, u, t):
                first = isinstance(g, int) and g == 0
                second = isinstance(g, int) and g == 1
                last_one = isinstance(g, int) and g == GROUPS
                b = g - 1
                if not first:
                    pe.wait_ge(w_row_ready, b + 1)
                    pe.wait_ge(tp_taken, NB * (b + 1))
                    pe.wait_ge(cat_taken, NOH * (b + 1))
                    for i in range(GB):
                        if i >= len(hid_banks):
                            pe.wait_ge(hid_ready, GB * b + i - len(hid_banks) + 1)
                        elif not (isinstance(b, int) and b == 0):
                            pe.wait_ge(hid_ready, GB * b)
                        nc.tensor.matmul(hid_banks[i % len(hid_banks)][0:D, 0:ROW], w_row[:, i, :],
                                         seqT[:, i, :, :].rearrange("d q l -> d (q l)"),
                                         start=True, stop=True).then_inc(hid_put, 1)
                        if i >= COLS and i % COLS == 0:
                            add_logits(b, i // COLS - 1)

                def look_up(j):
                    a, n = LOOKUPS[j]
                    m = j // TBLOCK
                    pe.wait_ge(onehot_ready, NO * g + m + 1)
                    if not (isinstance(g, int) and g == 0 and j < 2):
                        pe.wait_ge(cat_taken, NOH * g + j - 1)
                    for i in range(n):
                        at = (a + i - OBLOCKS[m][0][0]) * P
                        for c in range(CC):
                            last = nc.tensor.matmul(cp[(NOH * u + j) % 2][:, i * PARTS * D_CAT:(i + 1) * PARTS * D_CAT],
                                                    onehot[m % OB][:, c, at:at + P],
                                                    cat_parts[:, c, :, :].rearrange("p k d -> p (k d)"),
                                                    start=(c == 0), stop=(c == CC - 1))
                    last.then_inc(cat_put, 1)

                def spread_weights():
                    pe.wait_ge(prob_ready, b + 1)
                    if not second:
                        pe.wait_ge(poolT_ready, g - 1)
                    else:
                        pe.wait_ge(cat16_ready, 2)
                        pe.wait_ge(count_ready, 2)
                    if not (isinstance(b, int) and b == 0):
                        pe.wait_ge(lane_w_ready, b)
                    for q in range(SQ):
                        last = nc.tensor.matmul(sp_w, shift[:, P - GB * (q + 1):2 * P - GB * (q + 1)],
                                                prob[:, q // QUARTERS, (q % QUARTERS) * LQ:(q % QUARTERS + 1) * LQ],
                                                start=(q == 0), stop=(q == SQ - 1))
                    last.then_inc(spread_put, 1)

                def gather_pooled(b, after_turn=True):
                    pe.wait_ge(pooled_ready, b + 1)
                    if after_turn:
                        pe.wait_ge(cat16_ready, b + 3)
                        pe.wait_ge(count_ready, b + 3)
                    if not (isinstance(b, int) and b == 0):
                        pe.wait_ge(poolT_ready, b)
                    nc.tensor.matmul(sp_p, pooled[:, :], gather_lanes[:, :], start=True, stop=True).then_inc(pool_put, 1)

                if not last_one:
                    if not first:
                        pe.wait_ge(hid_ready, GB * b + GB - len(hp))
                    look_up(0)
                if not first:
                    add_logits(b, GB // COLS - 1)
                if not last_one:
                    for j in range(1, AHEAD):
                        look_up(j)
                if not first and not second:
                    gather_pooled(g - 2, after_turn=not last_one)
                if not last_one:
                    pe.wait_ge(count_ready, g + 1)
                    pe.nop(nofuse=True)
                    needed = pe.value_load(steps_needed[u][0:1, 0:1])
                    for j, (a, n) in enumerate(BATCHES):
                        if j == EARLY and not first:
                            spread_weights()
                        if j == PREPARE and not (isinstance(g, int) and g == GROUPS - 1):
                            if first:
                                pe.wait_ge(cat16_ready, 1)
                                pe.wait_ge(count_ready, 1)
                            else:
                                pe.wait_ge(lane_w_ready, g)
                            turn_indices(g + 1)
                        if j + AHEAD < NOH:
                            look_up(j + AHEAD)
                        put = NB * g + j
                        tile = tp[(u + j) % 2]
                        if j < ALWAYS:
                            pe.wait_ge(gathered[u][j], 16 * n * (t + 1))
                        for k, (lo, end) in enumerate(SPARED):
                            if not a <= lo < a + n:
                                continue
                            with pe.If(needed > lo):
                                pe.reg_mov(overwritten[u][k], 1)
                                pe.reg_add(counts[u][k], counts[u][k], 16 * (end - lo))
                                pe.wait_ge(spared_gathered[u][k], counts[u][k])
                                pe.nop(nofuse=True)
                            with pe.Else(), pe.If_cmp(overwritten[u][k], 1, "IS_EQ"):
                                pe.reg_mov(overwritten[u][k], 0)
                                pe.reg_add(fills, fills, 1)
                                pe.wait_ge(filled, fills)
                                pe.nop(nofuse=True)
                        if j < NOH:
                            pe.wait_ge(cat_taken, NOH * g + j + 1)
                        if j >= FIRST_CAT:
                            pe.wait_ge(cats_gathered[u][j - FIRST_CAT], 16 * (a + n - max(a, LO)) * (t + 1))
                        if not (isinstance(g, int) and g == 0 and j < 2):
                            pe.wait_ge(tp_taken, put - 1)
                        for i in range(n):
                            last = nc.tensor.transpose(tile[0:D, i, :], rows[u][:, a + i, :], ident[:, :])
                        last.then_inc(tp_put, 1)
                else:
                    spread_weights()
                    pe.wait_ge(user_gathered, 16 * CH)
                    for k in range(CH // TB):
                        if k >= 2:
                            pe.wait_ge(user_taken, k - 1)
                        else:
                            pe.wait_ge(tp_taken, NB * GROUPS)
                        for i in range(TB):
                            last = nc.tensor.transpose(tp[k % 2][0:D_USER, i, :], user_rows[:, k * TB + i, :], ident[:, :])
                        last.then_inc(user_put, 1)
                    gather_pooled(b, after_turn=False)

            groups(pe, body)

            pe.wait_ge(mlp_loaded, MLP_LOADS)
            pe.wait_ge(late_loaded, LATE_LOADS)
            pe.wait_ge(user_taken, CH // TB)
            pe.wait_ge(poolT_ready, GROUPS)
            for k in range(B // NT):
                s = slice(k * NT, (k + 1) * NT)
                for c in range(2):
                    if k:
                        pe.wait_ge(h1_ready, 2 * (k - 1) + c + 1)
                    m = slice(c * H1C, (c + 1) * H1C)
                    parts = [(fc1_s[:, m], smallT[:, s]), (fc1_x[:, 0, m], candT[:, s]),
                             (fc1_x[:, 1, m], poolT[:, 0, s]), (fc1_x[:, 2, m], poolT[:, 1, s])]
                    for n, (w, x) in enumerate(parts):
                        last = nc.tensor.matmul(hp[c][0:H1C, :], w, x, start=(n == 0), stop=(n == len(parts) - 1))
                    last.then_inc(h1_put, 1)
                pe.wait_ge(h1_ready, 2 * (k + 1))
                if k:
                    pe.wait_ge(h2_ready, k)
                for c in range(2):
                    last = nc.tensor.matmul(lp[0:H2, :], fc2_s[:, c, :], h1T[:, c, :], start=(c == 0), stop=(c == 1))
                last.then_inc(h2_put, 1)
            pe.wait_ge(h2_ready, B // NT)
            for c in range(CH):
                last = nc.tensor.matmul(sp_m[:, c:c + 1], h2T[:, c::CH], fc3_s[:, :], start=True, stop=True)
            last.then_inc(y_put, 1)

        @block.scalar
        def _(act):
            def keep_cats(n):
                act.wait_ge(turned_put, n + 1)
                if not (isinstance(n, int) and n == 0):
                    act.wait_ge(cat_stored, 16 * n)
                act.activation(cat16[:, :], turned, ACT.Copy).then_inc(cat16_ready, 1)

            keep_cats(0)

            def take_small(k, dst, w, put, taken):
                act.wait_ge(put, k + 1)
                act.activation(dst.rearrange("d (p c) -> d c p", c=CH)[:, k * TB:(k + 1) * TB, :],
                               tp[k % 2][0:w, :, :], ACT.Copy).then_inc(taken, 1)

            for k in range(CH // TB):
                take_small(k, candT[:, :], D, candT_put, candT_taken)
            act.wait_ge(att_loaded, 80)
            for k in range(B // NT):
                act.wait_ge(tgt_put, k + 1)
                act.activation(tgtT[:, k * NT:(k + 1) * NT], hp[k % 2][0:D, :], ACT.Identity,
                               bias=b1[:, :]).then_inc(tgt_taken, 1)
            act.wait_ge(tgt_taken, B // NT)

            def body(g, u, t):
                first = isinstance(g, int) and g == 0
                last_one = isinstance(g, int) and g == GROUPS
                b = g - 1
                if not first:
                    for i in range(GB):
                        act.wait_ge(hid_put, GB * b + i + 1)
                        if not (isinstance(b, int) and b == 0 and i < HB):
                            act.wait_ge(logit_add, GB // COLS * b + (i - HB) // COLS + 1)
                        act.activation(hid[:, i % HB, :], hid_banks[i % len(hid_banks)][0:D, 0:ROW], ACT.Relu,
                                       bias=tgtT[:, bass.ds(b * GB + i, 1)]).then_inc(hid_ready, 1)
                    act.wait_ge(logit_add, GB // COLS * (b + 1))
                    if not (isinstance(b, int) and b == 0):
                        act.wait_ge(spread_put, b)
                    act.activation(prob[:, :, :].rearrange("b s l -> b (s l)"), lp[:, 0:ROW], ACT.Identity,
                                   bias=b2[:, :]).then_inc(logit_ready, 1)
                    act.wait_ge(max_ready, b + 1)
                    for s in range(SEQS):
                        act.activation(prob[:, s, :], prob[:, s, :], ACT.Exp, bias=neg_max[:, s:s + 1],
                                       accum_out=exp_sum[:, s:s + 1]).then_inc(exp_ready, 1)

                def norm_weights():
                    act.wait_ge(inv_ready, b + 1)
                    for s in range(SEQS):
                        last = act.activation(prob[:, s, :], prob[:, s, :], ACT.Copy, scale=inv_sum[:, s:s + 1])
                    last.then_inc(prob_ready, 1)

                def lane_weights():
                    act.wait_ge(spread_put, b + 1)
                    if not (isinstance(b, int) and b == 0):
                        act.wait_ge(pooled_ready, b)
                    act.activation(lane_w[:, :], sp_w, ACT.Copy).then_inc(lane_w_ready, 1)

                def keep_pooled(b):
                    act.wait_ge(pool_put, b + 1)
                    act.activation(poolT[:, :, bass.ds(b * GB, GB)], sp_p.rearrange("d (s b) -> d s b", s=SEQS),
                                   ACT.Copy).then_inc(poolT_ready, 1)

                if not last_one:
                    for j, (a, n) in enumerate(BATCHES):
                        if j == 1 and not first:
                            norm_weights()
                        if j == 2 and not (isinstance(g, int) and g < 2):
                            keep_pooled(g - 2)
                        if j == EARLY and not first:
                            lane_weights()
                        act.wait_ge(tp_put, NB * g + j + 1)
                        if j == 0 and not first:
                            act.wait_ge(hid_put, GB * g)
                        act.activation(seqT[:, :, :, a:a + n].rearrange("d b q l -> d q b l"),
                                       tp[(u + j) % 2][0:D, 0:n, :].rearrange("d l (q b) -> d q b l", q=SQ),
                                       ACT.Copy).then_inc(tp_taken, 1)
                        if j == PREPARE and not (isinstance(g, int) and g == GROUPS - 1):
                            keep_cats(g + 1)
                else:
                    norm_weights()
                    keep_pooled(g - 2)
                    lane_weights()
                    act.wait_ge(hid_put, GB * GROUPS)
                    for k in range(CH // TB):
                        take_small(k, smallT[0:D_USER, :], D_USER, user_put, user_taken)
                    keep_pooled(b)

            groups(act, body)

            act.wait_ge(bn_step, 1)
            act.activation(bn1_w[:, 1, :], bn1_w[:, 0, :], ACT.Sqrt).then_inc(bn_sqrt, 1)
            act.activation(bn2_w[:, 1, :], bn2_w[:, 0, :], ACT.Sqrt).then_inc(bn_sqrt, 1)
            act.wait_ge(bn_ready, 1)
            for k in range(B // NT):
                for c in range(2):
                    act.wait_ge(h1_put, 2 * k + c + 1)
                    if k:
                        act.wait_ge(h2_put, k)
                    act.activation(h1T[:, c, :], hp[c][0:H1C, :], ACT.Relu, bias=bn1_w[:, 5, c:c + 1],
                                   scale=bn1_w[:, 3, c:c + 1]).then_inc(h1_ready, 1)
                act.wait_ge(h2_put, k + 1)
                act.activation(h2T[:, k * NT:(k + 1) * NT], lp[0:H2, :], ACT.Relu, bias=bn2_w[:, 5, :],
                               scale=bn2_w[:, 3, :]).then_inc(h2_ready, 1)
            act.wait_ge(fin_exp_in, 1)
            act.activation(fin[:, 1, :], fin[:, 0, :], ACT.Exp, scale=-1.0).then_inc(fin_exp, 1)

        @block.vector
        def _(dve):
            steps = [0]

            def link(ins, s=setup_step):
                steps[0] += 1
                ins.then_inc(s, 1)
                dve.wait_ge(s, steps[0])

            dve.wait_ge(small_loaded, 48)
            sizes = (N_ID, N_CAT, N_USER)
            for n, size in enumerate(sizes):
                last = nc.vector.tensor_scalar(idx_neg[:, n, :], idx_small[:, n, :], 0.0, float(size), ALU.is_lt, ALU.mult)
            link(last)
            link(nc.vector.tensor_tensor(idx_wrapped[:, :, :], idx_small[:, :, :], idx_neg[:, :, :], ALU.add))
            for n, size in enumerate(sizes):
                last = nc.vector.tensor_scalar(idx_fixed[:, n, :], idx_wrapped[:, n, :], 0.0, float(size - 1), ALU.max, ALU.min)
            last.then_inc(small_fixed, 1)

            def sort_step_of(n, u, k):
                V = nc.vector
                if k == 0:
                    dve.wait_ge(idx_loaded[u], 16 * (n - u) + 32)
                    if not (isinstance(n, int) and n == 0):
                        dve.wait_ge(idx_ready, n)
                    for c, size in enumerate((N_ID, N_CAT)):
                        last = V.tensor_scalar(grp_neg[:, c, :], idx_raw[u][:, c, :], 0.0, float(size), ALU.is_lt, ALU.mult)
                    last.then_inc(sort_step, 1)
                    return
                dve.wait_ge(sort_step, (SORT_STEPS - 1) * n + k)
                if k >= 4:
                    dve.nop(nofuse=True)
                if k == 1:
                    V.tensor_tensor(grp_wrapped[:, :, :], idx_raw[u][:, :, :], grp_neg[:, :, :], ALU.add).then_inc(sort_step, 1)
                elif k == 2:
                    for c, size in enumerate((N_ID, N_CAT)):
                        last = V.tensor_scalar(grp_ok[:, c, :], grp_wrapped[:, c, :], 0.0, float(size - 1), ALU.max, ALU.min)
                    last.then_inc(sort_step, 1)
                elif k == 3:
                    V.scalar_tensor_tensor(out=keys[0][:, :], in0=grp_ok[:, 0, :], scalar=float(-KEY),
                                           in1=grp_ok[:, 1, :], op0=ALU.mult, op1=ALU.add).then_inc(sort_step, 1)
                elif k % 2 == 0:
                    r = (k - 4) // 2
                    V.max(sorted_keys[:, 8 * r:8 * r + 8], keys[r % 2][:, :]).then_inc(
                        sorted_ready if r == ROUNDS - 1 else sort_step, 1)
                else:
                    r = (k - 5) // 2
                    V.match_replace(keys[(r + 1) % 2][:, :], sorted_keys[:, 8 * r:8 * r + 8], keys[r % 2][:, :],
                                    float(-KEY * N_ID)).then_inc(sort_step, 1)

            def decode(n, u):
                V = nc.vector
                top_key = float((N_ID - 1) * KEY)
                dve.wait_ge(sorted_ready, n + 1)
                if not (isinstance(n, int) and n == 0):
                    dve.wait_ge(turned_put, n)
                V.tensor_scalar(key_i[:, :], sorted_keys[:, 0:LQ], top_key, None, ALU.add).then_inc(idx_step, 1)
                V.tensor_scalar(is_other[:, :], sorted_keys[:, 0:LQ], KEY - top_key, 0.0, ALU.is_ge, ALU.add,
                                accum_out=others[:, :])
                dve.wait_ge(idx_step, 2 * n + 1)
                V.tensor_scalar(key_hi[:, :], key_i[:, :], KEY.bit_length() - 1, None, ALU.logical_shift_right).then_inc(idx_step, 1)
                dve.wait_ge(idx_step, 2 * n + 2)
                V.scalar_tensor_tensor(out=cat_lane[:, :], in0=key_hi[:, :], scalar=float(-KEY), in1=key_i[:, :],
                                       op0=ALU.mult, op1=ALU.add).then_inc(cat_lane_ready, 1)
                if not (isinstance(n, int) and n < 2):
                    dve.wait_ge(tp_put, NB * (n - 1))
                V.scalar_tensor_tensor(out=cat_idx[u][:, :], in0=key_hi[:, LO:LQ], scalar=float(-KEY), in1=key_i[:, LO:LQ],
                                       op0=ALU.mult, op1=ALU.add)
                V.tensor_scalar(idx[u][:, :], key_hi[:, :], -1.0, float(N_ID - 1), ALU.mult, ALU.add).then_inc(idx_ready, 1)

            def count_steps(n, u):
                dve.wait_ge(cat16_ready, n + 1)
                nc.vector.tensor_reduce(steps_needed[u][:, :], lane_counts, AX, ALU.max).then_inc(count_ready, 1)

            nc.vector.memset(cat_table[:, :, :], 0.0).then_inc(table_cleared, 1)
            for k in range(SORT_STEPS):
                sort_step_of(0, 0, k)
            decode(0, 0)
            for k in range(SORT_STEPS):
                sort_step_of(1, 1, k)
            count_steps(0, 0)

            dve.wait_ge(table_loaded, 16 * (1 + (N_CAT > FULL * P)))
            link(nc.vector.tensor_copy(cat_parts[:, :, 0, :], cat_table[:, :, :]))
            link(nc.vector.tensor_tensor(cat_left[0], cat_table[:, :, :], cat_parts[:, :, 0, :], ALU.subtract))
            link(nc.vector.tensor_copy(cat_parts[:, :, 1, :], cat_left[0]))
            link(nc.vector.tensor_tensor(cat_left[1], cat_left[0], cat_parts[:, :, 1, :], ALU.subtract))
            dve.wait_ge(rows_numbered, 1)
            nc.vector.tensor_copy(table_row[:, :], table_row_i[:, :])
            nc.vector.tensor_copy(cat_parts[:, :, 2, :], cat_left[1]).then_inc(table_ready, 1)
            dve.wait_ge(table_ready, 1)
            dve.wait_ge(att_loaded, 80)
            link(nc.vector.memset(w2_cols[:, :, :], 0.0))
            nc.vector.tensor_copy(w2_cols[:, :, :].rearrange("d a b -> d (a b)")[:, 0::P // COLS + 1],
                                  w2[:, :].to_broadcast([D, GB // COLS]))
            nc.vector.tensor_tensor(w_seq[:, :], w1_abc[:, 0, :], w1_abc[:, 2, :], ALU.add)
            dve.wait_ge(consts_made, 3)
            nc.vector.tensor_reduce(gather_lanes[:, :].rearrange("p (s b) -> p s b", s=SEQS),
                                    ident[:, :].rearrange("p (s q b) -> p s b q", s=SEQS, q=QUARTERS), AX, ALU.add)
            nc.vector.tensor_copy(shift[:, P - GB:P].rearrange("p (k c) -> p k c", c=COLS),
                                  ident[:, :].rearrange("p (c k) -> p k c", c=COLS)[:, 0:GB // COLS, :]).then_inc(shift_ready, 1)
            nc.vector.tensor_tensor(w_tgt[:, :], w1_abc[:, 1, :], w1_abc[:, 2, :], ALU.subtract).then_inc(att_ready, 1)
            dve.wait_ge(att_ready, 1)
            dve.wait_ge(candT_taken, CH // TB)

            def body(g, u, t):
                first = isinstance(g, int) and g == 0
                last_one = isinstance(g, int) and g == GROUPS
                b = g - 1
                v = 1 - u
                more_to_sort = not (isinstance(g, int) and g >= GROUPS - 2)

                def make_onehot(m, halves=(0, 1)):
                    if m == 0:
                        dve.wait_ge(cat_spread[u], 16 * (t + 1))
                    k = NO * g + m
                    if m >= OB:
                        dve.wait_ge(cat_put, NOH * g + TBLOCK * (m - OB + 1))
                    elif not first:
                        dve.wait_ge(cat_put, NOH * g)
                    lo = OBLOCKS[m][0][0] * P
                    w = sum(n for _, n in OBLOCKS[m]) * P
                    for c in range(halves[0] * CC // 2, (halves[-1] + 1) * CC // 2):
                        last = nc.vector.tensor_scalar(onehot[m % OB][:, c, 0:w], cat_of[u][:, lo:lo + w],
                                                       table_row[:, c:c + 1], None, ALU.is_equal)
                    if halves[-1] == 1:
                        last.then_inc(onehot_ready, 1)

                def take_cat(j):
                    if j >= NOH:
                        return
                    a, n = LOOKUPS[j]
                    dve.wait_ge(cat_put, NOH * g + j + 1)
                    nc.vector.tensor_reduce(rows[u][:, a:a + n, D_ID:D],
                                            cp[(NOH * u + j) % 2][:, 0:n * PARTS * D_CAT].rearrange(
                                                "p (l k d) -> p l d k", k=PARTS, d=D_CAT), AX, ALU.add).then_inc(cat_taken, 1)

                def weight_chunk(b, v, c):
                    if c == 0:
                        dve.wait_ge(lane_w_ready, b + 1)
                    if c >= WB:
                        dve.wait_ge(chunk_pooled, NC * b + c - WB + 1)
                    elif not (isinstance(b, int) and b == 0):
                        dve.wait_ge(chunk_pooled, NC * b)
                    ls = slice(c * LC, (c + 1) * LC)
                    nc.vector.tensor_tensor(weighted[c % WB][:, :, :], rows[v][:, ls, :],
                                            lane_w[:, ls].unsqueeze(2).to_broadcast([P, LC, D]),
                                            ALU.mult).then_inc(chunk_weighted, 1)

                def add_chunk(b, c):
                    dve.wait_ge(chunk_weighted, NC * b + c + 1)
                    nc.vector.tensor_reduce(partial[:, c, :], weighted[c % WB][:, :, :].rearrange("p l d -> p d l"), AX,
                                            ALU.add).then_inc(chunk_pooled, 1)

                def make_right_sides(quarter):
                    if quarter == 0 and not first:
                        dve.wait_ge(hid_put, GB * g)
                    for i in range(quarter * GB // 4, (quarter + 1) * GB // 4):
                        last = nc.vector.scalar_tensor_tensor(
                            out=w_row[:, i, :], in0=w_prod[:, :], scalar=candT[:, bass.ds(g * GB + i, 1)],
                            in1=w_seq[:, :], op0=ALU.mult, op1=ALU.add)
                    if quarter == 3:
                        last.then_inc(w_row_ready, 1)

                def behind(j):
                    for kind, n in BEHIND.get(j, []):
                        if kind == "p":
                            make_right_sides(n)
                        elif kind == "s" and more_to_sort:
                            sort_step_of(g + 2, u, n)
                        elif kind == "c" and not (isinstance(g, int) and g == GROUPS - 1):
                            count_steps(g + 1, v)
                        elif kind == "w" and not first:
                            weight_chunk(b, v, n)
                        elif kind == "a" and not first:
                            add_chunk(b, n)
                        elif isinstance(kind, int):
                            make_onehot(kind, (n,))

                def finish_pooling(b):
                    dve.wait_ge(chunk_pooled, NC * (b + 1))
                    if not (isinstance(b, int) and b == 0):
                        dve.wait_ge(pool_put, b)
                    nc.vector.tensor_reduce(pooled[:, :], partial[:, :, :].rearrange("p c d -> p d c"), AX,
                                            ALU.add).then_inc(pooled_ready, 1)

                if not last_one:
                    make_onehot(0)
                    make_onehot(1)
                if not (isinstance(g, int) and g < 2):
                    for c in range(TAIL, NC):
                        weight_chunk(g - 2, u, c)
                        add_chunk(g - 2, c)
                    finish_pooling(g - 2)
                if not last_one:
                    for m in range(2, OB):
                        make_onehot(m)
                    for j in range(AHEAD):
                        take_cat(j)
                        behind(j)
                if not first:
                    dve.wait_ge(logit_ready, b + 1)
                    nc.vector.tensor_reduce(neg_max[:, :], prob[:, :, :], AX, ALU.max, negate=True).then_inc(max_ready, 1)
                if not last_one:
                    take_cat(AHEAD)
                    behind(AHEAD)
                if not first:
                    dve.wait_ge(exp_ready, SEQS * (b + 1))
                    nc.vector.reciprocal(inv_sum[:, :], exp_sum[:, :]).then_inc(inv_ready, 1)
                if not last_one and not (isinstance(g, int) and g == GROUPS - 1):
                    decode(g + 1, v)
                if not last_one:
                    for j in range(AHEAD + 1, NB):
                        take_cat(j)
                        behind(j)
                else:
                    for c in range(NC):
                        weight_chunk(b, v, c)
                        add_chunk(b, c)
                    finish_pooling(b)

            groups(dve, body)

            dve.wait_ge(mlp_loaded, MLP_LOADS)
            for src, w in ((bn1, bn1_w), (bn2, bn2_w)):
                last = nc.vector.tensor_scalar(w[:, 0, :], src[:, 4, :], BN_EPS, None, ALU.add)
            last.then_inc(bn_step, 1)
            dve.wait_ge(bn_sqrt, 2)
            steps[0] = 1
            for src, w in ((bn1, bn1_w), (bn2, bn2_w)):
                link(nc.vector.reciprocal(w[:, 2, :], w[:, 1, :]), bn_step)
                link(nc.vector.tensor_tensor(w[:, 3, :], w[:, 2, :], src[:, 1, :], ALU.mult), bn_step)
                link(nc.vector.tensor_tensor(w[:, 4, :], src[:, 0, :], src[:, 3, :], ALU.subtract), bn_step)
                link(nc.vector.tensor_tensor(w[:, 2, :], w[:, 4, :], w[:, 3, :], ALU.mult), bn_step)
                link(nc.vector.tensor_tensor(w[:, 5, :], w[:, 2, :], src[:, 2, :], ALU.add), bn_step)
            nc.vector.memset(fin[:, 7, :], 0.0).then_inc(bn_ready, 1)
            dve.wait_ge(bn_ready, 1)
            dve.wait_ge(y_put, 1)
            nc.vector.tensor_scalar(fin[:, 0, :], sp_m[:, 0:CH], fc3_bias[:, :], None, ALU.add).then_inc(fin_exp_in, 1)
            dve.wait_ge(fin_exp, 1)
            steps[0] = 0
            link(nc.vector.tensor_scalar(fin[:, 2, :], fin[:, 1, :], 1e-37, 1e37, ALU.max, ALU.min), fin_step)
            link(nc.vector.tensor_scalar(fin[:, 3, :], score_s[:, :], -1.0, 1.0, ALU.mult, ALU.add), fin_step)
            link(nc.vector.tensor_tensor(fin[:, 4, :], fin[:, 2, :], fin[:, 3, :], ALU.mult), fin_step)
            link(nc.vector.tensor_tensor(fin[:, 5, :], fin[:, 4, :], score_s[:, :], ALU.add), fin_step)
            link(nc.vector.reciprocal(fin[:, 6, :], fin[:, 5, :]), fin_step)
            nc.vector.tensor_tensor(fin[:, 7, :], fin[:, 6, :], score_s[:, :], ALU.mult).then_inc(fin_step, 1)


def kernel(**inputs):
    import numpy as np
    import concourse.bacc as bacc
    from concourse.bass_utils import run_bass_kernel_spmd

    def lanes(exp, ipv):
        x = np.stack([np.asarray(exp), np.asarray(ipv)]).reshape(SEQS, GROUPS, GB, LQ, QUARTERS)
        return x.transpose(1, 0, 4, 2, 3).reshape(GROUPS * P, LQ)

    nc = bacc.Bacc("TRN2", target_bir_lowering=False, num_devices=1)
    given = {n: inputs[n] for n in ("r_num_feat1", "r_num_feat2", "r_score", "r_user_id", "r_cand_item_id", "r_cand_item_cat")}
    given["seq_item_id"] = lanes(inputs["r_exp_item_id"], inputs["r_ipv_item_id"])
    given["seq_item_cat"] = lanes(inputs["r_exp_item_cat"], inputs["r_ipv_item_cat"])
    for n in ("emb_item_id", "emb_item_cat", "emb_user", "att_w1", "att_b1", "att_w2", "att_b2",
              "fc1_w", "fc1_b", "bn1_g", "bn1_b", "bn1_m", "bn1_v",
              "fc2_w", "fc2_b", "bn2_g", "bn2_b", "bn2_m", "bn2_v", "fc3_w", "fc3_b"):
        given[n] = inputs["L0_rec_" + n]
    arrays, args = {}, []
    for n, a in given.items():
        a = np.ascontiguousarray(a)
        arrays[f"in_{n}"] = a
        args.append(nc.dram_tensor(f"in_{n}", a.shape, mybir.dt.from_np(a.dtype), kind="ExternalInput").ap())
    args.append(nc.dram_tensor("out_0", (B, 1), mybir.dt.float32, kind="ExternalOutput").ap())
    build(nc, *args)
    r = run_bass_kernel_spmd(nc, [arrays], core_ids=[0])
    return r.results[0]["out_0"]
```
